# Optimizing a Trainium2 kernel written in Bass

```python
import numpy as np
import jax
import jax.numpy as jnp

def _softmax(x, axis=-1):
    return jax.nn.softmax(x, axis=axis)

def _gelu(x):
    return jax.nn.gelu(x, approximate=True)

def _silu(x):
    return jax.nn.silu(x)

def _sigmoid(x):
    return jax.nn.sigmoid(x)

def _layernorm(x, axis=-1, eps=1e-05):
    m = jnp.mean(x, axis=axis, keepdims=True)
    v = jnp.var(x, axis=axis, keepdims=True)
    return (x - m) / jnp.sqrt(v + eps)

def _scatter_add(tgt, idx, src, axis=0):
    return tgt.at[idx].add(src)

def _segment_sum(src, seg, n):
    return jax.ops.segment_sum(src, seg, n)
kernel_name = 'mk_adaln_d2_jaxref_r4_bd1af2'

def setup_inputs(seed: int=0):
    np.random.seed(seed)
    _w = jnp.asarray

    def _L0_attn_setup():
        import jax, jax.numpy as jnp
        import numpy as np
        B, T, D = (4, 512, 256)
        HID = 2 * D
        EPS = 1e-06

        def _rmsnorm(x, w):
            return x * jax.lax.rsqrt(jnp.mean(x * x, axis=-1, keepdims=True) + EPS) * w

        def _ema_scan(v, alpha):

            def step(prev, v_t):
                cur = alpha * v_t + (1.0 - alpha) * prev
                return (cur, cur)
            v_tm = jnp.swapaxes(v, 0, 1)
            _, out = jax.lax.scan(step, jnp.zeros(v.shape[::2], v.dtype), v_tm)
            return jnp.swapaxes(out, 0, 1)

        def _delta_scan(q, k, v, beta):

            def step(S, inp):
                q_t, k_t, v_t, b_t = inp
                Sk = jnp.einsum('bij,bj->bi', S, k_t)
                S = S + b_t[:, None, None] * (v_t - Sk)[:, :, None] * k_t[:, None, :]
                o_t = jnp.einsum('bij,bj->bi', S, q_t)
                return (S, o_t)
            tm = lambda a: jnp.swapaxes(a, 0, 1)
            S0 = jnp.zeros((q.shape[0], q.shape[2], q.shape[2]), q.dtype)
            _, out = jax.lax.scan(step, S0, (tm(q), tm(k), tm(v), tm(beta)))
            return jnp.swapaxes(out, 0, 1)
        key = jax.random.key(seed)
        ks = jax.random.split(key, 12)
        s = 0.02
        return {'x': jax.random.normal(ks[0], (B, T, D), jnp.float32), 'norm1_w': jnp.ones((D,), jnp.float32), 'Wq': jax.random.normal(ks[1], (D, D), jnp.float32) * s, 'Wk': jax.random.normal(ks[2], (D, D), jnp.float32) * s, 'Wv': jax.random.normal(ks[3], (D, D), jnp.float32) * s, 'beta_w': jax.random.normal(ks[4], (D, 1), jnp.float32) * s, 'beta_b': jnp.zeros((1,), jnp.float32), 'Wo': jax.random.normal(ks[5], (D, D), jnp.float32) * s, 'alpha_logit': jnp.full((D,), float(np.log(0.1 / 0.9)), jnp.float32), 'norm2_w': jnp.ones((D,), jnp.float32), 'w_gate': jax.random.normal(ks[6], (D, HID), jnp.float32) * s, 'w_up': jax.random.normal(ks[7], (D, HID), jnp.float32) * s, 'w_down': jax.random.normal(ks[8], (HID, D), jnp.float32) * s}
    _L0_attn_in = _L0_attn_setup()

    def _L0_ffn_setup():
        import jax, jax.numpy as jnp
        import numpy as np
        H, I, E, NS, C = (256, 256, 6, 2, 2)
        TOPK = 2
        TEMP = 1.0
        EPS = 1e-06
        key = jax.random.key(seed)
        ks = jax.random.split(key, 20)
        sd = 0.02
        inp = {'x': jax.random.normal(ks[0], (4, 512, H), jnp.float32), 'router_W': jax.random.normal(ks[1], (C, H, E), jnp.float32) * sd, 'router_b': jax.random.normal(ks[2], (C, E), jnp.float32) * sd, 'gate_bias': jax.random.normal(ks[3], (C, E), jnp.float32) * sd, 'exp_Wup': jax.random.normal(ks[4], (E, H, I), jnp.float32) * sd, 'exp_bup': jnp.zeros((E, I), jnp.float32), 'exp_Wg': jax.random.normal(ks[5], (E, I, I), jnp.float32) * sd, 'exp_bg': jnp.zeros((E, I), jnp.float32), 'exp_Wdown': jax.random.normal(ks[6], (E, I, H), jnp.float32) * sd, 'exp_bdown': jnp.zeros((E, H), jnp.float32), 'share_Wup': jax.random.normal(ks[7], (H, NS * I), jnp.float32) * sd, 'share_bup': jnp.zeros((NS * I,), jnp.float32), 'share_Wg': jax.random.normal(ks[8], (I, I), jnp.float32) * sd, 'share_bg': jnp.zeros((I,), jnp.float32), 'share_Wdown': jax.random.normal(ks[9], (I, H), jnp.float32) * sd, 'share_bdown': jnp.zeros((H,), jnp.float32), 'norm_w': jnp.ones((C, H), jnp.float32)}
        return inp
    _L0_ffn_in = _L0_ffn_setup()
    _L0_c = _w((lambda *s: np.random.randn(*s).astype(np.float32) * 0.05)(1, 256))
    _L0_wmod = _w((lambda *s: np.random.randn(*s).astype(np.float32) * 0.05)(256, 6 * 256) * 256 ** (-0.5))

    def _L1_attn_setup():
        import jax, jax.numpy as jnp
        import numpy as np
        import math
        D_MODEL = 256
        N_HEADS = 16
        D_HEAD = D_MODEL // N_HEADS
        SEQ = 512
        BATCH = 2
        key = jax.random.key(seed)
        ks = jax.random.split(key, 8)
        xav = math.sqrt(2.0 / (D_MODEL + D_MODEL))

        def lin(k):
            return jax.random.normal(k, (D_MODEL, D_MODEL), jnp.float32) * xav
        zeros = jnp.zeros((D_MODEL,), jnp.float32)
        return {'x': jax.random.normal(ks[0], (SEQ, BATCH, D_MODEL), jnp.float32), 'beta': jax.random.normal(ks[1], (N_HEADS,), jnp.float32) * 0.1, 'Wq': lin(ks[2]), 'bq': zeros, 'Wk': lin(ks[3]), 'bk': zeros, 'Wv': lin(ks[4]), 'bv': zeros, 'Wo': lin(ks[5]), 'bo': zeros}
    _L1_attn_in = _L1_attn_setup()

    def _L1_ffn_setup():
        import jax, jax.numpy as jnp
        import numpy as np
        D_MODEL, HIDDEN, N_EXPERTS, TOP_K = (256, 512, 8, 2)
        RMS_EPS = 1e-06
        key = jax.random.key(seed)
        ks = jax.random.split(key, 6)
        B, S = (4, 512)
        return {'x': jax.random.normal(ks[0], (B, S, D_MODEL), jnp.float32), 'norm_weight': jnp.ones((D_MODEL,), jnp.float32), 'gate_w': jax.random.normal(ks[1], (N_EXPERTS, D_MODEL), jnp.float32) * 0.02, 'w1': jax.random.normal(ks[2], (N_EXPERTS, HIDDEN, D_MODEL), jnp.float32) * 0.02, 'b1': jnp.zeros((N_EXPERTS, HIDDEN), jnp.float32), 'w2': jax.random.normal(ks[3], (N_EXPERTS, D_MODEL, HIDDEN), jnp.float32) * 0.02, 'b2': jnp.zeros((N_EXPERTS, D_MODEL), jnp.float32)}
    _L1_ffn_in = _L1_ffn_setup()
    _L1_c = _w((lambda *s: np.random.randn(*s).astype(np.float32) * 0.05)(1, 256))
    _L1_wmod = _w((lambda *s: np.random.randn(*s).astype(np.float32) * 0.05)(256, 6 * 256) * 256 ** (-0.5))
    _d = {'L0_attn_x': _L0_attn_in['x'], 'L0_attn_norm1_w': _L0_attn_in['norm1_w'], 'L0_attn_Wq': _L0_attn_in['Wq'], 'L0_attn_Wk': _L0_attn_in['Wk'], 'L0_attn_Wv': _L0_attn_in['Wv'], 'L0_attn_beta_w': _L0_attn_in['beta_w'], 'L0_attn_beta_b': _L0_attn_in['beta_b'], 'L0_attn_Wo': _L0_attn_in['Wo'], 'L0_attn_alpha_logit': _L0_attn_in['alpha_logit'], 'L0_attn_norm2_w': _L0_attn_in['norm2_w'], 'L0_attn_w_gate': _L0_attn_in['w_gate'], 'L0_attn_w_up': _L0_attn_in['w_up'], 'L0_attn_w_down': _L0_attn_in['w_down'], 'L0_ffn_router_W': _L0_ffn_in['router_W'], 'L0_ffn_router_b': _L0_ffn_in['router_b'], 'L0_ffn_gate_bias': _L0_ffn_in['gate_bias'], 'L0_ffn_exp_Wup': _L0_ffn_in['exp_Wup'], 'L0_ffn_exp_bup': _L0_ffn_in['exp_bup'], 'L0_ffn_exp_Wg': _L0_ffn_in['exp_Wg'], 'L0_ffn_exp_bg': _L0_ffn_in['exp_bg'], 'L0_ffn_exp_Wdown': _L0_ffn_in['exp_Wdown'], 'L0_ffn_exp_bdown': _L0_ffn_in['exp_bdown'], 'L0_ffn_share_Wup': _L0_ffn_in['share_Wup'], 'L0_ffn_share_bup': _L0_ffn_in['share_bup'], 'L0_ffn_share_Wg': _L0_ffn_in['share_Wg'], 'L0_ffn_share_bg': _L0_ffn_in['share_bg'], 'L0_ffn_share_Wdown': _L0_ffn_in['share_Wdown'], 'L0_ffn_share_bdown': _L0_ffn_in['share_bdown'], 'L0_ffn_norm_w': _L0_ffn_in['norm_w'], 'L0_c': _L0_c, 'L0_wmod': _L0_wmod, 'L1_attn_beta': _L1_attn_in['beta'], 'L1_attn_Wq': _L1_attn_in['Wq'], 'L1_attn_bq': _L1_attn_in['bq'], 'L1_attn_Wk': _L1_attn_in['Wk'], 'L1_attn_bk': _L1_attn_in['bk'], 'L1_attn_Wv': _L1_attn_in['Wv'], 'L1_attn_bv': _L1_attn_in['bv'], 'L1_attn_Wo': _L1_attn_in['Wo'], 'L1_attn_bo': _L1_attn_in['bo'], 'L1_ffn_norm_weight': _L1_ffn_in['norm_weight'], 'L1_ffn_gate_w': _L1_ffn_in['gate_w'], 'L1_ffn_w1': _L1_ffn_in['w1'], 'L1_ffn_b1': _L1_ffn_in['b1'], 'L1_ffn_w2': _L1_ffn_in['w2'], 'L1_ffn_b2': _L1_ffn_in['b2'], 'L1_c': _L1_c, 'L1_wmod': _L1_wmod}
    _x0 = _d['L0_attn_x']
    _d['L0_attn_x'] = jax.random.normal(jax.random.fold_in(jax.random.key(seed), 1), (1, 4096, 256), dtype=_x0.dtype)
    del _x0
    return _d

def reference(L0_attn_x, L0_attn_norm1_w, L0_attn_Wq, L0_attn_Wk, L0_attn_Wv, L0_attn_beta_w, L0_attn_beta_b, L0_attn_Wo, L0_attn_alpha_logit, L0_attn_norm2_w, L0_attn_w_gate, L0_attn_w_up, L0_attn_w_down, L0_ffn_router_W, L0_ffn_router_b, L0_ffn_gate_bias, L0_ffn_exp_Wup, L0_ffn_exp_bup, L0_ffn_exp_Wg, L0_ffn_exp_bg, L0_ffn_exp_Wdown, L0_ffn_exp_bdown, L0_ffn_share_Wup, L0_ffn_share_bup, L0_ffn_share_Wg, L0_ffn_share_bg, L0_ffn_share_Wdown, L0_ffn_share_bdown, L0_ffn_norm_w, L0_c, L0_wmod, L1_attn_beta, L1_attn_Wq, L1_attn_bq, L1_attn_Wk, L1_attn_bk, L1_attn_Wv, L1_attn_bv, L1_attn_Wo, L1_attn_bo, L1_ffn_norm_weight, L1_ffn_gate_w, L1_ffn_w1, L1_ffn_b1, L1_ffn_w2, L1_ffn_b2, L1_c, L1_wmod):

    def _L0_attn_ref(x, norm1_w, Wq, Wk, Wv, beta_w, beta_b, Wo, alpha_logit, norm2_w, w_gate, w_up, w_down):
        import jax, jax.numpy as jnp
        import numpy as np
        B, T, D = (4, 512, 256)
        HID = 2 * D
        EPS = 1e-06

        def _rmsnorm(x, w):
            return x * jax.lax.rsqrt(jnp.mean(x * x, axis=-1, keepdims=True) + EPS) * w

        def _ema_scan(v, alpha):

            def step(prev, v_t):
                cur = alpha * v_t + (1.0 - alpha) * prev
                return (cur, cur)
            v_tm = jnp.swapaxes(v, 0, 1)
            _, out = jax.lax.scan(step, jnp.zeros(v.shape[::2], v.dtype), v_tm)
            return jnp.swapaxes(out, 0, 1)

        def _delta_scan(q, k, v, beta):

            def step(S, inp):
                q_t, k_t, v_t, b_t = inp
                Sk = jnp.einsum('bij,bj->bi', S, k_t)
                S = S + b_t[:, None, None] * (v_t - Sk)[:, :, None] * k_t[:, None, :]
                o_t = jnp.einsum('bij,bj->bi', S, q_t)
                return (S, o_t)
            tm = lambda a: jnp.swapaxes(a, 0, 1)
            S0 = jnp.zeros((q.shape[0], q.shape[2], q.shape[2]), q.dtype)
            _, out = jax.lax.scan(step, S0, (tm(q), tm(k), tm(v), tm(beta)))
            return jnp.swapaxes(out, 0, 1)
        h = _rmsnorm(x, norm1_w)
        q = h @ Wq
        k = h @ Wk
        k = k / jnp.maximum(jnp.linalg.norm(k, axis=-1, keepdims=True), 1e-12)
        v = h @ Wv
        v = _ema_scan(v, jax.nn.sigmoid(alpha_logit))
        beta = jax.nn.sigmoid(h @ beta_w + beta_b)[..., 0]
        attn_out = _delta_scan(q, k, v, beta)
        x = x + attn_out @ Wo
        h2 = _rmsnorm(x, norm2_w)
        mlp = jax.nn.silu(h2 @ w_gate) * (h2 @ w_up) @ w_down
        return x + mlp

    def _L0_ffn_ref(x, router_W, router_b, gate_bias, exp_Wup, exp_bup, exp_Wg, exp_bg, exp_Wdown, exp_bdown, share_Wup, share_bup, share_Wg, share_bg, share_Wdown, share_bdown, norm_w):
        import jax, jax.numpy as jnp
        import numpy as np
        H, I, E, NS, C = (256, 256, 6, 2, 2)
        TOPK = 2
        TEMP = 1.0
        EPS = 1e-06
        B, S, Hd = x.shape
        xf = x.reshape(-1, Hd)
        for j in range(C):
            residual = xf
            gate = (xf @ router_W[j] + router_b[j]) / TEMP
            biased = gate + gate_bias[j]
            _, ids = jax.lax.top_k(biased, TOPK)
            sel = (ids[:, :, None] == jnp.arange(E)[None, None, :]).any(axis=1)
            weights = jax.nn.softmax(jnp.where(sel, gate, -jnp.inf), axis=-1)
            h = jnp.einsum('nh,ehi->eni', xf, exp_Wup) + exp_bup[:, None, :]
            h = jax.nn.silu(jnp.einsum('eni,eij->enj', h, exp_Wg) + exp_bg[:, None, :]) * h
            eo = jnp.einsum('eni,eih->enh', h, exp_Wdown) + exp_bdown[:, None, :]
            combined = jnp.einsum('ne,enh->nh', weights, eo)
            s = (xf @ share_Wup + share_bup).reshape(-1, NS, I)
            s = jax.nn.silu(s @ share_Wg + share_bg) * s
            share_out = (s @ share_Wdown + share_bdown).sum(axis=1)
            z = combined + share_out
            y = residual + z
            y = y * jax.lax.rsqrt(jnp.mean(y * y, axis=-1, keepdims=True) + EPS) * norm_w[j]
            xf = y
        return xf.reshape(B, S, Hd)

    def _L1_attn_ref(x, beta, Wq, bq, Wk, bk, Wv, bv, Wo, bo):
        import jax, jax.numpy as jnp
        import numpy as np
        import math
        D_MODEL = 256
        N_HEADS = 16
        D_HEAD = D_MODEL // N_HEADS
        SEQ = 512
        BATCH = 2
        s, b, d = x.shape
        h, dh = (N_HEADS, D_HEAD)

        def proj(W, bias):
            y = x @ W.T + bias
            return y.reshape(s, b, h, dh).transpose(1, 2, 0, 3)
        q = proj(Wq, bq)
        k = proj(Wk, bk)
        v = proj(Wv, bv)
        scale = math.sqrt(dh) * jnp.exp(beta)[None, :, None, None]
        q = jax.nn.softplus(q / scale)
        k = jax.nn.softplus(k / scale)
        kv = jnp.cumsum(k[..., :, None] * v[..., None, :], axis=2)
        kn = jnp.cumsum(k, axis=2)
        num = jnp.einsum('bhsk,bhskv->bhsv', q, kv)
        den = jnp.einsum('bhsk,bhsk->bhs', q, kn)
        out = num / den[..., None]
        out = out.transpose(2, 0, 1, 3).reshape(s, b, d)
        return out @ Wo.T + bo

    def _L1_ffn_ref(x, norm_weight, gate_w, w1, b1, w2, b2):
        import jax, jax.numpy as jnp
        import numpy as np
        D_MODEL, HIDDEN, N_EXPERTS, TOP_K = (256, 512, 8, 2)
        RMS_EPS = 1e-06
        B, S, D = x.shape
        E = gate_w.shape[0]
        t = x * jax.lax.rsqrt(jnp.mean(x * x, axis=-1, keepdims=True) + RMS_EPS) * norm_weight
        tokens = t.reshape(-1, D)
        T = tokens.shape[0]
        gate_logits = tokens @ gate_w.T
        gate_scores, expert_idx = jax.lax.top_k(gate_logits, TOP_K)
        routing_weights = jax.nn.softmax(gate_scores, axis=-1)
        combine = jnp.zeros((T, E), tokens.dtype).at[jnp.arange(T)[:, None], expert_idx].add(routing_weights)

        def body(acc, params):
            W1, B1, W2, B2, c = params
            h = jax.nn.gelu(tokens @ W1.T + B1, approximate=False)
            o = h @ W2.T + B2
            return (acc + c[:, None] * o, None)
        out, _ = jax.lax.scan(body, jnp.zeros_like(tokens), (w1, b1, w2, b2, combine.T))
        return x + out.reshape(B, S, D)
    x = L0_attn_x
    mod = (_silu(L0_c) @ L0_wmod).reshape(L0_c.shape[0], 6, 1, -1)
    sa, ca, ga, sb, cb, gb = (mod[:, 0], mod[:, 1], mod[:, 2], mod[:, 3], mod[:, 4], mod[:, 5])
    ga = (2 * (ga >= 0) - 1) * jnp.maximum(jnp.abs(ga), 0.25)
    gb = (2 * (gb >= 0) - 1) * jnp.maximum(jnp.abs(gb), 0.25)
    h = _layernorm(x, axis=-1) * (1 + ca) + sa
    x = x + ga * _L0_attn_ref(h, L0_attn_norm1_w, L0_attn_Wq, L0_attn_Wk, L0_attn_Wv, L0_attn_beta_w, L0_attn_beta_b, L0_attn_Wo, L0_attn_alpha_logit, L0_attn_norm2_w, L0_attn_w_gate, L0_attn_w_up, L0_attn_w_down)
    h = _layernorm(x, axis=-1) * (1 + cb) + sb
    x = x + gb * _L0_ffn_ref(h, L0_ffn_router_W, L0_ffn_router_b, L0_ffn_gate_bias, L0_ffn_exp_Wup, L0_ffn_exp_bup, L0_ffn_exp_Wg, L0_ffn_exp_bg, L0_ffn_exp_Wdown, L0_ffn_exp_bdown, L0_ffn_share_Wup, L0_ffn_share_bup, L0_ffn_share_Wg, L0_ffn_share_bg, L0_ffn_share_Wdown, L0_ffn_share_bdown, L0_ffn_norm_w)
    mod = (_silu(L1_c) @ L1_wmod).reshape(L1_c.shape[0], 6, 1, -1)
    sa, ca, ga, sb, cb, gb = (mod[:, 0], mod[:, 1], mod[:, 2], mod[:, 3], mod[:, 4], mod[:, 5])
    ga = (2 * (ga >= 0) - 1) * jnp.maximum(jnp.abs(ga), 0.25)
    gb = (2 * (gb >= 0) - 1) * jnp.maximum(jnp.abs(gb), 0.25)
    h = _layernorm(x, axis=-1) * (1 + ca) + sa
    x = x + ga * _L1_attn_ref(h, L1_attn_beta, L1_attn_Wq, L1_attn_bq, L1_attn_Wk, L1_attn_bk, L1_attn_Wv, L1_attn_bv, L1_attn_Wo, L1_attn_bo)
    h = _layernorm(x, axis=-1) * (1 + cb) + sb
    x = x + gb * _L1_ffn_ref(h, L1_ffn_norm_weight, L1_ffn_gate_w, L1_ffn_w1, L1_ffn_b1, L1_ffn_w2, L1_ffn_b2)
    return x

_drawn_inputs = setup_inputs


def setup_inputs(seed=0):
    import zlib

    import numpy as np

    out = dict(_drawn_inputs(seed))
    spreads = {'L0_attn_norm1_w': (1.0, 0.6),
     'L0_attn_alpha_logit': (-2.1972246170043945, 0.6),
     'L0_attn_norm2_w': (1.0, 0.6),
     'L0_ffn_exp_bup': (0.0, 0.8),
     'L0_ffn_exp_bg': (0.0, 0.8),
     'L0_ffn_exp_bdown': (0.0, 0.31),
     'L0_ffn_share_bup': (0.0, 0.8),
     'L0_ffn_share_bg': (0.0, 0.8),
     'L0_ffn_share_bdown': (0.0, 0.1),
     'L0_ffn_norm_w': (1.0, 0.2),
     'L1_attn_bq': (0.0, 0.8),
     'L1_attn_bk': (0.0, 0.8),
     'L1_attn_bv': (0.0, 0.334),
     'L1_attn_bo': (0.0, 0.35),
     'L1_ffn_norm_weight': (1.0, 0.6),
     'L1_ffn_b1': (0.0, 0.8),
     'L1_ffn_b2': (0.0, 0.491)}
    factors = {'L0_attn_Wq': 2.77,
     'L0_attn_Wk': 2.754,
     'L0_attn_Wv': 2.773,
     'L0_attn_beta_w': 8.0,
     'L0_attn_Wo': 2.754,
     'L0_attn_w_gate': 8.0,
     'L0_attn_w_up': 8.0,
     'L0_attn_w_down': 8.0,
     'L0_ffn_router_W': 3.12,
     'L0_ffn_router_b': 8.0,
     'L0_ffn_gate_bias': 8.0,
     'L0_ffn_exp_Wup': 8.0,
     'L0_ffn_exp_Wg': 8.0,
     'L0_ffn_exp_Wdown': 8.0,
     'L0_ffn_share_Wup': 8.0,
     'L0_ffn_share_Wg': 8.0,
     'L0_ffn_share_Wdown': 8.0,
     'L1_attn_beta': 8.0,
     'L1_attn_Wq': 8.0,
     'L1_attn_Wk': 8.0,
     'L1_ffn_gate_w': 2.941,
     'L1_ffn_w1': 4.266,
     'L1_ffn_w2': 3.983}
    for name, (base, spread) in spreads.items():
        noise = np.random.default_rng([zlib.crc32(name.encode()), seed]).standard_normal(out[name].shape)
        drawn = base * np.exp(spread * noise) if base else spread * noise
        out[name] = jnp.asarray(drawn.astype(out[name].dtype))
    for name, factor in factors.items():
        out[name] = (out[name] * factor).astype(out[name].dtype)
    return out
```

```python
import concourse.bass as bass
from concourse import mybir
from contextlib import ExitStack

F32, F32R, I32 = mybir.dt.float32, mybir.dt.float32r, mybir.dt.int32
ALU, ACT = mybir.AluOpType, mybir.ActivationFunctionType
AX = mybir.AxisListType

P = 128
N, D = 4096, 256
KD = D // P
NT = N // P
TB = 512
NB = N // TB
CT = TB // P
HID = 2 * D
KH = HID // P
E0, NS, R0 = 6, 2, 2
U0 = NS + E0
E1 = 8
EP = 8
HEADS = 16
DH = D // HEADS
LEVELS = 7
LN_EPS, RMS_EPS = 1e-5, 1e-6
BIG = 3.0e38

COL = {}
_n = 0
for _name, _w in (("norm1", KD), ("norm2", KD), ("alpha", KD), ("norm3", KD), ("bq", KD), ("bk", KD), ("bv", KD),
                  ("hbeta", KD), ("c0", KD), ("c1", KD), ("bup", U0 * KD), ("bg", U0 * KD), ("b1", E1 * KH)):
    COL[_name] = _n
    _n += _w
NCOL = _n
ROW = {}
_n = 0
for _name, _w in (("norm_w", R0 * D), ("rb", R0 * E0), ("gb", R0 * E0), ("bo", D), ("beta_b", 1)):
    ROW[_name] = _n
    _n += _w
NROW = _n


class Names(dict):

    def __getattr__(self, name):
        return self[name]

    def __setattr__(self, name, value):
        self[name] = value


class Signal:

    def __init__(self, sem, per=1, credit=0):
        self.sem, self.per, self.credit = sem, per, credit

    def at(self, t, k=None):
        return t * self.per + (self.credit + (self.per if k is None else k))

    def again(self, turns, per=None):
        return Signal(self.sem, self.per if per is None else per, self.credit + turns * self.per)


class Chain:

    def __init__(self, sem):
        self.sem, self.base, self.n = sem, 0, 0

    def loop(self, t, per):
        self.before, self.base, self.n, self.per = self.base + self.n, self.base + self.n + t * per, 0, per

    def end(self, turns):
        assert self.n == self.per, (self.n, self.per)
        self.base, self.n = self.before + turns * self.per, 0

    def next(self):
        self.n += 1
        return self.base + self.n


def rsqrt(g, link, out, x, neg_half, scale, eps, floor=None):
    if floor is None:
        g.tensor_scalar(out, x, scale, eps, ALU.mult, ALU.add).then_inc(link.sem, 1)
        g.wait_ge(link.sem, link.next())
    else:
        g.tensor_scalar(out, x, scale, floor, ALU.mult, ALU.max).then_inc(link.sem, 1)
        g.wait_ge(link.sem, link.next())
    return g.tensor_tensor(out, out, neg_half, ALU.pow)


def three(pe, out, lhs, rhs, first=True, last=True):
    n, of = 0, 3 * len(lhs)
    for (lh, ll), (rh, rl) in zip(lhs, rhs):
        for a, b in ((lh, rh), (lh, rl), (ll, rh)):
            ins = pe.matmul(out, a, b, start=first and n == 0, stop=last and n == of - 1)
            n += 1
    return ins


def absorb(eng, b, i=0):
    if eng is b.scalar:
        eng.activation(b.spare_s[:, i:i + 1], b.neg_half[:, 0:1], ACT.Copy)
    elif eng is b.gpsimd:
        eng.tensor_tensor(b.spare_g[:, i:i + 1], b.neg_half[:, 0:1], b.neg_half[:, 0:1], ALU.mult)
    else:
        eng.memset(b.spare_v[:, i:i + 1], 0.0)


def flat(ap):
    return ap.rearrange("p c n -> p (c n)")


def mid(vec, n):
    return vec.unsqueeze(1).broadcast_to([P, n, vec.shape[1]])


def spread(cols, w):
    return cols.unsqueeze(2).broadcast_to([P, cols.shape[1], w])


SA, CA, GA, SB, CB, GB = range(6)


def modulation_scalar(act, b, s, layer):
    c0 = COL[f"c{layer}"]
    if layer == 0:
        act.wait_ge(s.load_small.sem, s.load_small.at(0))
    act.activation(b.silu_c[:, :], b.cols[:, c0:c0 + KD], ACT.Silu).then_inc(s.silu_c[layer].sem, 1)
    act.wait_ge(s.silu_c[layer].sem, s.silu_c[layer].at(0))
    for k in range(KD):
        act.activation(b.silu_rep[layer][:, k, :], b.ones[:, :], ACT.Copy, scale=b.silu_c[:, k:k + 1]).then_inc(s.silu_rep[layer].sem, 1)
    for j in range(3):
        act.wait_ge(s.mod_ps[layer].sem, s.mod_ps[layer].at(0, j + 1))
        act.activation(b.mod[:, 2 * j:2 * j + 2, :], b.bank[j][:, :], ACT.Copy).then_inc(s.mod_raw[layer].sem, 1)


def modulation_tensor(pe, b, s, layer):
    pe.wait_ge(s.silu_rep[layer].sem, s.silu_rep[layer].at(0))
    pe.wait_ge(s.load_wmod[layer].sem, s.load_wmod[layer].at(0))
    for j in range(3):
        for k in range(KD):
            ins = pe.matmul(b.bank[j][:, :], b.silu_rep[layer][:, k, :], b.wmod[layer][:, k, j * TB:(j + 1) * TB], start=k == 0, stop=k == KD - 1)
        ins.then_inc(s.mod_ps[layer].sem, 1)


def modulation_vector(v, b, s, link, layer):
    v.wait_ge(s.mod_raw[layer].sem, s.mod_raw[layer].at(0))
    for j in (CA, CB):
        v.tensor_scalar(b.mod[:, j, :], b.mod[:, j, :], 1.0, None, ALU.add).then_inc(link.sem, 1)
        v.wait_ge(link.sem, link.next())
    for j in (GA, GB):
        v.tensor_scalar(b.gate_sign[layer][:, :], b.mod[:, j, :], 0.0, 2.0, ALU.is_ge, ALU.mult).then_inc(link.sem, 1)
        v.wait_ge(link.sem, link.next())
        v.scalar_tensor_tensor(b.mod[:, j, :], b.mod[:, j, :], -1.0, b.mod[:, j, :], ALU.mult, ALU.max).then_inc(link.sem, 1)
        v.wait_ge(link.sem, link.next())
        v.tensor_scalar(b.mod[:, j, :], b.mod[:, j, :], 0.25, None, ALU.max).then_inc(link.sem, 1)
        v.wait_ge(link.sem, link.next())
        last = v.scalar_tensor_tensor(b.mod[:, j, :], b.gate_sign[layer][:, :], -1.0, b.mod[:, j, :], ALU.add, ALU.mult)
        if j == GA:
            last.then_inc(link.sem, 1)
            v.wait_ge(link.sem, link.next())
    last.then_inc(s.mod[layer].sem, 1)
    v.wait_ge(s.mod[layer].sem, s.mod[layer].at(0))


A_MATS = (("wk", KD, D, "norm1"), ("beta_w", KD, 2, "norm1"), ("wv", KD, D, "norm1"), ("wq", KD, D, "norm1"), ("wo", KD, D, None),
          ("w_gate", KD, HID, "norm2"), ("w_up", KD, HID, "norm2"), ("w_down", KH, D, None))


def a_weights_vector(v, b, s, link):
    for i, (name, kb, w, norm) in enumerate(A_MATS):
        v.wait_ge(s.load_a[i].sem, s.load_a[i].at(0))
        raw, hi, lo = b.a_raw[name], b.a_hi[name], b.a_lo[name]
        if norm:
            for k in range(kb):
                v.tensor_scalar(raw[:, k, :], raw[:, k, :], b.cols[:, COL[norm] + k:COL[norm] + k + 1], None, ALU.mult).then_inc(link.sem, 1)
                v.wait_ge(link.sem, link.next())
        v.tensor_copy(hi, raw).then_inc(link.sem, 1)
        v.wait_ge(link.sem, link.next())
        v.tensor_tensor(lo, raw, hi.bitcast(F32), ALU.subtract).then_inc(s.a_w.sem, 1)


def a_tensor(pe, b, s):
    B = b.bank
    h = lambda k, c0=0, w=TB: (b.hT_hi[:, k, c0:c0 + w], b.hT_lo[:, k, c0:c0 + w])
    W = lambda name, k, c0=0, w=D: (b.a_hi[name][:, k, c0:c0 + w], b.a_lo[name][:, k, c0:c0 + w])
    chunk = lambda c: slice(c * P, (c + 1) * P)

    def tokens(t):
        pe.wait_ge(s.hn.sem, s.hn.at(t))
        for k in range(KD):
            for c in range(CT):
                ins = pe.transpose(B[k][:, chunk(c)], b.hn[:, c, k * P:(k + 1) * P], b.ident)
            ins.then_inc(s.hT_ps.sem, 1)

    def keys(t):
        for c in range(CT):
            ins = three(pe, B[c // 2][:, (c % 2) * D:(c % 2 + 1) * D], [h(k, c * P, P) for k in range(KD)], [W("wk", k) for k in range(KD)])
            if c % 2:
                ins.then_inc(s.k_ps.sem, 1)

    def block(t, more):
        for name, at, sig in (("wv", 4, s.v_ps), ("wq", 2, s.q_ps)):
            for o in range(KD):
                three(pe, B[at + o][:, :], [W(name, k, o * P, P) for k in range(KD)], [h(k) for k in range(KD)]).then_inc(sig.sem, 1)
        pe.wait_ge(s.y.sem, s.y.at(t - 1))
        for c in range(CT):
            ins = three(pe, B[6][:, 2 * c:2 * c + 2], [h(k, c * P, P) for k in range(KD)], [W("beta_w", k, 0, 2) for k in range(KD)])
        ins.then_inc(s.beta_ps.sem, 1)
        pe.wait_ge(s.k.sem, s.k.at(t))
        pe.wait_ge(s.av.sem, s.av.at(t))
        for k in range(KD):
            for c in range(CT):
                ins = pe.transpose(B[4 + k][:, chunk(c)], b.k[:, c, k * P:(k + 1) * P], b.ident)
            ins.then_inc(s.kT_ps.sem, 1)
        pe.wait_ge(s.ema.sem, s.ema.at(t))
        pe.wait_ge(s.qT.sem, s.qT.at(t))
        for c in range(CT):
            for o in range(KD):
                ins = pe.transpose(B[2 + c // 2][:, (c % 2) * D + o * P:(c % 2) * D + (o + 1) * P], b.ema[:, o, chunk(c)], b.ident)
            if c % 2:
                ins.then_inc(s.vtok_ps.sem, 1)
        pe.wait_ge(s.kT.sem, s.kT.at(t))
        pe.wait_ge(s.beta_e.sem, s.beta_e.at(t))
        for c in range(CT):
            for k in range(KD):
                ins = pe.matmul(B[6][:, chunk(c)], b.kT[:, k, chunk(c)], b.kT[:, k, chunk(c)], start=k == 0, stop=k == KD - 1)
        ins.then_inc(s.g_ps.sem, 1)
        for c in range(CT):
            for k in range(KD):
                ins = pe.matmul(B[7][:, chunk(c)], b.kT[:, k, chunk(c)], b.qT[:, k, chunk(c)], start=k == 0, stop=k == KD - 1)
        ins.then_inc(s.pt_ps.sem, 1)
        pe.wait_ge(s.a.sem, s.a.at(t))
        for c in range(CT):
            ins = pe.transpose(B[0][:, chunk(c)], b.a[:, chunk(c)], b.ident)
        ins.then_inc(s.aT_ps.sem, 1)
        pe.wait_ge(s.vtok.sem, s.vtok.at(t))
        for l in range(1, LEVELS):
            pe.wait_ge(s.aTm.sem, s.aTm.at(t, l))
            pe.wait_ge(s.x.sem, s.x.at(t, l))
            for c in range(CT):
                ins = pe.matmul(B[1][:, chunk(c)], b.aTm[l % 2][:, chunk(c)], b.xx[:, chunk(c)], start=True, stop=True)
            ins.then_inc(s.ax_ps.sem, 1)
            pe.wait_ge(s.ax.sem, s.ax.at(t, l))
            pe.wait_ge(s.xT.sem, s.xT.at(t, l))
            if l < LEVELS - 1:
                for c in range(CT):
                    ins = pe.matmul(B[2][:, chunk(c)], b.xT[:, chunk(c)], b.ax[:, chunk(c)], start=True, stop=True)
                ins.then_inc(s.xax_ps.sem, 1)
            for c in range(CT):
                ins = pe.matmul(B[3][:, chunk(c)], b.ax[:, chunk(c)], b.xT[:, chunk(c)], start=True, stop=True)
            ins.then_inc(s.xaxT_ps.sem, 1)
        pe.wait_ge(s.tT.sem, s.tT.at(t))
        for k in range(KD):
            for c in range(CT):
                ins = pe.matmul(B[4 + k][:, chunk(c)], b.k[:, c, k * P:(k + 1) * P], b.tT[:, chunk(c)], start=True, stop=True)
            ins.then_inc(s.wT_ps.sem, 1)
        pe.wait_ge(s.pT.sem, s.pT.at(t))
        pe.wait_ge(s.wT.sem, s.wT.at(t))
        for c in range(CT):
            state = b.m[c % 2]
            pe.matmul(B[6][:, 0:D], b.tT[:, chunk(c)], b.v[:, c, :], start=True, stop=False)
            pe.wait_ge(s.m.sem, s.m.at(t, c))
            for k in range(KD):
                ins = pe.matmul(B[6][:, 0:D], b.wT[:, k, chunk(c)], state[:, k, :], start=False, stop=k == KD - 1)
            ins.then_inc(s.u_ps.sem, 1)
            pe.wait_ge(s.u.sem, s.u.at(t, c + 1))
            for k in range(KD):
                ins = pe.matmul(B[7][:, k * D:(k + 1) * D], b.k[:, c, k * P:(k + 1) * P], b.u[c % 2][:, :], start=True, stop=True)
            ins.then_inc(s.dm_ps.sem, 1)
            for o in range(KD):
                for k in range(KD):
                    pe.matmul(B[o][:, chunk(c)], state[:, k, o * P:(o + 1) * P], b.qT[:, k, chunk(c)], start=k == 0, stop=False)
                ins = pe.matmul(B[o][:, chunk(c)], b.u[c % 2][:, o * P:(o + 1) * P], b.pT[:, chunk(c)], start=False, stop=True)
        ins.then_inc(s.oT_ps.sem, 1)
        pe.wait_ge(s.oT_hi.sem, s.oT_hi.at(t))
        pe.wait_ge(s.oT_lo.sem, s.oT_lo.at(t))
        for c in range(CT):
            ins = three(pe, B[2 + c // 2][:, (c % 2) * D:(c % 2 + 1) * D], [(b.oT_hi[:, k, chunk(c)], b.oT_lo[:, k, chunk(c)]) for k in range(KD)],
                        [W("wo", k) for k in range(KD)])
            if c % 2:
                ins.then_inc(s.wo_ps.sem, 1)
        if more:
            tokens(t + 1)
        pe.wait_ge(s.hn2.sem, s.hn2.at(t))
        for k in range(KD):
            for c in range(CT):
                ins = pe.transpose(B[4 + k][:, chunk(c)], b.hn2[:, c, k * P:(k + 1) * P], b.ident)
            ins.then_inc(s.h2T_ps.sem, 1)
        pe.wait_ge(s.h2T_hi.sem, s.h2T_hi.at(t))
        pe.wait_ge(s.h2T_lo.sem, s.h2T_lo.at(t))
        h2 = [(b.h2T_hi[:, k, :], b.h2T_lo[:, k, :]) for k in range(KD)]
        for o, at in enumerate((6, 7, 0, 1)):
            if o == 2 and more:
                pe.wait_ge(s.hT_hi.sem, s.hT_hi.at(t + 1))
                pe.wait_ge(s.hT_lo.sem, s.hT_lo.at(t + 1))
            three(pe, B[at][:, :], [W("w_gate", k, o * P, P) for k in range(KD)], h2).then_inc(s.gate_ps.sem, 1)
        for o in range(KH):
            three(pe, B[2 + o][:, :], [W("w_up", k, o * P, P) for k in range(KD)], h2).then_inc(s.up_ps.sem, 1)
        if more:
            pe.wait_ge(s.sg.sem, s.sg.at(t))
            keys(t + 1)
        pe.wait_ge(s.mm_hi.sem, s.mm_hi.at(t))
        pe.wait_ge(s.mm_lo.sem, s.mm_lo.at(t))
        for c in range(CT):
            ins = three(pe, B[6 + c // 2][:, (c % 2) * D:(c % 2 + 1) * D], [(b.mm_hi[:, k, chunk(c)], b.mm_lo[:, k, chunk(c)]) for k in range(KH)],
                        [W("w_down", k) for k in range(KH)])
            if c % 2:
                ins.then_inc(s.down_ps.sem, 1)

    tokens(0)
    pe.wait_ge(s.a_w.sem, s.a_w.at(0))
    pe.wait_ge(s.hT_hi.sem, s.hT_hi.at(0))
    pe.wait_ge(s.hT_lo.sem, s.hT_lo.at(0))
    keys(0)
    with pe.Fori(0, NB - 1) as t:
        block(t, True)
    block(NB - 1, False)


def a_scalar(act, b, s):
    B = b.bank
    act.wait_ge(s.load_small.sem, s.load_small.at(0))

    def square(t, c):
        act.wait_ge(s.h1.sem, s.h1.at(t, c + 1))
        act.activation(b.sg[:, c, 0:D], b.h1_next[:, c, :], ACT.Square, accum_out=b.ss1[:, c:c + 1]).then_inc(s.ss1.sem, 1)

    def tokens(t):
        for k in range(KD):
            act.wait_ge(s.hT_ps.sem, s.hT_ps.at(t, k + 1))
            act.activation(b.hT_hi[:, k, :], B[k][:, :], ACT.Copy).then_inc(s.hT_hi.sem, 1)

    def keys(t):
        for c in range(CT):
            act.wait_ge(s.k_ps.sem, s.k_ps.at(t, c // 2 + 1))
            act.activation(b.sg[:, c, D:2 * D], B[c // 2][:, (c % 2) * D:(c % 2 + 1) * D], ACT.Square, accum_out=b.kss[:, c:c + 1]).then_inc(s.kss.sem, 1)

    def block(t, more):
        for o in range(KD):
            act.wait_ge(s.v_ps.sem, s.v_ps.at(t, o + 1))
            act.activation(b.av[:, o, :], B[4 + o][:, :], ACT.Copy, scale=b.alpha[:, o:o + 1]).then_inc(s.av.sem, 1)
        for o in range(KD):
            act.wait_ge(s.q_ps.sem, s.q_ps.at(t, o + 1))
            act.activation(b.qT[:, o, :], B[2 + o][:, :], ACT.Copy).then_inc(s.qT.sem, 1)
        act.wait_ge(s.beta_ps.sem, s.beta_ps.at(t))
        act.activation(b.beta_e[:, :], B[6][:, 0:2 * CT:2], ACT.Exp, bias=b.neg_beta_b[:, :], scale=-1.0).then_inc(s.beta_e.sem, 1)
        for k in range(KD):
            act.wait_ge(s.kT_ps.sem, s.kT_ps.at(t, k + 1))
            act.activation(b.kT[:, k, :], B[4 + k][:, :], ACT.Copy).then_inc(s.kT.sem, 1)
        for i in range(2):
            act.wait_ge(s.vtok_ps.sem, s.vtok_ps.at(t, i + 1))
            act.activation(b.v[:, 2 * i:2 * i + 2, :], B[2 + i][:, :], ACT.Copy).then_inc(s.vtok.sem, 1)
        act.wait_ge(s.aT_ps.sem, s.aT_ps.at(t))
        act.activation(b.aT[:, :], B[0][:, :], ACT.Copy).then_inc(s.aT.sem, 1)
        for l in range(1, LEVELS):
            act.wait_ge(s.ax_ps.sem, s.ax_ps.at(t, l))
            act.activation(b.ax[:, :], B[1][:, :], ACT.Copy).then_inc(s.ax.sem, 1)
            if more and 2 <= l < 2 + CT:
                square(t + 1, l - 2)
        for k in range(KD):
            act.wait_ge(s.wT_ps.sem, s.wT_ps.at(t, k + 1))
            act.activation(b.wT[:, k, :], B[4 + k][:, :], ACT.Copy, scale=-1.0).then_inc(s.wT.sem, 1)
        for c in range(CT):
            act.wait_ge(s.u_ps.sem, s.u_ps.at(t, c + 1))
            act.activation(b.u[c % 2][:, :], B[6][:, 0:D], ACT.Copy).then_inc(s.u.sem, 1)
        act.wait_ge(s.oT_ps.sem, s.oT_ps.at(t))
        for o in range(KD):
            act.activation(b.oT_hi[:, o, :], B[o][:, :], ACT.Copy).then_inc(s.oT_hi.sem, 1)
        for c in range(CT):
            act.wait_ge(s.xa.sem, s.xa.at(t, c // 2 + 1))
            act.activation(b.v[:, c, :], b.xa[:, c, :], ACT.Square, accum_out=b.ss2[:, c:c + 1]).then_inc(s.ss2.sem, 1)
        if more:
            tokens(t + 1)
        for k in range(KD):
            act.wait_ge(s.h2T_ps.sem, s.h2T_ps.at(t, k + 1))
            act.activation(b.h2T_hi[:, k, :], B[4 + k][:, :], ACT.Copy).then_inc(s.h2T_hi.sem, 1)
        for o, at in enumerate((6, 7, 0, 1)):
            act.wait_ge(s.gate_ps.sem, s.gate_ps.at(t, o + 1))
            act.activation(b.sg[:, o, :], B[at][:, :], ACT.Silu).then_inc(s.sg.sem, 1)
        for o in range(KH):
            act.wait_ge(s.mm.sem, s.mm.at(t, o + 1))
            act.activation(b.mm_hi[:, o, :], B[2 + o][:, :], ACT.Copy).then_inc(s.mm_hi.sem, 1)
        if more:
            keys(t + 1)
            act.activation(flat(b.h1[:, :, :]), flat(b.h1_next[:, :, :]), ACT.Copy).then_inc(s.h1_kept.sem, 1)

    for c in range(CT):
        square(0, c)
    act.activation(flat(b.h1[:, :, :]), flat(b.h1_next[:, :, :]), ACT.Copy).then_inc(s.h1_kept.sem, 1)
    tokens(0)
    keys(0)
    with act.Fori(0, NB - 1) as t:
        block(t, True)
    block(NB - 1, False)


def a_vector(v, b, s, link):
    B = b.bank
    f32 = lambda ap: ap.bitcast(F32)
    four = lambda ap: ap.rearrange("p (c n) -> p c n", c=CT)
    PER = 4

    def stats(t):
        for c in range(CT):
            v.bn_stats(b.stats[:, c, :], b.x[:, bass.ds((t * CT + c) * D, D)]).then_inc(s.stats.sem, 1)
        v.wait_ge(s.stats.sem, s.stats.at(t))
        absorb(v, b)
        for c in range(CT):
            v.bn_aggr(b.mv[:, c, :], b.stats[:, c, :]).then_inc(s.mv.sem, 1)

    def modulate(t, c):
        if c == 0:
            v.wait_ge(s.rs1.sem, s.rs1.at(t))
        v.scalar_tensor_tensor(b.h1_next[:, c, :], b.x[:, bass.ds((t * CT + c) * D, D)], b.mv[:, c, 0:1], b.mod[:, CA, :],
                               ALU.subtract, ALU.mult).then_inc(s.xn.sem, 1)
        v.wait_ge(s.xn.sem, s.xn.at(t, c + 1))
        v.scalar_tensor_tensor(b.h1_next[:, c, :], b.h1_next[:, c, :], b.rs1[:, c:c + 1], b.mod[:, SA, :], ALU.mult, ALU.add).then_inc(s.h1.sem, 1)

    def normalise(t, c):
        if c == 0:
            v.wait_ge(s.rs2.sem, s.rs2.at(t))
        v.tensor_scalar(b.hn[:, c, :], b.h1_next[:, c, :], b.rs2[:, c:c + 1], None, ALU.mult).then_inc(s.hn.sem, 1)

    def tokens(t):
        for k in range(KD):
            v.wait_ge(s.hT_hi.sem, s.hT_hi.at(t, k + 1))
            v.tensor_tensor(b.hT_lo[:, k, :], B[k][:, :], f32(b.hT_hi[:, k, :]), ALU.subtract).then_inc(s.hT_lo.sem, 1)

    def block(t, more):
        v.wait_ge(s.rk.sem, s.rk.at(t))
        for c in range(CT):
            v.tensor_scalar(b.k[:, c, :], B[c // 2][:, (c % 2) * D:(c % 2 + 1) * D], b.rk[:, c:c + 1], None, ALU.mult).then_inc(s.k.sem, 1)
        v.wait_ge(s.beta_e.sem, s.beta_e.at(t))
        v.tensor_scalar(b.beta_e[:, :], b.beta_e[:, :], 1.0, None, ALU.add).then_inc(link.sem, 1)
        v.wait_ge(link.sem, link.next())
        v.reciprocal(b.beta[:, :], b.beta_e[:, :]).then_inc(link.sem, 1)
        v.wait_ge(link.sem, link.next())
        for o in range(KD):
            v.wait_ge(s.av.sem, s.av.at(t, o + 1))
            v.tensor_tensor_scan(b.ema[:, o, :], b.decay[:, o:o + 1].broadcast_to([P, TB]), b.av[:, o, :], b.carry[:, o:o + 1],
                                 ALU.mult, ALU.add).then_inc(s.ema.sem, 1)
        v.wait_ge(s.ema.sem, s.ema.at(t))
        v.tensor_copy(b.carry[:, :], b.ema[:, :, TB - 1:TB].squeeze(2)).then_inc(link.sem, 1)
        v.wait_ge(link.sem, link.next())
        if more:
            stats(t + 1)
        v.wait_ge(s.g_ps.sem, s.g_ps.at(t))
        v.tensor_tensor(four(b.a[:, :]), four(B[6][:, :]), spread(b.beta[:, :], P), ALU.mult).then_inc(s.a.sem, 1)
        v.wait_ge(s.pt_ps.sem, s.pt_ps.at(t))
        v.tensor_tensor(four(b.pT[:, :]), four(B[7][:, :]), mid(b.upper, CT), ALU.mult).then_inc(s.pT.sem, 1)
        v.wait_ge(s.a.sem, s.a.at(t))
        v.tensor_tensor(four(b.x_tmp[:, :]), four(b.a[:, :]), mid(b.mask0, CT), ALU.mult).then_inc(link.sem, 1)
        v.wait_ge(link.sem, link.next())
        v.tensor_tensor(four(b.xx[:, :]), mid(b.ident, CT), four(b.x_tmp[:, :]), ALU.subtract).then_inc(s.x.sem, 1)
        v.wait_ge(s.aTm0.sem, s.aTm0.at(t))
        v.tensor_tensor(four(b.xT[:, :]), mid(b.ident, CT), four(b.aTm[0][:, :]), ALU.subtract).then_inc(s.xT.sem, 1)
        for l in range(1, LEVELS):
            if l < LEVELS - 1:
                v.wait_ge(s.xax_ps.sem, s.xax_ps.at(t, l))
                v.wait_ge(s.x.sem, s.x.at(t, l))
                v.tensor_tensor(b.xx[:, :], b.xx[:, :], B[2][:, :], ALU.subtract).then_inc(s.x.sem, 1)
            v.wait_ge(s.xaxT_ps.sem, s.xaxT_ps.at(t, l))
            v.wait_ge(s.xT.sem, s.xT.at(t, l))
            v.tensor_tensor(b.xT[:, :], b.xT[:, :], B[3][:, :], ALU.subtract).then_inc(s.xT.sem, 1)
            if more and l <= CT:
                modulate(t + 1, l - 1)
        v.wait_ge(s.xT.sem, s.xT.at(t))
        v.tensor_tensor(four(b.tT[:, :]), four(b.xT[:, :]), spread(b.beta[:, :], P), ALU.mult).then_inc(s.tT.sem, 1)
        for c in range(CT):
            v.wait_ge(s.dm_ps.sem, s.dm_ps.at(t, c + 1))
            v.wait_ge(s.m.sem, s.m.at(t, c))
            old, new = b.m[c % 2], b.m[1 - c % 2]
            v.tensor_tensor(new.rearrange("p k n -> p (k n)"), old.rearrange("p k n -> p (k n)"), B[7][:, :], ALU.add).then_inc(s.m.sem, 1)
            if more:
                normalise(t + 1, c)
        for o in range(KD):
            v.wait_ge(s.oT_hi.sem, s.oT_hi.at(t, o + 1))
            v.tensor_tensor(b.oT_lo[:, o, :], B[o][:, :], f32(b.oT_hi[:, o, :]), ALU.subtract).then_inc(s.oT_lo.sem, 1)
        v.wait_ge(s.h1_kept.sem, s.h1_kept.at(t))
        for i in range(2):
            v.wait_ge(s.wo_ps.sem, s.wo_ps.at(t, i + 1))
            v.tensor_tensor(b.xa[:, 2 * i:2 * i + 2, :], b.h1[:, 2 * i:2 * i + 2, :], B[2 + i][:, :].rearrange("p (c n) -> p c n", c=2),
                            ALU.add).then_inc(s.xa.sem, 1)
        if more:
            tokens(t + 1)
        v.wait_ge(s.rs3.sem, s.rs3.at(t))
        for c in range(CT):
            v.tensor_scalar(b.hn2[:, c, :], b.xa[:, c, :], b.rs3[:, c:c + 1], None, ALU.mult).then_inc(s.hn2.sem, 1)
        for k in range(KD):
            v.wait_ge(s.h2T_hi.sem, s.h2T_hi.at(t, k + 1))
            v.tensor_tensor(b.h2T_lo[:, k, :], B[4 + k][:, :], f32(b.h2T_hi[:, k, :]), ALU.subtract).then_inc(s.h2T_lo.sem, 1)
        for o in range(KH):
            v.wait_ge(s.sg.sem, s.sg.at(t, o + 1))
            v.wait_ge(s.up_ps.sem, s.up_ps.at(t, o + 1))
            v.tensor_tensor(B[2 + o][:, :], B[2 + o][:, :], b.sg[:, o, :], ALU.mult).then_inc(s.mm.sem, 1)
        for o in range(KH):
            v.wait_ge(s.mm_hi.sem, s.mm_hi.at(t, o + 1))
            v.tensor_tensor(b.mm_lo[:, o, :], B[2 + o][:, :], f32(b.mm_hi[:, o, :]), ALU.subtract).then_inc(s.mm_lo.sem, 1)
        for i in range(2):
            v.wait_ge(s.down_ps.sem, s.down_ps.at(t, i + 1))
            v.tensor_tensor(b.xa[:, 2 * i:2 * i + 2, :], b.xa[:, 2 * i:2 * i + 2, :], B[6 + i][:, :].rearrange("p (c n) -> p c n", c=2),
                            ALU.add).then_inc(s.y.sem, 1)

    stats(0)
    for c in range(CT):
        modulate(0, c)
    for c in range(CT):
        normalise(0, c)
    tokens(0)
    with v.Fori(0, NB - 1) as t:
        link.loop(t, PER)
        block(t, True)
    link.end(NB - 1)
    block(NB - 1, False)


def a_gpsimd(g, b, s, link):
    four = lambda ap: ap.rearrange("p (c n) -> p c n", c=CT)
    PER = 4

    def rs1(t):
        g.wait_ge(s.mv.sem, s.mv.at(t))
        absorb(g, b, 0)
        rsqrt(g, link, b.rs1[:, :], b.mv[:, :, 1:2].squeeze(2), b.neg_half[:, 0:CT], 1.0, LN_EPS).then_inc(s.rs1.sem, 1)

    def rs2(t):
        g.wait_ge(s.ss1.sem, s.ss1.at(t))
        absorb(g, b, 1)
        rsqrt(g, link, b.rs2[:, :], b.ss1[:, :], b.neg_half[:, 0:CT], 1.0 / D, RMS_EPS).then_inc(s.rs2.sem, 1)

    def rk(t):
        g.wait_ge(s.kss.sem, s.kss.at(t))
        absorb(g, b, 2)
        rsqrt(g, link, b.rk[:, :], b.kss[:, :], b.neg_half[:, 0:CT], 1.0, 0.0, floor=1e-24).then_inc(s.rk.sem, 1)

    def block(t, more):
        if more:
            rs1(t + 1)
        g.wait_ge(s.aT.sem, s.aT.at(t))
        for l in range(LEVELS):
            if l == 2:
                g.wait_ge(s.xT.sem, s.xT.at(t, 1))
            if l > 2:
                g.wait_ge(s.ax_ps.sem, s.ax_ps.at(t, l - 2))
            g.tensor_tensor(four(b.aTm[l % 2][:, :]), four(b.aT[:, :]), mid(b.maskT[:, l, :], CT), ALU.mult).then_inc((s.aTm if l else s.aTm0).sem, 1)
        if more:
            rs2(t + 1)
        g.wait_ge(s.ss2.sem, s.ss2.at(t))
        absorb(g, b, 3)
        rsqrt(g, link, b.rs3[:, :], b.ss2[:, :], b.neg_half[:, 0:CT], 1.0 / D, RMS_EPS).then_inc(s.rs3.sem, 1)
        if more:
            rk(t + 1)
        for c in range(CT):
            g.wait_ge(s.y.sem, s.y.at(t, c // 2 + 1))
            g.tensor_tensor(b.hn2[:, c, :], b.xa[:, c, :], b.mod[:, GA, :], ALU.mult).then_inc(s.gy.sem, 1)
            g.wait_ge(s.gy.sem, s.gy.at(t, c + 1))
            xt = b.x[:, bass.ds((t * CT + c) * D, D)]
            g.tensor_tensor(xt, xt, b.hn2[:, c, :], ALU.add).then_inc(s.x_done.sem, 1)

    rs1(0)
    rs2(0)
    rk(0)
    with g.Fori(0, NB - 1) as t:
        link.loop(t, PER)
        block(t, True)
    link.end(NB - 1)
    block(NB - 1, False)



def groups(eng):
    with eng.Fori(0, NB // 2) as q:
        for par in range(2):
            yield 2 * q + par, par


def staggered(eng):
    yield 0, 0, False, False, True
    yield 1, 1, True, False, True
    with eng.Fori(0, NB // 2 - 2) as q:
        for par in range(2):
            yield 2 * q + (2 + par), par, True, True, True
    yield NB - 2, 0, True, True, True
    yield NB - 1, 1, True, True, False


def prep_vector(v, b, s, kind, r):
    cm, sm = (CA, SA) if kind == "C" else (CB, SB)

    def stats(t, par):
        for c in range(CT):
            v.bn_stats(b.p_stats[par][:, c, :], b.x[:, bass.ds((t * CT + c) * D, D)]).then_inc(r.stats.sem, 1)
        v.wait_ge(r.stats.sem, r.stats.at(t))
        absorb(v, b, par)
        for c in range(CT):
            v.bn_aggr(b.p_mv[par][:, c, :], b.p_stats[par][:, c, :]).then_inc(r.mv.sem, 1)

    def modulate(t, par):
        v.wait_ge(r.rs.sem, r.rs.at(t))
        h = b.p_h[par]
        for c in range(CT):
            if kind == "B1":
                v.scalar_tensor_tensor(h[:, c, :], b.y[:, bass.ds((t * CT + c) * D, D)], b.p_rs[par][:, c:c + 1], b.rows[:, ROW["norm_w"]:ROW["norm_w"] + D],
                                       ALU.mult, ALU.mult).then_inc(r.h.sem, 1)
            else:
                v.scalar_tensor_tensor(h[:, c, :], b.x[:, bass.ds((t * CT + c) * D, D)], b.p_mv[par][:, c, 0:1], b.mod[:, cm, :],
                                       ALU.subtract, ALU.mult).then_inc(r.xn.sem, 1)
        if kind != "B1":
            for c in range(CT):
                v.wait_ge(r.xn.sem, r.xn.at(t, c + 1))
                v.scalar_tensor_tensor(h[:, c, :], h[:, c, :], b.p_rs[par][:, c:c + 1], b.mod[:, sm, :], ALU.mult, ALU.add).then_inc(r.h.sem, 1)

    def gate(t, par):
        for c in range(CT):
            v.wait_ge(r.h.sem, r.h.at(t, c + 1))
            v.tensor_tensor(b.p_gh[par][:, c, :], b.p_h[par][:, c, :], b.mod[:, GB, :], ALU.mult).then_inc(r.gh.sem, 1)

    def normalise(t, par):
        v.wait_ge(r.rs2.sem, r.rs2.at(t))
        for c in range(CT):
            v.tensor_scalar(b.p_xn[par][:, c, :], b.p_h[par][:, c, :], b.p_rs2[par][:, c:c + 1], None, ALU.mult).then_inc(r.hn.sem, 1)

    def low(t, par):
        for k in range(KD):
            v.wait_ge(r.hT_hi.sem, r.hT_hi.at(t, k + 1))
            v.tensor_tensor(b.hT_lo_all[:, k, bass.ds(t * TB, TB)], b.bank[2 * par + k][:, :], b.hT_hi_all[:, k, bass.ds(t * TB, TB)].bitcast(F32),
                            ALU.subtract).then_inc(r.hT_lo.sem, 1)
        if kind != "C":
            E = E1 if kind == "D" else E0
            v.wait_ge(r.logit_ps.sem, r.logit_ps.at(t))
            src = b.bank[4 + par][:, 0:CT * E].rearrange("p (c e) -> p c e", c=CT)
            dst = b.logits[:, bass.ds(t * CT, CT), 0:E]
            if kind == "D":
                v.tensor_copy(dst, src).then_inc(r.logits.sem, 1)
            else:
                row = ROW["rb"] + (kind == "B1") * E0
                v.tensor_tensor(dst, src, mid(b.rows[:, row:row + E0], CT), ALU.add).then_inc(r.logits.sem, 1)

    if kind != "B1":
        stats(0, 0)
    for t, par, second, third, more in staggered(v):
        if kind == "D" and third:
            v.wait_ge(r.hn.sem, r.hn.at(t - 2))
        modulate(t, par)
        if kind != "B1" and more:
            stats(t + 1, 1 - par)
        if kind == "D":
            gate(t, par)
            if second:
                normalise(t - 1, 1 - par)
            if third:
                low(t - 2, par)
        elif second:
            low(t - 1, 1 - par)
    if kind == "D":
        normalise(NB - 1, 1)
        low(NB - 2, 0)
    low(NB - 1, 1)


def prep_gpsimd(g, b, s, link, kind, r):
    def rs(t, par):
        if kind == "B1":
            g.wait_ge(r.ss.sem, r.ss.at(t))
            absorb(g, b, par)
            g.tensor_scalar(b.p_rs[par][:, :], b.p_ss[par][:, :], 1.0 / D, RMS_EPS, ALU.mult, ALU.add).then_inc(r.var.sem, 1)
        else:
            g.wait_ge(r.mv.sem, r.mv.at(t))
            absorb(g, b, par)
            g.tensor_scalar(b.p_rs[par][:, :], b.p_mv[par][:, :, 1:2].squeeze(2), 1.0, LN_EPS, ALU.mult, ALU.add).then_inc(r.var.sem, 1)
        g.wait_ge(r.var.sem, r.var.at(t))
        g.tensor_tensor(b.p_rs[par][:, :], b.p_rs[par][:, :], b.neg_half[:, 0:CT], ALU.pow).then_inc(r.rs.sem, 1)

    if kind != "D":
        for t, par in groups(g):
            rs(t, par)
        return
    rs(0, 0)
    for t, par, _, _, more in staggered(g):
        if more:
            rs(t + 1, 1 - par)
        g.wait_ge(r.ss.sem, r.ss.at(t))
        absorb(g, b, 2 + par)
        g.tensor_scalar(b.p_rs2[par][:, :], b.p_ss[par][:, :], 1.0 / D, RMS_EPS, ALU.mult, ALU.add).then_inc(r.var2.sem, 1)
        g.wait_ge(r.var2.sem, r.var2.at(t))
        g.tensor_tensor(b.p_rs2[par][:, :], b.p_rs2[par][:, :], b.neg_half[:, 0:CT], ALU.pow).then_inc(r.rs2.sem, 1)
        for c in range(CT):
            xt = b.x[:, bass.ds((t * CT + c) * D, D)]
            g.wait_ge(r.gh.sem, r.gh.at(t, c + 1))
            g.tensor_tensor(xt, xt, b.p_gh[par][:, c, :], ALU.add).then_inc(r.xh.sem, 1)


def prep_scalar(act, b, s, kind, r):
    def squares(t, par):
        for c in range(CT):
            if kind == "B1":
                act.activation(b.p_xn[par][:, c, :], b.y[:, bass.ds((t * CT + c) * D, D)], ACT.Square, accum_out=b.p_ss[par][:, c:c + 1]).then_inc(r.ss.sem, 1)
            else:
                act.wait_ge(r.h.sem, r.h.at(t, c + 1))
                act.activation(b.p_sq[par][:, c, :], b.p_h[par][:, c, :], ACT.Square, accum_out=b.p_ss[par][:, c:c + 1]).then_inc(r.ss.sem, 1)

    def take(t, par):
        if kind in ("B0", "B1"):
            act.wait_ge(r.h.sem, r.h.at(t))
            absorb(act, b, par)
            act.activation(b.y[:, bass.ds(t * CT * D, CT * D)], flat(b.p_h[par][:, :, :]), ACT.Copy).then_inc(r.y.sem, 1)
        for k in range(KD):
            act.wait_ge(r.hT_ps.sem, r.hT_ps.at(t, k + 1))
            if kind != "C":
                act.activation(b.p_hT[par][:, k, :], b.bank[2 * par + k][:, :], ACT.Copy).then_inc(r.hT.sem, 1)
            else:
                absorb(act, b, 2 * par + k)
            act.activation(b.hT_hi_all[:, k, bass.ds(t * TB, TB)], b.bank[2 * par + k][:, :], ACT.Copy).then_inc(r.hT_hi.sem, 1)

    if kind == "B1":
        squares(0, 0)
    for t, par, second, third, more in staggered(act):
        if kind == "B1" and more:
            squares(t + 1, 1 - par)
        if kind == "D":
            squares(t, par)
            if second:
                take(t - 1, 1 - par)
        else:
            take(t, par)
    if kind == "D":
        take(NB - 1, 1)


def prep_tensor(pe, b, s, kind, r):
    for t, par in groups(pe):
        src = b.p_xn if kind == "D" else b.p_h
        ready = r.hn if kind == "D" else r.h
        pe.wait_ge(ready.sem, ready.at(t))
        pe.wait_ge(r.free.sem, r.free.at(t - 2))
        for k in range(KD):
            for c in range(CT):
                ins = pe.transpose(b.bank[2 * par + k][:, c * P:(c + 1) * P], src[par][:, c, k * P:(k + 1) * P], b.ident)
            ins.then_inc(r.hT_ps.sem, 1)
        if kind != "C":
            E = E1 if kind == "D" else E0
            router = b.router[kind]
            pe.wait_ge(r.hT.sem, r.hT.at(t))
            for c in range(CT):
                for k in range(KD):
                    ins = pe.matmul(b.bank[4 + par][:, c * E:(c + 1) * E], b.p_hT[par][:, k, c * P:(c + 1) * P], router[:, k, :],
                                    start=k == 0, stop=k == KD - 1)
            ins.then_inc(r.logit_ps.sem, 1)


def routing_vector(v, b, s, link, kind):
    E, first = (E1, 0) if kind == "D" else (E0, NS)
    g = b.logits[:, :, 0:E]
    z, t, one, two = (x[:, :, 0:E] for x in (b.r_z, b.r_t, b.r_one, b.r_two))
    top, ga, gb = b.r_top[:, :], b.r_ga[:, :], b.r_gb[:, :]
    rank = mid(b.rank[:, 0:E], NT)
    if kind == "D":
        v.tensor_copy(z, g).then_inc(link.sem, 1)
        v.wait_ge(link.sem, link.next())
    else:
        row = ROW["gb"] + (kind == "B1") * E0
        v.tensor_tensor(z, g, mid(b.rows[:, row:row + E0], NT), ALU.add).then_inc(link.sem, 1)
        v.wait_ge(link.sem, link.next())
    for pick, gate in ((one, ga), (two, gb)):
        if pick is two:
            v.tensor_scalar(t, one, -2.0, 1.0, ALU.mult, ALU.add).then_inc(link.sem, 1)
            v.wait_ge(link.sem, link.next())
            v.tensor_scalar(t, t, BIG, None, ALU.mult).then_inc(link.sem, 1)
            v.wait_ge(link.sem, link.next())
            v.tensor_tensor(z, z, t, ALU.min).then_inc(link.sem, 1)
            v.wait_ge(link.sem, link.next())
        v.tensor_reduce(top, z, AX.X, ALU.max).then_inc(link.sem, 1)
        v.wait_ge(link.sem, link.next())
        v.tensor_tensor(t, z, spread(top, E), ALU.is_equal).then_inc(link.sem, 1)
        v.wait_ge(link.sem, link.next())
        v.tensor_tensor(t, t, rank, ALU.mult).then_inc(link.sem, 1)
        v.wait_ge(link.sem, link.next())
        v.tensor_reduce(top, t, AX.X, ALU.max).then_inc(link.sem, 1)
        v.wait_ge(link.sem, link.next())
        v.tensor_tensor(pick, t, spread(top, E), ALU.is_equal).then_inc(link.sem, 1)
        v.wait_ge(link.sem, link.next())
        v.tensor_tensor(t, pick, g, ALU.mult).then_inc(link.sem, 1)
        v.wait_ge(link.sem, link.next())
        v.tensor_reduce(gate, t, AX.X, ALU.add).then_inc(link.sem, 1)
        v.wait_ge(link.sem, link.next())
    v.tensor_tensor(top, ga, gb, ALU.max).then_inc(link.sem, 1)
    v.wait_ge(link.sem, link.next())
    v.tensor_tensor(ga, ga, top, ALU.subtract).then_inc(link.sem, 1)
    v.wait_ge(link.sem, link.next())
    v.tensor_tensor(gb, gb, top, ALU.subtract).then_inc(s.gates[kind].sem, 1)
    v.wait_ge(s.gate_exp[kind].sem, s.gate_exp[kind].at(0))
    v.tensor_tensor(top, ga, gb, ALU.add).then_inc(link.sem, 1)
    v.wait_ge(link.sem, link.next())
    v.reciprocal(top, top).then_inc(link.sem, 1)
    v.wait_ge(link.sem, link.next())
    v.tensor_tensor(ga, ga, top, ALU.mult).then_inc(link.sem, 1)
    v.wait_ge(link.sem, link.next())
    v.tensor_tensor(gb, gb, top, ALU.mult).then_inc(link.sem, 1)
    v.wait_ge(link.sem, link.next())
    v.tensor_tensor(one, one, spread(ga, E), ALU.mult).then_inc(link.sem, 1)
    v.wait_ge(link.sem, link.next())
    v.tensor_tensor(two, two, spread(gb, E), ALU.mult).then_inc(link.sem, 1)
    v.wait_ge(link.sem, link.next())
    v.tensor_tensor(b.weight[:, first:first + E, :].rearrange("p e t -> p t e"), one, two, ALU.add).then_inc(link.sem, 1)
    v.wait_ge(link.sem, link.next())


def routing_scalar(act, b, s, kind):
    act.wait_ge(s.gates[kind].sem, s.gates[kind].at(0))
    act.activation(b.r_ga[:, :], b.r_ga[:, :], ACT.Exp).then_inc(s.gate_exp[kind].sem, 1)
    act.activation(b.r_gb[:, :], b.r_gb[:, :], ACT.Exp).then_inc(s.gate_exp[kind].sem, 1)



class Step:
    def __init__(self, i, t, par, unit):
        self.i, self.t, self.par, self.unit = i, t, par, unit


def pair_steps(eng, p, i0):
    def at(j, expr=None):
        j0 = j if expr is None else expr
        return Step(2 * NB * p + j0 + i0, j0 - NB * (j // NB), j % 2, j // NB)

    yield at(0), at(1), None
    for unit in range(2):
        o = unit * NB
        with eng.Fori(0, NB // 2 - 1) as q:
            for n in (1, 2):
                e = 2 * q + (o + n)
                yield at(o + n, e), at(o + n + 1, e + 1) if n == 1 else Step(2 * NB * p + e + 1 + i0, e + 1 - o, 1, unit), at(o + n - 1, e - 1)
        if unit == 0:
            yield at(NB - 1), at(NB), at(NB - 2)
            yield at(NB), at(NB + 1), at(NB - 1)
    yield at(2 * NB - 1), None, at(2 * NB - 2)


def feature_block(b, st, k):
    return b.hT_hi_all[:, k, bass.ds(st.t * TB, TB)], b.hT_lo_all[:, k, bass.ds(st.t * TB, TB)]


def b_experts_tensor(pe, b, s, r, rnd):
    B = b.bank
    i0, p0 = rnd * U0 * NB, rnd * (U0 // 2)

    def part(st, mat, k, c0, w):
        return tuple(x[st.unit][:, mat * KD + k, c0:c0 + w] for x in (b.w_hi, b.w_lo))

    def up(st):
        pe.wait_ge(r.m_lo.sem, r.m_lo.at(st.i - 2))
        for o in range(KD):
            three(pe, B[2 * st.par + o][:, :], [part(st, 0, k, o * P, P) for k in range(KD)], [feature_block(b, st, k) for k in range(KD)]).then_inc(r.up_ps.sem, 1)

    def gate(st):
        pe.wait_ge(r.h_lo.sem, r.h_lo.at(st.i))
        pe.wait_ge(r.sg.sem, r.sg.at(st.i - 1))
        for o in range(KD):
            three(pe, B[4 + o][:, :], [part(st, 1, k, o * P, P) for k in range(KD)], [(b.h_hi[:, k, :], b.h_lo[:, k, :]) for k in range(KD)]).then_inc(r.gate_ps.sem, 1)

    def down(st, p):
        pe.wait_ge(r.m_lo.sem, r.m_lo.at(st.i))
        pe.wait_ge(r.acc.sem, r.acc.at(st.i - 1))
        for c in range(CT):
            out = B[6 + c // 2][:, (c % 2) * D:(c % 2 + 1) * D]
            three(pe, out, [(b.m_hi[st.par][:, k, c * P:(c + 1) * P], b.m_lo[st.par][:, k, c * P:(c + 1) * P]) for k in range(KD)],
                  [part(st, 2, k, 0, D) for k in range(KD)], last=False)
            ins = pe.matmul(out, b.ones_r[:, :], b.bias_all[:, bass.ds((2 * p + st.unit) * D, D)], start=False, stop=True)
            if c % 2:
                ins.then_inc(r.down_ps.sem, 1)

    with pe.Fori(0, U0 // 2) as p:
        for st, after, before in pair_steps(pe, p, i0):
            if before is None:
                pe.wait_ge(b.split[0].sem, b.split[0].at(p0 + p))
                up(st)
            gate(st)
            if after is not None:
                if after.unit != st.unit:
                    pe.wait_ge(b.split[1].sem, b.split[1].at(p0 + p))
                up(after)
            if before is not None:
                down(before, p)
            if after is None:
                down(st, p)


def b_experts_scalar(act, b, s, r, rnd):
    B = b.bank
    i0, p0 = rnd * U0 * NB, rnd * (U0 // 2)

    def h_hi(st):
        for o in range(KD):
            act.wait_ge(r.up_ps.sem, r.up_ps.at(st.i, o + 1))
            act.activation(b.h_hi[:, o, :], B[2 * st.par + o][:, :], ACT.Identity, bias=b.bias_cols[st.unit][:, o:o + 1]).then_inc(r.h_hi.sem, 1)

    with act.Fori(0, U0 // 2) as p:
        for st, after, before in pair_steps(act, p, i0):
            if before is None:
                act.wait_ge(b.split[0].sem, b.split[0].at(p0 + p))
                h_hi(st)
            for o in range(KD):
                act.wait_ge(r.gate_ps.sem, r.gate_ps.at(st.i, o + 1))
                act.wait_ge(r.m.sem, r.m.at(st.i - 1, o + 1))
                act.activation(b.sgate[:, o, :], B[4 + o][:, :], ACT.Silu, bias=b.bias_cols[st.unit][:, KD + o:KD + o + 1]).then_inc(r.sg.sem, 1)
            for o in range(KD):
                act.wait_ge(r.m.sem, r.m.at(st.i, o + 1))
                act.activation(b.m_hi[st.par][:, o, :], B[2 * st.par + o][:, :], ACT.Copy).then_inc(r.m_hi.sem, 1)
            if after is not None:
                if after.unit != st.unit:
                    act.wait_ge(b.split[1].sem, b.split[1].at(p0 + p))
                h_hi(after)


def b_experts_vector(v, b, s, r, rnd):
    B = b.bank
    i0 = rnd * U0 * NB

    def h_lo(st):
        for o in range(KD):
            v.wait_ge(r.h_hi.sem, r.h_hi.at(st.i, o + 1))
            v.scalar_tensor_tensor(b.h_lo[:, o, :], B[2 * st.par + o][:, :], b.bias_cols[st.unit][:, o:o + 1], b.h_hi[:, o, :].bitcast(F32),
                                   ALU.add, ALU.subtract).then_inc(r.h_lo.sem, 1)

    with v.Fori(0, U0 // 2) as p:
        for st, after, before in pair_steps(v, p, i0):
            if before is None:
                h_lo(st)
            for o in range(KD):
                v.wait_ge(r.sg.sem, r.sg.at(st.i, o + 1))
                bank = B[2 * st.par + o][:, :]
                v.scalar_tensor_tensor(bank, bank, b.bias_cols[st.unit][:, o:o + 1], b.sgate[:, o, :], ALU.add, ALU.mult).then_inc(r.m.sem, 1)
            for o in range(KD):
                v.wait_ge(r.m_hi.sem, r.m_hi.at(st.i, o + 1))
                v.tensor_tensor(b.m_lo[st.par][:, o, :], B[2 * st.par + o][:, :], b.m_hi[st.par][:, o, :].bitcast(F32), ALU.subtract).then_inc(r.m_lo.sem, 1)
            if after is not None:
                h_lo(after)
            if before is not None:
                accumulate(v, b, r, before, p, b.y, (B[6], B[7]))
            if after is None:
                accumulate(v, b, r, st, p, b.y, (B[6], B[7]))


def accumulate(v, b, r, st, p, to, banks):
    for c in range(CT):
        if c % 2 == 0:
            v.wait_ge(r.down_ps.sem, r.down_ps.at(st.i, c // 2 + 1))
        tile = to[:, bass.ds((st.t * CT + c) * D, D)]
        w = b.weight_flat[:, bass.ds((2 * p + st.unit) * NT + st.t * CT + c, 1)]
        v.scalar_tensor_tensor(tile, banks[c // 2][:, (c % 2) * D:(c % 2 + 1) * D], w, tile, ALU.mult, ALU.add).then_inc(r.acc.sem, 1)


def weights_sync(sp, b, dram, raw, rnd, pairs, split, loaded):
    with sp.Fori(0, pairs) as p:
        for unit in range(2):
            sp.wait_ge(split[1 - unit].sem, split[1 - unit].at(rnd * pairs + p + unit - 1))
            sp.dma_start(raw[:, :], dram[bass.ds(2 * p + unit, 1), :, :].squeeze(0)).then_inc(loaded[unit].sem, 16)


def weights_gpsimd(g, b, link, rnd, pairs, prepare, raw, hi, lo, split, loaded, r):
    with g.Fori(0, pairs) as p:
        link.loop(p, prepare.per)
        for unit in range(2):
            g.wait_ge(loaded[unit].sem, loaded[unit].at(rnd * pairs + p))
            g.wait_ge(r.down_ps.sem, r.down_ps.at(2 * NB * (rnd * pairs + p - 1) + NB * (unit + 1) - 1))
            absorb(g, b)
            prepare(g, link, p, unit)
            g.tensor_copy(hi[unit], raw[:, :]).then_inc(link.sem, 1)
            g.wait_ge(link.sem, link.next())
            g.tensor_tensor(lo[unit], raw[:, :], hi[unit].bitcast(F32), ALU.subtract).then_inc(split[unit].sem, 1)
    link.end(pairs)


def bias_table_vector(v, b, link, raw, tmp, scale):
    if scale is not None:
        v.tensor_tensor(raw.rearrange("p (u n) -> p u n", n=D), raw.rearrange("p (u n) -> p u n", n=D), mid(scale, EP), ALU.mult).then_inc(link.sem, 1)
        v.wait_ge(link.sem, link.next())
    v.tensor_copy(tmp.bitcast(F32R), raw).then_inc(link.sem, 1)
    v.wait_ge(link.sem, link.next())
    v.tensor_scalar(raw, raw, b.ident[:, 1:2], None, ALU.mult).then_inc(link.sem, 1)
    v.wait_ge(link.sem, link.next())
    v.tensor_scalar(b.row_sign[:, :], b.ident[:, 1:2], -2.0, 1.0, ALU.mult, ALU.add).then_inc(link.sem, 1)
    v.wait_ge(link.sem, link.next())
    v.scalar_tensor_tensor(b.bias_all[:, :], tmp, b.row_sign[:, :], raw, ALU.mult, ALU.add).then_inc(link.sem, 1)
    v.wait_ge(link.sem, link.next())


def close_scalar(act, b, r):
    for t, par in groups(act):
        act.wait_ge(r.xn.sem, r.xn.at(t - 2))
        absorb(act, b, par)
        for c in range(CT):
            act.activation(b.p_h[par][:, c, :], b.y[:, bass.ds((t * CT + c) * D, D)], ACT.Square, accum_out=b.p_ss[par][:, c:c + 1]).then_inc(r.ss.sem, 1)


def close_gpsimd(g, b, r):
    for t, par in groups(g):
        g.wait_ge(r.ss.sem, r.ss.at(t))
        absorb(g, b, par)
        g.tensor_scalar(b.p_rs[par][:, :], b.p_ss[par][:, :], 1.0 / D, RMS_EPS, ALU.mult, ALU.add).then_inc(r.var.sem, 1)
        g.wait_ge(r.var.sem, r.var.at(t))
        g.tensor_tensor(b.p_rs[par][:, :], b.p_rs[par][:, :], b.neg_half[:, 0:CT], ALU.pow).then_inc(r.rs.sem, 1)


def close_vector(v, b, r):
    for t, par in groups(v):
        v.wait_ge(r.rs.sem, r.rs.at(t))
        for c in range(CT):
            v.scalar_tensor_tensor(b.p_xn[par][:, c, :], b.y[:, bass.ds((t * CT + c) * D, D)], b.p_rs[par][:, c:c + 1], b.norm_gate[:, :],
                                   ALU.mult, ALU.mult).then_inc(r.xn.sem, 1)
        for c in range(CT):
            v.wait_ge(r.xn.sem, r.xn.at(t, c + 1))
            xt = b.x[:, bass.ds((t * CT + c) * D, D)]
            v.tensor_tensor(xt, xt, b.p_xn[par][:, c, :], ALU.add).then_inc(r.x.sem, 1)



def softplus_scale_vector(v, b, s, link):
    v.wait_ge(s.head_scale.sem, s.head_scale.at(0))
    v.tensor_scalar(b.c_scale[:, :], b.c_scale[:, :], DH ** -0.5, None, ALU.mult).then_inc(link.sem, 1)
    v.wait_ge(link.sem, link.next())
    for j, name in enumerate(("bq", "bk")):
        v.tensor_tensor(b.c_bias[:, j * KD:(j + 1) * KD], b.cols[:, COL[name]:COL[name] + KD], b.c_scale[:, :], ALU.mult).then_inc(link.sem, 1)
        v.wait_ge(link.sem, link.next())


def c_weights_vector(v, b, s, link):
    for i, name in enumerate(C_MATS):
        v.wait_ge(s.load_c[i].sem, s.load_c[i].at(0))
        raw, hi, lo = b.c_raw[name], b.c_hi[name], b.c_lo[name]
        v.tensor_copy(hi, raw).then_inc(link.sem, 1)
        v.wait_ge(link.sem, link.next())
        v.tensor_tensor(lo, raw, hi.bitcast(F32), ALU.subtract).then_inc(s.c_w.sem, 1)


C_MATS = ("c_wq", "c_wk", "c_wv", "c_wo")


def c_tensor(pe, b, s, r):
    B = b.bank
    W = lambda name, k, c0=0, w=D: (b.c_hi[name][:, k, c0:c0 + w], b.c_lo[name][:, k, c0:c0 + w])

    def project(t):
        pe.wait_ge(r.y.sem, r.y.at(t - 1))
        h = [(b.hT_hi_all[:, k, bass.ds(t * TB, TB)], b.hT_lo_all[:, k, bass.ds(t * TB, TB)]) for k in range(KD)]
        for j, name in enumerate(C_MATS[:3]):
            if j == 2:
                pe.wait_ge(r.v.sem, r.v.at(t - 1))
            for o in range(KD):
                three(pe, B[2 * j + o][:, :], [W(name, k, o * P, P) for k in range(KD)], h).then_inc(r.qkv_ps.sem, 1)

    def attend(t):
        pe.wait_ge(r.o_taken.sem, r.o_taken.at(t - 1))
        for o in range(KD):
            pe.wait_ge(r.qk_lo.sem, r.qk_lo.at(t, o + 1))
            pe.matmul(B[6 + o][:, :], b.heads_r[:, :], b.qk_hi[:, o, :], start=True, stop=False)
            pe.matmul(B[6 + o][:, :], b.heads_r[:, :], b.qk_lo[:, o, :], start=False, stop=True).then_inc(r.den_ps.sem, 1)
        pe.wait_ge(r.out_lo.sem, r.out_lo.at(t))
        for c in range(CT):
            ins = three(pe, B[6 + c // 2][:, (c % 2) * D:(c % 2 + 1) * D],
                        [(b.out_hi[:, k, c * P:(c + 1) * P], b.out_lo[:, k, c * P:(c + 1) * P]) for k in range(KD)], [W("c_wo", k) for k in range(KD)])
            if c % 2:
                ins.then_inc(r.o_ps.sem, 1)

    project(0)
    with pe.Fori(0, NB - 1) as t:
        project(t + 1)
        attend(t)
    attend(NB - 1)


def c_scalar(act, b, s, r):
    B = b.bank

    def take(t):
        for j in range(2 * KD):
            act.wait_ge(r.qkv_ps.sem, r.qkv_ps.at(t, j + 1))
            if j == 0:
                act.wait_ge(r.soft.sem, r.soft.at(t - 1))
            act.activation(b.c_y[:, j, :], B[j][:, :], ACT.Identity, bias=b.c_bias[:, j:j + 1], scale=b.c_scale[:, j % KD:j % KD + 1]).then_inc(r.y.sem, 1)

    def soften(t):
        half = lambda x, j: x[:, j * KD:(j + 1) * KD, :].rearrange("p k n -> p (k n)")
        act.wait_ge(r.y.sem, r.y.at(t))
        for j in range(2):
            act.activation(half(b.c_e, j), half(b.c_y, j), ACT.Abs).then_inc(r.abs.sem, 1)
        for j in range(2):
            act.wait_ge(r.abs.sem, r.abs.at(t, j + 1))
            act.activation(half(b.c_e, j), half(b.c_e, j), ACT.Exp, scale=-1.0).then_inc(r.exp.sem, 1)
        for j in range(2):
            act.wait_ge(r.exp.sem, r.exp.at(t, j + 1))
            act.activation(half(b.c_l, j), half(b.c_e, j), ACT.Ln, bias=b.ones[:, 0:1]).then_inc(r.ln.sem, 1)
        for o in range(KD):
            act.wait_ge(r.qk.sem, r.qk.at(t))
            act.activation(b.qk_hi[:, o, :], b.c_qk[:, o, :], ACT.Copy).then_inc(r.qk_hi.sem, 1)
        for o in range(KD):
            act.wait_ge(r.out.sem, r.out.at(t, o + 1))
            act.activation(b.out_hi[:, o, :], b.c_out[:, o, :], ACT.Copy).then_inc(r.out_hi.sem, 1)

    take(0)
    with act.Fori(0, NB - 1) as t:
        soften(t)
        take(t + 1)
    soften(NB - 1)


def c_gpsimd(g, b, s, r):
    with g.Fori(0, NB) as t:
        for j in range(2):
            half = lambda x: x[:, j * KD:(j + 1) * KD, :].rearrange("p k n -> p (k n)")
            g.wait_ge(r.exp.sem, r.exp.at(t, j + 1))
            absorb(g, b)
            g.tensor_scalar(half(b.c_t), half(b.c_e), -0.5, 1.0, ALU.mult, ALU.add).then_inc(r.tail0.sem, 1)
            g.wait_ge(r.tail0.sem, r.tail0.at(t, j + 1))
            g.tensor_tensor(half(b.c_t), half(b.c_t), half(b.c_e), ALU.mult).then_inc(r.tail.sem, 1)
        for c in range(CT):
            g.wait_ge(r.o_taken.sem, r.o_taken.at(t, c // 2 + 1))
            g.tensor_tensor(b.c_o[:, c, :], b.c_o[:, c, :], b.mod[:, GA, :], ALU.mult).then_inc(r.go.sem, 1)
            g.wait_ge(r.go.sem, r.go.at(t, c + 1))
            xt = b.x[:, bass.ds((t * CT + c) * D, D)]
            g.tensor_tensor(xt, xt, b.c_o[:, c, :], ALU.add).then_inc(r.x.sem, 1)


def c_vector(v, b, s, r):
    B = b.bank
    with v.Fori(0, NB) as t:
        for o in range(KD):
            v.wait_ge(r.qkv_ps.sem, r.qkv_ps.at(t, 2 * KD + o + 1))
            v.tensor_scalar(b.c_v[:, o, :], B[4 + o][:, :], b.cols[:, COL["bv"] + o:COL["bv"] + o + 1], None, ALU.add).then_inc(r.v.sem, 1)
        for j in range(2):
            half = lambda x: x[:, j * KD:(j + 1) * KD, :].rearrange("p k n -> p (k n)")
            v.wait_ge(r.ln.sem, r.ln.at(t, j + 1))
            v.wait_ge(r.tail.sem, r.tail.at(t, j + 1))
            v.tensor_tensor(half(b.c_l), half(b.c_l), half(b.c_t), ALU.max).then_inc(r.lmax.sem, 1)
            v.wait_ge(r.lmax.sem, r.lmax.at(t, j + 1))
            v.scalar_tensor_tensor(half(b.c_l), half(b.c_y), 0.0, half(b.c_l), ALU.max, ALU.add).then_inc(r.soft.sem, 1)
        v.wait_ge(r.soft.sem, r.soft.at(t))
        v.tensor_tensor(b.c_qk[:, :, :], b.c_l[:, 0:KD, :], b.c_l[:, KD:2 * KD, :], ALU.mult).then_inc(r.qk.sem, 1)
        for o in range(KD):
            v.wait_ge(r.qk_hi.sem, r.qk_hi.at(t, o + 1))
            v.tensor_tensor(b.qk_lo[:, o, :], b.c_qk[:, o, :], b.qk_hi[:, o, :].bitcast(F32), ALU.subtract).then_inc(r.qk_lo.sem, 1)
        for o in range(KD):
            v.wait_ge(r.den_ps.sem, r.den_ps.at(t, o + 1))
            v.tensor_tensor(b.c_v[:, o, :], b.c_v[:, o, :], B[6 + o][:, :], ALU.mult).then_inc(r.num.sem, 1)
            v.reciprocal(b.c_r[:, o, :], B[6 + o][:, :]).then_inc(r.rden.sem, 1)
            v.wait_ge(r.rden.sem, r.rden.at(t, o + 1))
            v.tensor_tensor(b.c_out[:, o, :], b.c_v[:, o, :], b.c_r[:, o, :], ALU.mult).then_inc(r.out.sem, 1)
        for o in range(KD):
            v.wait_ge(r.out_hi.sem, r.out_hi.at(t, o + 1))
            v.tensor_tensor(b.out_lo[:, o, :], b.c_out[:, o, :], b.out_hi[:, o, :].bitcast(F32), ALU.subtract).then_inc(r.out_lo.sem, 1)
        v.wait_ge(r.x.sem, r.x.at(t - 1))
        for i in range(2):
            v.wait_ge(r.o_ps.sem, r.o_ps.at(t, i + 1))
            v.tensor_tensor(b.c_o[:, 2 * i:2 * i + 2, :], B[6 + i][:, :].rearrange("p (c n) -> p c n", c=2), mid(b.rows[:, ROW["bo"]:ROW["bo"] + D], 2),
                            ALU.add).then_inc(r.o_taken.sem, 1)


def d_experts_tensor(pe, b, s, r):
    B = b.bank

    def up(st):
        for o in range(KH):
            pe.wait_ge(r.m_lo.sem, r.m_lo.at(st.i - 1, o + 1))
            three(pe, B[o][:, :], [(b.v1_hi[st.unit][:, k, o * P:(o + 1) * P], b.v1_lo[st.unit][:, k, o * P:(o + 1) * P]) for k in range(KD)],
                  [feature_block(b, st, k) for k in range(KD)]).then_inc(r.up_ps.sem, 1)

    def down(st, p):
        pe.wait_ge(r.m_lo.sem, r.m_lo.at(st.i))
        pe.wait_ge(r.acc.sem, r.acc.at(st.i - 2))
        for c in range(CT):
            out = B[4 + 2 * st.par + c // 2][:, (c % 2) * D:(c % 2 + 1) * D]
            three(pe, out, [(b.m_hi[st.par][:, k, c * P:(c + 1) * P], b.m_lo[st.par][:, k, c * P:(c + 1) * P]) for k in range(KH)],
                  [(b.v2_hi[st.unit][:, k, :], b.v2_lo[st.unit][:, k, :]) for k in range(KH)], last=False)
            ins = pe.matmul(out, b.ones_r[:, :], b.bias_all[:, bass.ds((2 * p + st.unit) * D, D)], start=False, stop=True)
            if c % 2:
                ins.then_inc(r.down_ps.sem, 1)

    with pe.Fori(0, E1 // 2) as p:
        for st, after, before in pair_steps(pe, p, 0):
            if before is None:
                pe.wait_ge(b.split1[0].sem, b.split1[0].at(p))
                up(st)
            if after is not None:
                if after.unit != st.unit:
                    pe.wait_ge(b.split1[1].sem, b.split1[1].at(p))
                up(after)
            down(st, p)


def d_experts_scalar(act, b, s, r):
    with act.Fori(0, E1 // 2) as p:
        for st, after, before in pair_steps(act, p, 0):
            for o in range(KH):
                act.wait_ge(r.up_ps.sem, r.up_ps.at(st.i, o + 1))
                act.activation(b.bank[o][:, :], b.bank[o][:, :], ACT.Gelu, bias=b.bias_cols1[st.unit][:, o:o + 1]).then_inc(r.m.sem, 1)
            for o in range(KH):
                act.wait_ge(r.m.sem, r.m.at(st.i, o + 1))
                act.activation(b.m_hi[st.par][:, o, :], b.bank[o][:, :], ACT.Copy).then_inc(r.m_hi.sem, 1)


def d_experts_vector(v, b, s, r):
    with v.Fori(0, E1 // 2) as p:
        for st, after, before in pair_steps(v, p, 0):
            for o in range(KH):
                v.wait_ge(r.m_hi.sem, r.m_hi.at(st.i, o + 1))
                v.tensor_tensor(b.m_lo[st.par][:, o, :], b.bank[o][:, :], b.m_hi[st.par][:, o, :].bitcast(F32), ALU.subtract).then_inc(r.m_lo.sem, 1)
            for x in ((before, st) if after is None else (before,)):
                if x is not None:
                    accumulate(v, b, r, x, p, b.x, b.bank[4 + 2 * x.par:6 + 2 * x.par])




def program(nc, d, out):
    ctx = ExitStack()
    with ctx:
        b = Names()
        b.gpsimd, b.scalar = nc.gpsimd, nc.scalar

        def sb(scope, name, shape, dt=F32):
            return scope.enter_context(nc.sbuf_tensor(name, shape, dt))[(slice(None),) * len(shape)]

        def signal(name, per=1, credit=0):
            return Signal(ctx.enter_context(nc.semaphore(name)), per, credit)

        def signals(prefix, table):
            return {name: signal(prefix + name, *(spec if isinstance(spec, tuple) else (spec,))) for name, spec in table.items()}

        b.bank = [ctx.enter_context(nc.psum_tensor(f"bank{i}", [P, TB], F32)) for i in range(8)]
        b.x = sb(ctx, "x", [P, NT * D])
        b.cols = sb(ctx, "cols", [P, NCOL])
        b.rows = sb(ctx, "rows", [P, NROW])
        b.mod = sb(ctx, "mod", [P, 6, D])
        consts = sb(ctx, "consts", [P, 2, P])
        b.ident, b.heads = consts[:, 0, :], consts[:, 1, :]
        b.neg_half = sb(ctx, "neg_half", [P, NT])
        b.spare_g, b.spare_v, b.spare_s = (sb(ctx, "spare_" + e, [P, 4]) for e in "gvs")
        b.ones = sb(ctx, "ones", [P, P])
        b.silu_c = sb(ctx, "silu_c", [P, KD])
        b.silu_rep, b.gate_sign = [None, None], [None, None]
        b.alpha, b.decay, b.carry = (sb(ctx, n, [P, KD]) for n in ("alpha", "decay", "carry"))
        b.neg_beta_b = sb(ctx, "neg_beta_b", [P, 1])

        with ExitStack() as a:
            masks = sb(a, "masks", [P, 2 + LEVELS, P])
            b.upper, b.mask0, b.maskT = masks[:, 0, :], masks[:, 1, :], masks[:, 2:, :]
            b.a_hi, b.a_lo, b.a_raw = {}, {}, {}
            for name, kb, w, _ in A_MATS:
                b.a_hi[name] = sb(a, "a_hi_" + name, [P, kb, w], F32R)[:, :, :]
                b.a_lo[name] = sb(a, "a_lo_" + name, [P, kb, w], F32R)[:, :, :]
            b.hT_hi, b.hT_lo, b.oT_hi, b.oT_lo = (sb(a, "a_" + n, [P, KD, TB], F32R) for n in ("hT_hi", "hT_lo", "oT_hi", "oT_lo"))
            b.qT, b.av, b.ema, b.kT = (sb(a, "a_" + n, [P, KD, TB]) for n in ("qT", "av", "ema", "kT"))
            b.wT = b.av
            b.h1, b.h1_next, b.hn, b.k, b.v, b.xa = (sb(a, "a_" + n, [P, CT, D]) for n in ("h1", "h1_next", "hn", "k", "v", "xa"))
            b.a, b.aT, b.xx, b.xT, b.ax, b.pT, b.tT, b.x_tmp = (sb(a, "a_" + n, [P, TB]) for n in ("a", "aT", "xx", "xT", "ax", "pT", "tT", "x_tmp"))
            b.aTm = [sb(a, f"a_aTm{i}", [P, TB]) for i in range(2)]
            b.u = [sb(a, f"a_u{i}", [P, D]) for i in range(2)]
            b.m = [sb(a, f"a_m{i}", [P, KD, D])[:, :, :] for i in range(2)]
            b.stats = sb(a, "a_stats", [P, CT, 6])
            b.mv = sb(a, "a_mv", [P, CT, 2])
            b.ss1, b.ss2, b.kss, b.rs1, b.rs2, b.rs3, b.rk, b.beta, b.beta_e = (
                sb(a, "a_" + n, [P, CT]) for n in ("ss1", "ss2", "kss", "rs1", "rs2", "rs3", "rk", "beta", "beta_e"))
            with ExitStack() as raw:
                for name, kb, w, _ in A_MATS:
                    b.a_raw[name] = sb(raw, "a_raw_" + name, [P, kb, w])[:, :, :]
                b.silu_rep[0], b.gate_sign[0] = sb(raw, "silu_rep0", [P, KD, P]), sb(raw, "gate_sign0", [P, D])
                b.wmod = [sb(raw, "wmod0", [P, KD, 6 * D]), None]
            with ExitStack() as late:
                b.h2T_hi = sb(late, "a_h2T_hi", [P, KD, TB], F32R)
                b.h2T_lo = sb(late, "a_h2T_lo", [P, KD, TB], F32R)
                b.hn2 = sb(late, "a_hn2", [P, CT, D])
                b.sg = sb(late, "a_sg", [P, KH, TB])
                b.mm_hi = sb(late, "a_mm_hi", [P, KH, TB], F32R)
                b.mm_lo = sb(late, "a_mm_lo", [P, KH, TB], F32R)

        s_table = signals("", dict(load_small=80, load_x=16, set=1, alpha_e=1, h1_kept=1, stored=16, a_w=len(A_MATS), stats=CT, mv=CT, rs1=1, xn=CT, h1=CT, ss1=CT,
                               rs2=1, hn=CT, hT_ps=KD, hT_hi=KD, hT_lo=KD, k_ps=2, kss=CT, rk=1, k=CT, beta_ps=1, beta_e=1, v_ps=KD, q_ps=KD, av=KD,
                               ema=KD, qT=KD, vtok_ps=2, vtok=2, kT_ps=KD, kT=KD, g_ps=1, pt_ps=1, a=1, pT=1, aT_ps=1, aT=1, aTm0=1, aTm=LEVELS - 1,
                               x=LEVELS - 1, xT=LEVELS, ax_ps=LEVELS - 1, ax=LEVELS - 1, xax_ps=LEVELS - 2, xaxT_ps=LEVELS - 1, tT=1, wT_ps=KD, wT=KD,
                               u_ps=CT, u=CT, dm_ps=CT, m=(CT, 1), oT_ps=1, oT_hi=KD, oT_lo=KD, wo_ps=2, xa=2, ss2=CT, rs3=1, hn2=CT,
                               h2T_ps=KD, h2T_hi=KD, h2T_lo=KD, gate_ps=KH, up_ps=KH, sg=KH, mm=KH, mm_hi=KH, mm_lo=KH, down_ps=2, y=(2, 1),
                               gy=CT, x_done=CT))
        s = Names(**s_table)
        s.load_a = [signal("load_" + name, 16) for name, _, _, _ in A_MATS]
        s.silu_c = [signal(f"silu_c{i}") for i in range(2)]
        s.silu_rep = [signal(f"silu_rep{i}", KD) for i in range(2)]
        s.load_wmod = [signal(f"load_wmod{i}", 16) for i in range(2)]
        s.mod_ps = [signal(f"mod_ps{i}", 3) for i in range(2)]
        s.mod_raw = [signal(f"mod_raw{i}", 3) for i in range(2)]
        s.mod = [signal(f"mod{i}") for i in range(2)]
        W0, W1 = 3 * KD * D, KD * HID + KH * D
        after_a = ctx.enter_context(ExitStack())
        b.hT_hi_all = sb(after_a, "hT_hi_all", [P, KD, N], F32R)
        b.hT_lo_all = sb(after_a, "hT_lo_all", [P, KD, N], F32R)
        weight = sb(after_a, "weight", [P, EP * NT])
        b.weight, b.weight_flat = weight[:, :].rearrange("p (e t) -> p e t", e=EP), weight
        b.rank = sb(after_a, "rank", [P, EP])
        b.row_sign = sb(after_a, "row_sign", [P, 1])
        b.ones_r = sb(after_a, "ones_r", [P, P], F32R)
        b.bias_all = sb(after_a, "bias_all", [P, EP * D], F32R)
        b.router = {kind: sb(after_a, "router_" + kind, [P, KD, E1 if kind == "D" else E0]) for kind in ("B0", "B1", "D")}
        b.bias_cols = [sb(after_a, f"bias_cols{i}", [P, 2 * KD]) for i in range(2)]
        b.bias_cols1 = [sb(after_a, f"bias_cols1{i}", [P, KH]) for i in range(2)]

        def prep_buffers(scope, name, kinds):
            pair = lambda n, shape: [sb(scope, f"{name}_{n}{i}", shape) for i in range(2)]
            b.p_stats, b.p_mv, b.p_xn, b.p_h = pair("stats", [P, CT, 6]), pair("mv", [P, CT, 2]), pair("xn", [P, CT, D]), pair("h", [P, CT, D])
            b.p_rs, b.p_rs2, b.p_ss = pair("rs", [P, CT]), pair("rs2", [P, CT]), pair("ss", [P, CT])
            if kinds == "D":
                b.p_sq, b.p_gh = pair("sq", [P, CT, D]), pair("gh", [P, CT, D])
            if kinds != "C":
                b.logits = sb(scope, name + "_logits", [P, NT, EP])
                b.r_top, b.r_ga, b.r_gb = (sb(scope, f"{name}_r_{n}", [P, NT]) for n in ("top", "ga", "gb"))
                with ExitStack() as over:
                    b.p_hT = [sb(over, f"{name}_hT{i}", [P, KD, TB]) for i in range(2)]
                with ExitStack() as over:
                    b.r_z, b.r_t, b.r_one, b.r_two = (sb(over, f"{name}_r_{n}", [P, NT, EP]) for n in ("z", "t", "one", "two"))

        with ExitStack() as sc:
            b.y = sb(sc, "y", [P, NT * D])
            b.w_raw = sb(sc, "w_raw", [P, W0])
            b.w_hi_flat = [sb(sc, f"w_hi{i}", [P, W0], F32R) for i in range(2)]
            b.w_lo_flat = [sb(sc, f"w_lo{i}", [P, W0], F32R) for i in range(2)]
            b.w_hi, b.w_lo = ([w[:, :].rearrange("p (m n) -> p m n", n=D) for w in ws] for ws in (b.w_hi_flat, b.w_lo_flat))
            with ExitStack() as e:
                b.h_hi, b.h_lo = (sb(e, n, [P, KD, TB], F32R) for n in ("h_hi", "h_lo"))
                b.m_hi, b.m_lo = ([sb(e, f"{n}{i}", [P, KD, TB], F32R) for i in range(2)] for n in ("m_hi", "m_lo"))
                b.sgate = sb(e, "sgate", [P, KD, TB])
            with ExitStack() as e:
                b.norm_gate = sb(e, "norm_gate", [P, D])
                prep_buffers(e, "pb", "B")
            b.split, b.loaded = ([signal(f"split{i}", 1, i) for i in range(2)], [signal(f"loaded{i}", 16) for i in range(2)])
            bB = Names(b)
        with ExitStack() as sc:
            b.c_hi = {n: sb(sc, n + "_hi", [P, KD, D], F32R) for n in C_MATS}
            b.c_lo = {n: sb(sc, n + "_lo", [P, KD, D], F32R) for n in C_MATS}
            b.heads_r = sb(sc, "heads_r", [P, P], F32R)
            b.c_scale, b.c_bias = sb(sc, "c_scale", [P, KD]), sb(sc, "c_bias", [P, 2 * KD])
            with ExitStack() as e:
                b.c_raw = {n: sb(e, n + "_raw", [P, KD, D]) for n in C_MATS}
                b.silu_rep[1], b.gate_sign[1] = sb(e, "silu_rep1", [P, KD, P]), sb(e, "gate_sign1", [P, D])
                b.wmod[1] = sb(e, "wmod1", [P, KD, 6 * D])
                prep_buffers(e, "pc", "C")
            with ExitStack() as e:
                b.c_y, b.c_e, b.c_l, b.c_t = (sb(e, n, [P, 2 * KD, TB]) for n in ("c_y", "c_e", "c_l", "c_t"))
                b.c_qk, b.c_v, b.c_r, b.c_out = (sb(e, n, [P, KD, TB]) for n in ("c_qk", "c_v", "c_r", "c_out"))
                b.qk_hi, b.qk_lo, b.out_hi, b.out_lo = (sb(e, n, [P, KD, TB], F32R) for n in ("qk_hi", "qk_lo", "out_hi", "out_lo"))
                b.c_o = sb(e, "c_o", [P, CT, D])
            bC = Names(b)
        with ExitStack() as sc:
            b.w_raw = sb(sc, "v_raw", [P, W1])
            b.w_hi_flat = [sb(sc, f"v_hi{i}", [P, W1], F32R) for i in range(2)]
            b.w_lo_flat = [sb(sc, f"v_lo{i}", [P, W1], F32R) for i in range(2)]
            b.v1_hi, b.v1_lo = ([w[:, 0:KD * HID].rearrange("p (k n) -> p k n", k=KD) for w in ws] for ws in (b.w_hi_flat, b.w_lo_flat))
            b.v2_hi, b.v2_lo = ([w[:, KD * HID:W1].rearrange("p (k n) -> p k n", k=KH) for w in ws] for ws in (b.w_hi_flat, b.w_lo_flat))
            with ExitStack() as e:
                b.m_hi, b.m_lo = ([sb(e, f"d_{n}{i}", [P, KH, TB], F32R) for i in range(2)] for n in ("m_hi", "m_lo"))
            with ExitStack() as e:
                b.bias_raw, b.bias_tmp = sb(e, "bias_raw", [P, EP * D]), sb(e, "bias_tmp", [P, EP * D])
            with ExitStack() as e:
                prep_buffers(e, "pd", "D")
            b.split1 = b.split = [sig.again(R0 * U0 // 2) for sig in bB.split]
            b.loaded = [sig.again(R0 * U0 // 2) for sig in bB.loaded]
            bD = Names(b)

        common = signals("prep_", dict(rs=1, xn=CT, h=CT, var=1, hT_ps=KD, hT_hi=KD, hT_lo=(KD, 3), hT=KD, logit_ps=1,
                                              logits=(1, 2), stats=CT, mv=CT, y=1, ss=CT, rs2=1, var2=1, hn=CT, gh=CT, xh=CT))
        turns = {name: 0 for name in common}

        def prep_signals(*names):
            r = {}
            for name in names:
                r[name] = common[name].again(turns[name])
                turns[name] += NB
            return Names(**r)

        moved = ("hT_ps", "hT_hi", "hT_lo")
        routed = ("hT", "logit_ps", "logits")
        modulated = ("stats", "mv", "rs", "xn", "h", "var")
        rp = {"B0": prep_signals(*moved, *routed, *modulated, "y"), "B1": prep_signals(*moved, *routed, "rs", "h", "var", "y", "ss")}
        rx = prep_signals("ss", "var", "rs", "xn")
        rx.x = signal("close_x", CT)
        rp["C"] = prep_signals(*moved, *modulated)
        rp["D"] = prep_signals(*moved, *routed, *modulated, "ss", "hn", "rs2", "var2", "gh", "xh")
        for kind, r in rp.items():
            r.free = r.hT_lo if kind == "C" else r.logits
        experts = signals("expert_", dict(up_ps=KD, h_hi=KD, h_lo=KD, gate_ps=KD, sg=(KD, 1), m=(KD, 2), m_hi=KD,
                                            m_lo=(KD, 3), down_ps=(2, 17), acc=(CT, 1)))
        rb = Names(**experts)
        rd = Names(**{name: experts[name].again(R0 * U0 * NB, per) for name, per in dict(up_ps=KH, m=KH, m_hi=KH, m_lo=KH, down_ps=2, acc=CT).items()})
        rc = Names(**{name: s_table[old].again(NB, per) for name, (old, per) in dict(
                y=("ss1", 2 * KD), abs=("hT_hi", 2), exp=("beta_e", 2), ln=("kss", 2), qk_hi=("av", KD), out_hi=("qT", KD),
                v=("k", KD), o_taken=("y", 2), qk_lo=("hT_lo", KD), out_lo=("oT_lo", KD), soft=("m", 2), qk=("a", 1), out=("xn", KD), lmax=("pT", 2),
                num=("hn", KD), rden=("xa", KD), qkv_ps=("v_ps", 3 * KD), den_ps=("q_ps", KD), o_ps=("wo_ps", 2),
                tail0=("rs1", 2), tail=("rs2", 2), go=("gy", CT), x=("x_done", CT)).items()})
        s.load_b, s.load_bias1, s.head_scale, s.c_w = signal("load_b", 16 * 6), signal("load_bias1", 32), signal("head_scale"), signal("c_w", len(C_MATS))
        s.zeroed, s.zeroed1, s.b_ready, s.d_ready = (signal(n) for n in ("zeroed", "zeroed1", "b_ready", "d_ready"))
        s.load_c = [signal("load_" + n, 16) for n in C_MATS]
        s.gates = {k: signal("gates_" + k) for k in ("B0", "B1", "D")}
        s.gate_exp = {k: signal("gate_exp_" + k, 2) for k in ("B0", "B1", "D")}
        last = NB - 1
        vector_chain, gpsimd_chain = (ctx.enter_context(nc.semaphore(n)) for n in ("vector_chain", "gpsimd_chain"))
        def sync_b(sp):
            sp.wait_ge(s.x_done.sem, s.x_done.at(last))
            sp.dma_start(b.rank[:, :], d["rank"]).then_inc(s.load_b.sem, 16)
            for i, kind in enumerate(("B0", "B1")):
                sp.dma_start(b.router[kind][:, :, :], d["router"][i].rearrange("(k p) e -> p k e", p=P)).then_inc(s.load_b.sem, 16)
            sp.dma_start(b.router["D"][:, :, :], d["gate_w"].rearrange("(k p) e -> p k e", p=P)).then_inc(s.load_b.sem, 16)
            sp.wait_ge(s.zeroed.sem, s.zeroed.at(0))
            for row in range(2):
                sp.dma_start(bB.y[row:row + 1, 0:EP * D], d["b_down0"]).then_inc(s.load_b.sem, 16)
            for rnd in range(R0):
                weights_sync(sp, bB, d["units0"], bB.w_raw, rnd, U0 // 2, bB.split, bB.loaded)

        def sync_c(sp):
            sp.wait_ge(rx.x.sem, rx.x.at(last))
            sp.dma_start(bC.wmod[1][:, :, :], d["wmod1"].rearrange("(k p) n -> p k n", p=P)).then_inc(s.load_wmod[1].sem, 16)
            for name, sig in zip(C_MATS, s.load_c):
                sp.dma_start(bC.c_raw[name][:, :, :], d[name].rearrange("(k p) n -> p k n", p=P)).then_inc(sig.sem, 16)

        def sync_d(sp):
            sp.wait_ge(rc.x.sem, rc.x.at(last))
            sp.wait_ge(s.zeroed1.sem, s.zeroed1.at(0))
            for row in range(2):
                sp.dma_start(bD.bias_raw[row:row + 1, :], d["b_down1"]).then_inc(s.load_bias1.sem, 16)
            weights_sync(sp, bD, d["units1"], bD.w_raw, 0, E1 // 2, bD.split, bD.loaded)

        def prepare0(g, link, p, unit):
            for i, name in enumerate(("bup", "bg")):
                g.tensor_copy(bB.bias_cols[unit][:, i * KD:(i + 1) * KD], b.cols[:, bass.ds(COL[name] + (2 * p + unit) * KD, KD)])

        def prepare1(g, link, p, unit):
            g.tensor_copy(bD.bias_cols1[unit][:, :], b.cols[:, bass.ds(COL["b1"] + (2 * p + unit) * KH, KH)])
            for k in range(KD):
                w = bD.w_raw[:, k * HID:(k + 1) * HID]
                g.tensor_scalar(w, w, b.cols[:, COL["norm3"] + k:COL["norm3"] + k + 1], None, ALU.mult)
            w = bD.w_raw[:, KD * HID:W1].rearrange("p (k n) -> p k n", n=D)
            g.tensor_tensor(w, w, mid(b.mod[:, GB, :], KH), ALU.mult).then_inc(link.sem, 1)
            g.wait_ge(link.sem, link.next())
            absorb(g, b)

        prepare0.per, prepare1.per = 2, 4

        def gpsimd_b(g, link):
            g.wait_ge(s.x_done.sem, s.x_done.at(last))
            g.memset(bB.y[:, 0:EP * D], 0.0)
            g.memset(b.weight_flat[:, 0:NS * NT], 1.0).then_inc(s.zeroed.sem, 1)
            prep_gpsimd(g, bB, s, link, "B0", rp["B0"])
            weights_gpsimd(g, bB, link, 0, U0 // 2, prepare0, bB.w_raw, bB.w_hi_flat, bB.w_lo_flat, bB.split, bB.loaded, rb)
            prep_gpsimd(g, bB, s, link, "B1", rp["B1"])
            weights_gpsimd(g, bB, link, 1, U0 // 2, prepare0, bB.w_raw, bB.w_hi_flat, bB.w_lo_flat, bB.split, bB.loaded, rb)
            close_gpsimd(g, bB, rx)

        def scalar_b(act):
            act.wait_ge(s.b_ready.sem, s.b_ready.at(0))
            prep_scalar(act, bB, s, "B0", rp["B0"])
            routing_scalar(act, bB, s, "B0")
            b_experts_scalar(act, bB, s, rb, 0)
            act.wait_ge(rb.acc.sem, rb.acc.at(U0 * NB - 1))
            prep_scalar(act, bB, s, "B1", rp["B1"])
            routing_scalar(act, bB, s, "B1")
            b_experts_scalar(act, bB, s, rb, 1)
            act.wait_ge(rb.acc.sem, rb.acc.at(R0 * U0 * NB - 1))
            close_scalar(act, bB, rx)

        def vector_b(v, link):
            v.wait_ge(s.x_done.sem, s.x_done.at(last))
            v.wait_ge(s.load_b.sem, s.load_b.at(0))
            v.tensor_copy(b.ones_r[:, :], b.ones[:, :]).then_inc(link.sem, 1)
            v.wait_ge(link.sem, link.next())
            bias_table_vector(v, b, link, bB.y[:, 0:EP * D], bB.y[:, EP * D:2 * EP * D], None)
            for k in range(KD):
                v.tensor_scalar(b.router["D"][:, k, :], b.router["D"][:, k, :], b.cols[:, COL["norm3"] + k:COL["norm3"] + k + 1], None, ALU.mult).then_inc(link.sem, 1)
                v.wait_ge(link.sem, link.next())
            v.memset(b.spare_v[:, 0:1], 0.0).then_inc(s.b_ready.sem, 1)
            v.wait_ge(s.b_ready.sem, s.b_ready.at(0))
            for rnd, kind in enumerate(("B0", "B1")):
                prep_vector(v, bB, s, kind, rp[kind])
                v.wait_ge(rp[kind].logits.sem, rp[kind].logits.at(last))
                routing_vector(v, bB, s, link, kind)
                v.wait_ge(rp[kind].y.sem, rp[kind].y.at(last))
                b_experts_vector(v, bB, s, rb, rnd)
                v.wait_ge(rb.acc.sem, rb.acc.at((rnd + 1) * U0 * NB - 1))
            v.tensor_tensor(bB.norm_gate[:, :], b.rows[:, ROW["norm_w"] + D:ROW["norm_w"] + 2 * D], b.mod[:, GB, :], ALU.mult).then_inc(link.sem, 1)
            v.wait_ge(link.sem, link.next())
            close_vector(v, bB, rx)

        def tensor_b(pe):
            pe.wait_ge(s.b_ready.sem, s.b_ready.at(0))
            for rnd, kind in enumerate(("B0", "B1")):
                prep_tensor(pe, bB, s, kind, rp[kind])
                pe.wait_ge(rp[kind].logits.sem, rp[kind].logits.at(last))
                pe.wait_ge(rp[kind].hT_lo.sem, rp[kind].hT_lo.at(last))
                b_experts_tensor(pe, bB, s, rb, rnd)
                pe.wait_ge(rb.acc.sem, rb.acc.at((rnd + 1) * U0 * NB - 1))

        def gpsimd_c(g, link):
            g.wait_ge(s.mod[1].sem, s.mod[1].at(0))
            prep_gpsimd(g, bC, s, link, "C", rp["C"])
            c_gpsimd(g, bC, s, rc)

        def scalar_c(act):
            act.wait_ge(rx.x.sem, rx.x.at(last))
            modulation_scalar(act, b, s, 1)
            act.activation(b.c_scale[:, :], b.cols[:, COL["hbeta"]:COL["hbeta"] + KD], ACT.Exp, scale=-1.0).then_inc(s.head_scale.sem, 1)
            prep_scalar(act, bC, s, "C", rp["C"])
            act.wait_ge(s.c_w.sem, s.c_w.at(0))
            c_scalar(act, bC, s, rc)

        def vector_c(v, link):
            v.wait_ge(rx.x.sem, rx.x.at(last))
            modulation_vector(v, b, s, link, 1)
            softplus_scale_vector(v, bC, s, link)
            v.tensor_copy(bC.heads_r[:, :], b.heads).then_inc(link.sem, 1)
            v.wait_ge(link.sem, link.next())
            prep_vector(v, bC, s, "C", rp["C"])
            c_weights_vector(v, bC, s, link)
            c_vector(v, bC, s, rc)

        def tensor_c(pe):
            pe.wait_ge(rx.x.sem, rx.x.at(last))
            modulation_tensor(pe, bC, s, 1)
            pe.wait_ge(s.mod_raw[1].sem, s.mod_raw[1].at(0))
            prep_tensor(pe, bC, s, "C", rp["C"])
            pe.wait_ge(rp["C"].hT_lo.sem, rp["C"].hT_lo.at(last))
            pe.wait_ge(s.c_w.sem, s.c_w.at(0))
            c_tensor(pe, bC, s, rc)

        def gpsimd_d(g, link):
            g.wait_ge(rc.x.sem, rc.x.at(last))
            g.memset(bD.bias_raw[:, :], 0.0).then_inc(s.zeroed1.sem, 1)
            g.wait_ge(s.d_ready.sem, s.d_ready.at(0))
            prep_gpsimd(g, bD, s, link, "D", rp["D"])
            weights_gpsimd(g, bD, link, 0, E1 // 2, prepare1, bD.w_raw, bD.w_hi_flat, bD.w_lo_flat, bD.split, bD.loaded, rd)

        def scalar_d(act):
            act.wait_ge(s.d_ready.sem, s.d_ready.at(0))
            prep_scalar(act, bD, s, "D", rp["D"])
            routing_scalar(act, bD, s, "D")
            act.wait_ge(bD.split[0].sem, bD.split[0].at(0))
            d_experts_scalar(act, bD, s, rd)

        def vector_d(v, link):
            v.wait_ge(rc.x.sem, rc.x.at(last))
            v.wait_ge(s.load_bias1.sem, s.load_bias1.at(0))
            bias_table_vector(v, b, link, bD.bias_raw[:, :], bD.bias_tmp[:, :], b.mod[:, GB, :])
            v.memset(b.spare_v[:, 0:1], 0.0).then_inc(s.d_ready.sem, 1)
            prep_vector(v, bD, s, "D", rp["D"])
            v.wait_ge(rp["D"].logits.sem, rp["D"].logits.at(last))
            routing_vector(v, bD, s, link, "D")
            v.wait_ge(rp["D"].xh.sem, rp["D"].xh.at(last))
            d_experts_vector(v, bD, s, rd)

        def tensor_d(pe):
            pe.wait_ge(s.d_ready.sem, s.d_ready.at(0))
            prep_tensor(pe, bD, s, "D", rp["D"])
            pe.wait_ge(rp["D"].logits.sem, rp["D"].logits.at(last))
            pe.wait_ge(rp["D"].hT_lo.sem, rp["D"].hT_lo.at(last))
            d_experts_tensor(pe, bD, s, rd)

        block = ctx.enter_context(nc.Block())

        @block.sync
        def _(sp):
            sp.dma_start(b.cols[:, :], d["cols"]).then_inc(s.load_small.sem, 16)
            sp.dma_start(b.rows[:, :], d["rows"]).then_inc(s.load_small.sem, 16)
            sp.dma_start(consts[:, :, :], d["consts"][:, 0:2, :]).then_inc(s.load_small.sem, 16)
            sp.dma_start(masks[:, :, :], d["consts"][:, 2:, :]).then_inc(s.load_small.sem, 16)
            sp.dma_start(b.ones[:, :], d["ones"]).then_inc(s.load_small.sem, 16)
            sp.dma_start(b.x[:, :].rearrange("p (t n) -> p t n", t=NT), d["x"].rearrange("(t p) n -> p t n", p=P)).then_inc(s.load_x.sem, 16)
            sp.dma_start(b.wmod[0][:, :, :], d["wmod0"].rearrange("(k p) n -> p k n", p=P)).then_inc(s.load_wmod[0].sem, 16)
            for (name, _, _, _), sig in zip(A_MATS, s.load_a):
                sp.dma_start(b.a_raw[name], d[name].rearrange("(k p) n -> p k n", p=P)).then_inc(sig.sem, 16)
            sync_b(sp)
            sync_c(sp)
            sync_d(sp)
            sp.wait_ge(rd.acc.sem, rd.acc.at(E1 * NB - 1))
            sp.dma_start(out.rearrange("(t p) n -> p t n", p=P), b.x[:, :].rearrange("p (t n) -> p t n", t=NT)).then_inc(s.stored.sem, 16)
            sp.wait_ge(s.stored.sem, s.stored.at(0))

        @block.gpsimd
        def _(g):
            g.sem_inc(bB.split[1].sem, bB.split[1].credit)
            link = Chain(gpsimd_chain)
            g.memset(b.neg_half[:, :], -0.5)
            g.memset(b.m[0], 0.0)
            g.memset(b.carry[:, :], 0.0).then_inc(s.set.sem, 1)
            g.wait_ge(s.set.sem, s.set.at(0))
            g.wait_ge(s.mod[0].sem, s.mod[0].at(0))
            a_gpsimd(g, b, s, link)
            gpsimd_b(g, link)
            gpsimd_c(g, link)
            gpsimd_d(g, link)

        @block.scalar
        def _(act):
            act.sem_inc(rb.sg.sem, rb.sg.credit)
            modulation_scalar(act, b, s, 0)
            act.activation(b.alpha[:, :], b.cols[:, COL["alpha"]:COL["alpha"] + KD], ACT.Exp, scale=-1.0)
            act.activation(b.neg_beta_b[:, :], b.rows[:, ROW["beta_b"]:ROW["beta_b"] + 1], ACT.Copy, scale=-1.0).then_inc(s.alpha_e.sem, 1)
            act.wait_ge(s.alpha_e.sem, s.alpha_e.at(0))
            act.wait_ge(s.a_w.sem, s.a_w.at(0))
            a_scalar(act, b, s)
            scalar_b(act)
            scalar_c(act)
            scalar_d(act)

        @block.vector
        def _(v):
            v.sem_inc(s.m.sem, s.m.credit)
            v.sem_inc(s.y.sem, s.y.credit)
            v.sem_inc(rp["B0"].hT_lo.sem, rp["B0"].hT_lo.credit)
            v.sem_inc(rp["B0"].logits.sem, rp["B0"].logits.credit)
            v.sem_inc(rb.m.sem, rb.m.credit)
            v.sem_inc(rb.m_lo.sem, rb.m_lo.credit)
            v.sem_inc(rb.acc.sem, rb.acc.credit)
            link = Chain(vector_chain)
            modulation_vector(v, b, s, link, 0)
            v.wait_ge(s.alpha_e.sem, s.alpha_e.at(0))
            v.tensor_scalar(b.alpha[:, :], b.alpha[:, :], 1.0, None, ALU.add).then_inc(link.sem, 1)
            v.wait_ge(link.sem, link.next())
            v.reciprocal(b.alpha[:, :], b.alpha[:, :]).then_inc(link.sem, 1)
            v.wait_ge(link.sem, link.next())
            v.tensor_scalar(b.decay[:, :], b.alpha[:, :], -1.0, 1.0, ALU.mult, ALU.add).then_inc(link.sem, 1)
            v.wait_ge(link.sem, link.next())
            a_weights_vector(v, b, s, link)
            v.wait_ge(s.load_x.sem, s.load_x.at(0))
            v.wait_ge(s.set.sem, s.set.at(0))
            a_vector(v, b, s, link)
            vector_b(v, link)
            vector_c(v, link)
            vector_d(v, link)

        @block.tensor
        def _(pe):
            pe.sem_inc(rb.down_ps.sem, rb.down_ps.credit)
            modulation_tensor(pe, b, s, 0)
            pe.wait_ge(s.mod_raw[0].sem, s.mod_raw[0].at(0))
            pe.wait_ge(s.set.sem, s.set.at(0))
            a_tensor(pe, b, s)
            tensor_b(pe)
            tensor_c(pe)
            tensor_d(pe)


def columns(a):
    import numpy as np

    return np.ascontiguousarray(np.asarray(a).reshape(-1, P).T)


def constants():
    import numpy as np

    i = np.arange(P)
    row, col = i[:, None], i[None, :]
    level = [((row // (2 << l)) == (col // (2 << l))) & (row % (2 << l) >= (1 << l)) & (col % (2 << l) < (1 << l)) for l in range(LEVELS)]
    parts = [row == col, row // DH == col // DH, row <= col, level[0]] + [m.T for m in level]
    return np.ascontiguousarray(np.stack([m.astype(np.float32) for m in parts], axis=1))


def laid_out(i):
    import numpy as np

    i = {k: np.asarray(v) for k, v in i.items()}
    g = lambda name: i["L0_attn_" + name]
    f = lambda name: i["L0_ffn_" + name]
    w = {}
    w["x"] = g("x").reshape(N, D)
    w["cols"] = np.concatenate([columns(v) for v in (
        g("norm1_w"), g("norm2_w"), g("alpha_logit"), i["L1_ffn_norm_weight"], i["L1_attn_bq"], i["L1_attn_bk"], i["L1_attn_bv"],
        np.repeat(i["L1_attn_beta"], DH), i["L0_c"], i["L1_c"],
        np.concatenate([f("share_bup").reshape(NS, D), f("exp_bup")]), np.concatenate([np.stack([f("share_bg")] * NS), f("exp_bg")]),
        i["L1_ffn_b1"])], axis=1)
    rows = np.concatenate([v.reshape(-1) for v in (f("norm_w"), f("router_b"), f("gate_bias"), i["L1_attn_bo"], g("beta_b"))])
    w["rows"] = np.broadcast_to(rows, (P, NROW))
    w["consts"] = constants()
    w["ones"] = np.ones((P, P), np.float32)
    w["wmod0"], w["wmod1"] = i["L0_wmod"], i["L1_wmod"]
    w["wq"], w["wk"], w["wv"], w["wo"] = g("Wq"), g("Wk"), g("Wv"), g("Wo")
    w["c_wq"], w["c_wk"], w["c_wv"], w["c_wo"] = (i["L1_attn_W" + n].T for n in "qkvo")
    w["router"], w["gate_w"] = f("router_W"), i["L1_ffn_gate_w"].T
    w["rank"] = np.broadcast_to(np.arange(EP, 0, -1, dtype=np.float32), (P, EP))
    on_partitions = lambda m: m.reshape(m.shape[0], -1, P, m.shape[2]).transpose(0, 2, 1, 3).reshape(m.shape[0], P, -1)
    w["units0"] = np.concatenate([on_partitions(m) for m in (
        np.concatenate([f("share_Wup").reshape(D, NS, D).transpose(1, 0, 2), f("exp_Wup")]),
        np.concatenate([np.stack([f("share_Wg")] * NS), f("exp_Wg")]),
        np.concatenate([np.stack([f("share_Wdown")] * NS), f("exp_Wdown")]))], axis=2)
    w["units1"] = np.concatenate([on_partitions(i["L1_ffn_w1"].transpose(0, 2, 1)), on_partitions(i["L1_ffn_w2"].transpose(0, 2, 1))], axis=2)
    w["b_down0"] = np.concatenate([np.stack([f("share_bdown")] * NS), f("exp_bdown")]).reshape(1, -1)
    w["b_down1"] = i["L1_ffn_b2"].reshape(1, -1)
    w["beta_w"] = np.concatenate([g("beta_w")] * 2, axis=1)
    w["w_gate"], w["w_up"], w["w_down"] = g("w_gate"), g("w_up"), g("w_down")
    return {k: np.ascontiguousarray(v) for k, v in w.items()}


def kernel(**inputs):
    import numpy as np
    import concourse.bacc as bacc
    from concourse.bass_utils import run_bass_kernel_spmd

    nc = bacc.Bacc("TRN2", target_bir_lowering=False, num_devices=1)
    arrays = {"in_" + k: v for k, v in laid_out(inputs).items()}
    d = {k[3:]: nc.dram_tensor(k, v.shape, mybir.dt.from_np(v.dtype), kind="ExternalInput").ap() for k, v in arrays.items()}
    out = nc.dram_tensor("out_x", (N, D), F32, kind="ExternalOutput").ap()
    program(nc, d, out)
    r = run_bass_kernel_spmd(nc, [arrays], core_ids=[0])
    return r.results[0]["out_x"].reshape(1, N, D)
```

```python
import concourse.bass as bass
from concourse import mybir
from contextlib import ExitStack

F32, F32R, I32 = mybir.dt.float32, mybir.dt.float32r, mybir.dt.int32
ALU, ACT = mybir.AluOpType, mybir.ActivationFunctionType
AX = mybir.AxisListType

P = 128
N, D = 4096, 256
KD = D // P
NT = N // P
TB = 512
NB = N // TB
CT = TB // P
HID = 2 * D
KH = HID // P
E0, NS, R0 = 6, 2, 2
U0 = NS + E0
E1 = 8
EP = 8
HEADS = 16
DH = D // HEADS
LEVELS = 7
LN_EPS, RMS_EPS = 1e-5, 1e-6
BIG = 3.0e38

COL = {}
_n = 0
for _name, _w in (("norm1", KD), ("norm2", KD), ("alpha", KD), ("norm3", KD), ("bq", KD), ("bk", KD), ("bv", KD),
                  ("hbeta", KD), ("c0", KD), ("c1", KD), ("bup", U0 * KD), ("bg", U0 * KD), ("b1", E1 * KH)):
    COL[_name] = _n
    _n += _w
NCOL = _n
ROW = {}
_n = 0
for _name, _w in (("norm_w", R0 * D), ("rb", R0 * E0), ("gb", R0 * E0), ("beta_b", 1)):
    ROW[_name] = _n
    _n += _w
NROW = _n


class Names(dict):

    def __getattr__(self, name):
        return self[name]

    def __setattr__(self, name, value):
        self[name] = value


class Signal:

    def __init__(self, sem, per=1, credit=0):
        self.sem, self.per, self.credit = sem, per, credit

    def at(self, t, k=None):
        return t * self.per + (self.credit + (self.per if k is None else k))

    def again(self, turns, per=None):
        return Signal(self.sem, self.per if per is None else per, self.credit + turns * self.per)


class Chain:

    def __init__(self, sem):
        self.sem, self.base, self.n = sem, 0, 0

    def loop(self, t, per):
        self.before, self.base, self.n, self.per = self.base + self.n, self.base + self.n + t * per, 0, per

    def end(self, turns):
        assert self.n == self.per, (self.n, self.per)
        self.base, self.n = self.before + turns * self.per, 0

    def next(self):
        self.n += 1
        return self.base + self.n


def rsqrt(g, link, out, x, neg_half, scale, eps, floor=None):
    if floor is None:
        g.tensor_scalar(out, x, scale, eps, ALU.mult, ALU.add).then_inc(link.sem, 1)
        g.wait_ge(link.sem, link.next())
    else:
        g.tensor_scalar(out, x, scale, floor, ALU.mult, ALU.max).then_inc(link.sem, 1)
        g.wait_ge(link.sem, link.next())
    return g.tensor_tensor(out, out, neg_half, ALU.pow)


def three(pe, out, lhs, rhs, first=True, last=True):
    n, of = 0, 3 * len(lhs)
    for (lh, ll), (rh, rl) in zip(lhs, rhs):
        for a, b in ((lh, rh), (lh, rl), (ll, rh)):
            ins = pe.matmul(out, a, b, start=first and n == 0, stop=last and n == of - 1)
            n += 1
    return ins


def absorb(eng, b, i=0):
    if eng is b.scalar:
        eng.activation(b.spare_s[:, i:i + 1], b.neg_half[:, 0:1], ACT.Copy)
    elif eng is b.gpsimd:
        eng.tensor_tensor(b.spare_g[:, i:i + 1], b.neg_half[:, 0:1], b.neg_half[:, 0:1], ALU.mult)
    else:
        eng.memset(b.spare_v[:, i:i + 1], 0.0)


def flat(ap):
    return ap.rearrange("p c n -> p (c n)")


def mid(vec, n):
    return vec.unsqueeze(1).broadcast_to([P, n, vec.shape[1]])


def spread(cols, w):
    return cols.unsqueeze(2).broadcast_to([P, cols.shape[1], w])


SA, CA, GA, SB, CB, GB = range(6)


def modulation_scalar(act, b, s, layer):
    c0 = COL[f"c{layer}"]
    if layer == 0:
        act.wait_ge(s.load_small.sem, s.load_small.at(0))
    act.activation(b.silu_c[layer][:, :], b.cols[:, c0:c0 + KD], ACT.Silu).then_inc(s.silu_c[layer].sem, 1)
    act.wait_ge(s.silu_c[layer].sem, s.silu_c[layer].at(0))
    for k in range(KD):
        act.activation(b.silu_rep[layer][:, k, :], b.ones[:, :], ACT.Copy, scale=b.silu_c[layer][:, k:k + 1]).then_inc(s.silu_rep[layer].sem, 1)
    for j in range(3):
        act.wait_ge(s.mod_ps[layer].sem, s.mod_ps[layer].at(0, j + 1))
        act.activation(b.mods[layer][:, 2 * j:2 * j + 2, :], b.bank[j][:, :], ACT.Copy).then_inc(s.mod_raw[layer].sem, 1)


def modulation_tensor(pe, b, s, layer):
    pe.wait_ge(s.silu_rep[layer].sem, s.silu_rep[layer].at(0))
    pe.wait_ge(s.load_wmod[layer].sem, s.load_wmod[layer].at(0))
    for j in range(3):
        for k in range(KD):
            ins = pe.matmul(b.bank[j][:, :], b.silu_rep[layer][:, k, :], b.wmod[layer][:, k, j * TB:(j + 1) * TB], start=k == 0, stop=k == KD - 1)
        ins.then_inc(s.mod_ps[layer].sem, 1)


def modulation_vector(v, b, s, link, layer):
    v.wait_ge(s.mod_raw[layer].sem, s.mod_raw[layer].at(0))
    for j in (CA, CB):
        v.tensor_scalar(b.mods[layer][:, j, :], b.mods[layer][:, j, :], 1.0, None, ALU.add).then_inc(link.sem, 1)
        v.wait_ge(link.sem, link.next())
    for j in (GA, GB):
        v.tensor_scalar(b.gate_sign[layer][:, :], b.mods[layer][:, j, :], 0.0, 2.0, ALU.is_ge, ALU.mult).then_inc(link.sem, 1)
        v.wait_ge(link.sem, link.next())
        v.scalar_tensor_tensor(b.mods[layer][:, j, :], b.mods[layer][:, j, :], -1.0, b.mods[layer][:, j, :], ALU.mult, ALU.max).then_inc(link.sem, 1)
        v.wait_ge(link.sem, link.next())
        v.tensor_scalar(b.mods[layer][:, j, :], b.mods[layer][:, j, :], 0.25, None, ALU.max).then_inc(link.sem, 1)
        v.wait_ge(link.sem, link.next())
        last = v.scalar_tensor_tensor(b.mods[layer][:, j, :], b.gate_sign[layer][:, :], -1.0, b.mods[layer][:, j, :], ALU.add, ALU.mult)
        if j == GA:
            last.then_inc(link.sem, 1)
            v.wait_ge(link.sem, link.next())
    last.then_inc(s.mod[layer].sem, 1)
    v.wait_ge(s.mod[layer].sem, s.mod[layer].at(0))


A_MATS = (("wk", KD, D, "norm1"), ("beta_w", KD, 2, "norm1"), ("wv", KD, D, "norm1"), ("wq", KD, D, "norm1"), ("wo", KD, D, None),
          ("w_gate", KD, HID, "norm2"), ("w_up", KD, HID, "norm2"), ("w_down", KH, D, None))


def a_weights_scalar(act, b, s):
    for i, (name, kb, w, norm) in enumerate(A_MATS):
        act.wait_ge(s.load_a[i].sem, s.load_a[i].at(0))
        for k in range(kb):
            if norm:
                act.activation(b.a_raw[name][:, k, :], b.a_raw[name][:, k, :], ACT.Copy, scale=b.cols[:, COL[norm] + k:COL[norm] + k + 1]).then_inc(s.a_scaled.sem, 1)
        if norm:
            act.wait_ge(s.a_scaled.sem, scaled_before(i + 1))
        act.activation(b.a_hi[name], b.a_raw[name], ACT.Copy).then_inc(s.a_hi_done.sem, 1)


def scaled_before(i):
    return sum(kb for _, kb, _, norm in A_MATS[:i] if norm)


def a_weights_vector(v, b, s, link):
    for i, (name, kb, w, norm) in enumerate(A_MATS):
        v.wait_ge(s.a_hi_done.sem, s.a_hi_done.at(i))
        raw, hi, lo = b.a_raw[name], b.a_hi[name], b.a_lo[name]
        v.tensor_tensor(lo, raw, hi.bitcast(F32), ALU.subtract).then_inc(s.a_w.sem, 1)


GATE_BANKS, UP_BANKS = (4, 5, 0, 1), (2, 3, 6, 7)


def a_tensor(pe, b, s):
    B = b.bank
    h = lambda k, c0=0, w=TB: (b.hT_hi[:, k, c0:c0 + w], b.hT_lo[:, k, c0:c0 + w])
    W = lambda name, k, c0=0, w=D: (b.a_hi[name][:, k, c0:c0 + w], b.a_lo[name][:, k, c0:c0 + w])
    chunk = lambda c: slice(c * P, (c + 1) * P)

    def tokens(t, c):
        if c == 0:
            pe.wait_ge(s.hn.sem, s.hn.at(t))
        k, c0 = divmod(2 * c, CT)
        for n in (c0, c0 + 1):
            ins = pe.transpose(B[2 + k][:, chunk(n)], b.hn[:, n, k * P:(k + 1) * P], b.ident)
        if c % 2:
            ins.then_inc(s.hT_ps.sem, 1)

    def keys(t):
        pe.wait_ge(s.hT_hi.sem, s.hT_hi.at(t))
        pe.wait_ge(s.hT_lo.sem, s.hT_lo.at(t))
        for c in range(CT):
            ins = three(pe, B[6 + c // 2][:, (c % 2) * D:(c % 2 + 1) * D], [h(k, c * P, P) for k in range(KD)], [W("wk", k) for k in range(KD)])
            if c % 2:
                ins.then_inc(s.k_ps.sem, 1)

    def values(t):
        for o in range(KD):
            three(pe, B[o][:, :], [W("wv", k, o * P, P) for k in range(KD)], [h(k) for k in range(KD)]).then_inc(s.v_ps.sem, 1)

    def queries(t):
        for o in range(KD):
            three(pe, B[4 + o][:, :], [W("wq", k, o * P, P) for k in range(KD)], [h(k) for k in range(KD)]).then_inc(s.q_ps.sem, 1)
        for c in range(CT):
            ins = three(pe, B[0][:, 2 * c:2 * c + 2], [h(k, c * P, P) for k in range(KD)], [W("beta_w", k, 0, 2) for k in range(KD)])
        ins.then_inc(s.beta_ps.sem, 1)

    def turned(t):
        pe.wait_ge(s.k.sem, s.k.at(t))
        for k in range(KD):
            for c in range(CT):
                ins = pe.transpose(B[6 + k][:, chunk(c)], b.k[:, c, k * P:(k + 1) * P], b.ident)
            ins.then_inc(s.kT_ps.sem, 1)
        pe.wait_ge(s.ema.sem, s.ema.at(t))
        pe.wait_ge(s.qT.sem, s.qT.at(t))
        for c in range(CT):
            for o in range(KD):
                ins = pe.transpose(B[4 + c // 2][:, (c % 2) * D + o * P:(c % 2) * D + (o + 1) * P], b.ema[:, o, chunk(c)], b.ident)
            if c % 2:
                ins.then_inc(s.vtok_ps.sem, 1)

    def block(t, more):
        pe.wait_ge(s.kT.sem, s.kT.at(t))
        for c in range(CT):
            for k in range(KD):
                ins = pe.matmul(B[6][:, chunk(c)], b.kT[:, k, chunk(c)], b.kT[:, k, chunk(c)], start=k == 0, stop=k == KD - 1)
        ins.then_inc(s.g_ps.sem, 1)
        for c in range(CT):
            for k in range(KD):
                ins = pe.matmul(B[7][:, chunk(c)], b.kT[:, k, chunk(c)], b.qT[:, k, chunk(c)], start=k == 0, stop=k == KD - 1)
        ins.then_inc(s.pt_ps.sem, 1)
        pe.wait_ge(s.a.sem, s.a.at(t))
        for c in range(CT):
            ins = pe.transpose(B[0][:, chunk(c)], b.a[:, chunk(c)], b.ident)
        ins.then_inc(s.aT_ps.sem, 1)
        pe.wait_ge(s.y.sem, s.y.at(t - 1))
        for l in range(1, LEVELS):
            pe.wait_ge(s.aTm.sem, s.aTm.at(t, l))
            pe.wait_ge(s.x.sem, s.x.at(t, l))
            for c in range(CT):
                ins = pe.matmul(B[1][:, chunk(c)], b.aTm[l % 2][:, chunk(c)], b.xx[:, chunk(c)], start=True, stop=True)
            ins.then_inc(s.ax_ps.sem, 1)
            pe.wait_ge(s.ax.sem, s.ax.at(t, l))
            pe.wait_ge(s.xT.sem, s.xT.at(t, l))
            if l < LEVELS - 1:
                for c in range(CT):
                    ins = pe.matmul(B[2][:, chunk(c)], b.xT[:, chunk(c)], b.ax[:, chunk(c)], start=True, stop=True)
                ins.then_inc(s.xax_ps.sem, 1)
            for c in range(CT):
                ins = pe.matmul(B[3][:, chunk(c)], b.ax[:, chunk(c)], b.xT[:, chunk(c)], start=True, stop=True)
            ins.then_inc(s.xaxT_ps.sem, 1)
        pe.wait_ge(s.vtok.sem, s.vtok.at(t))
        pe.wait_ge(s.tT.sem, s.tT.at(t))
        for k in range(KD):
            for c in range(CT):
                ins = pe.matmul(B[4 + k][:, chunk(c)], b.k[:, c, k * P:(k + 1) * P], b.tT[:, chunk(c)], start=True, stop=True)
            ins.then_inc(s.wT_ps.sem, 1)
        pe.wait_ge(s.pT.sem, s.pT.at(t))
        pe.wait_ge(s.wT.sem, s.wT.at(t))
        for c in range(CT):
            state = b.m[c % 2]
            pe.matmul(B[6][:, 0:D], b.tT[:, chunk(c)], b.v[:, c, :], start=True, stop=False)
            pe.wait_ge(s.m.sem, s.m.at(t, c))
            for k in range(KD):
                ins = pe.matmul(B[6][:, 0:D], b.wT[:, k, chunk(c)], state[:, k, :], start=False, stop=k == KD - 1)
            ins.then_inc(s.u_ps.sem, 1)
            if more:
                tokens(t + 1, c)
            pe.wait_ge(s.u.sem, s.u.at(t, c + 1))
            for k in range(KD):
                ins = pe.matmul(B[7][:, k * D:(k + 1) * D], b.k[:, c, k * P:(k + 1) * P], b.u[c % 2][:, :], start=True, stop=True)
            ins.then_inc(s.dm_ps.sem, 1)
            for o in range(KD):
                for k in range(KD):
                    pe.matmul(B[o][:, chunk(c)], state[:, k, o * P:(o + 1) * P], b.qT[:, k, chunk(c)], start=k == 0, stop=False)
                ins = pe.matmul(B[o][:, chunk(c)], b.u[c % 2][:, o * P:(o + 1) * P], b.pT[:, chunk(c)], start=False, stop=True)
        ins.then_inc(s.oT_ps.sem, 1)
        pe.wait_ge(s.m.sem, s.m.at(t, CT))
        if more:
            keys(t + 1)
        pe.wait_ge(s.oT_hi.sem, s.oT_hi.at(t))
        pe.wait_ge(s.oT_lo.sem, s.oT_lo.at(t))
        for c in range(CT):
            ins = three(pe, B[4 + c // 2][:, (c % 2) * D:(c % 2 + 1) * D], [(b.oT_hi[:, k, chunk(c)], b.oT_lo[:, k, chunk(c)]) for k in range(KD)],
                        [W("wo", k) for k in range(KD)])
            if c % 2:
                ins.then_inc(s.wo_ps.sem, 1)
        if more:
            values(t + 1)
        pe.wait_ge(s.hn2.sem, s.hn2.at(t))
        for k in range(KD):
            for c in range(CT):
                ins = pe.transpose(B[2 + k][:, chunk(c)], b.hn2[:, c, k * P:(k + 1) * P], b.ident)
            ins.then_inc(s.h2T_ps.sem, 1)
        pe.wait_ge(s.h2T_hi.sem, s.h2T_hi.at(t))
        pe.wait_ge(s.h2T_lo.sem, s.h2T_lo.at(t))
        h2 = [(b.h2T_hi[:, k, :], b.h2T_lo[:, k, :]) for k in range(KD)]
        for name, o in (("w_gate", 0), ("w_gate", 1), ("w_up", 0), ("w_up", 1), ("w_gate", 2), ("w_gate", 3), ("w_up", 2), ("w_up", 3)):
            gate = name == "w_gate"
            if more and gate and o == 2:
                pe.wait_ge(s.av.sem, s.av.at(t + 1))
            if more and not gate and o == 2:
                pe.wait_ge(s.k.sem, s.k.at(t + 1))
            three(pe, B[(GATE_BANKS if gate else UP_BANKS)[o]][:, :], [W(name, k, o * P, P) for k in range(KD)], h2).then_inc((s.gate_ps if gate else s.up_ps).sem, 1)
        if more:
            pe.wait_ge(s.sg.sem, s.sg.at(t, 3))
            queries(t + 1)
        pe.wait_ge(s.mm_hi.sem, s.mm_hi.at(t))
        pe.wait_ge(s.mm_lo.sem, s.mm_lo.at(t))
        for c in range(CT):
            ins = three(pe, B[2 + c // 2][:, (c % 2) * D:(c % 2 + 1) * D], [(b.mm_hi[:, k, chunk(c)], b.mm_lo[:, k, chunk(c)]) for k in range(KH)],
                        [W("w_down", k) for k in range(KH)])
            if c % 2:
                ins.then_inc(s.down_ps.sem, 1)
        if more:
            turned(t + 1)

    for c in range(CT):
        tokens(0, c)
    pe.wait_ge(s.a_w.sem, s.a_w.at(0))
    keys(0)
    values(0)
    pe.wait_ge(s.av.sem, s.av.at(0))
    queries(0)
    turned(0)
    with pe.Fori(0, NB - 1) as t:
        block(t, True)
    block(NB - 1, False)


def a_scalar(act, b, s):
    B = b.bank
    act.wait_ge(s.load_small.sem, s.load_small.at(0))

    def square(t, c, junk):
        act.wait_ge(s.h1.sem, s.h1.at(t, c + 1))
        act.activation(junk[:, c, 0:D], b.h1_next[:, c, :], ACT.Square, accum_out=b.ss1[:, c:c + 1]).then_inc(s.ss1.sem, 1)

    def tokens(t, k):
        act.wait_ge(s.hT_ps.sem, s.hT_ps.at(t, k + 1))
        act.activation(b.hT_hi[:, k, :], B[2 + k][:, :], ACT.Copy).then_inc(s.hT_hi.sem, 1)

    def keys(t, junk):
        for c in range(CT):
            act.wait_ge(s.k_ps.sem, s.k_ps.at(t, c // 2 + 1))
            act.activation(junk[:, c, 0:D], B[6 + c // 2][:, (c % 2) * D:(c % 2 + 1) * D], ACT.Square, accum_out=b.kss[:, c:c + 1]).then_inc(s.kss.sem, 1)

    def values(t):
        for o in range(KD):
            act.wait_ge(s.v_ps.sem, s.v_ps.at(t, o + 1))
            act.activation(b.av[:, o, :], B[o][:, :], ACT.Copy, scale=b.alpha[:, o:o + 1]).then_inc(s.av.sem, 1)

    def queries(t):
        for o in range(KD):
            act.wait_ge(s.q_ps.sem, s.q_ps.at(t, o + 1))
            act.activation(b.qT[:, o, :], B[4 + o][:, :], ACT.Copy).then_inc(s.qT.sem, 1)
        act.wait_ge(s.beta_ps.sem, s.beta_ps.at(t))
        act.activation(b.beta_e[:, :], B[0][:, 0:2 * CT:2], ACT.Exp, bias=b.neg_beta_b[:, :], scale=-1.0).then_inc(s.beta_e.sem, 1)

    def turned(t):
        for k in range(KD):
            act.wait_ge(s.kT_ps.sem, s.kT_ps.at(t, k + 1))
            act.activation(b.kT[:, k, :], B[6 + k][:, :], ACT.Copy).then_inc(s.kT.sem, 1)
        for i in range(2):
            act.wait_ge(s.vtok_ps.sem, s.vtok_ps.at(t, i + 1))
            act.activation(b.v[:, 2 * i:2 * i + 2, :], B[4 + i][:, :], ACT.Copy).then_inc(s.vtok.sem, 1)
        act.activation(flat(b.h1[:, :, :]), flat(b.h1_next[:, :, :]), ACT.Copy).then_inc(s.h1_kept.sem, 1)

    def silu(t, o):
        act.wait_ge(s.gate_ps.sem, s.gate_ps.at(t, o + 1))
        act.activation(b.sg[:, o, :], B[GATE_BANKS[o]][:, :], ACT.Silu).then_inc(s.sg.sem, 1)

    def hidden(t, o):
        act.wait_ge(s.mm.sem, s.mm.at(t, o + 1))
        act.activation(b.mm_hi[:, o, :], B[UP_BANKS[o]][:, :], ACT.Copy).then_inc(s.mm_hi.sem, 1)

    def block(t, more):
        act.wait_ge(s.aT_ps.sem, s.aT_ps.at(t))
        act.activation(b.aT[:, :], B[0][:, :], ACT.Copy).then_inc(s.aT.sem, 1)
        for l in range(1, LEVELS):
            act.wait_ge(s.ax_ps.sem, s.ax_ps.at(t, l))
            act.activation(b.ax[:, :], B[1][:, :], ACT.Copy).then_inc(s.ax.sem, 1)
            if more and l in (2, 3):
                for c in (2 * l - 4, 2 * l - 3):
                    square(t + 1, c, b.sg)
        for k in range(KD):
            act.wait_ge(s.wT_ps.sem, s.wT_ps.at(t, k + 1))
            act.activation(b.wT[:, k, :], B[4 + k][:, :], ACT.Copy, scale=-1.0).then_inc(s.wT.sem, 1)
        for c in range(CT):
            act.wait_ge(s.u_ps.sem, s.u_ps.at(t, c + 1))
            act.activation(b.u[c % 2][:, :], B[6][:, 0:D], ACT.Copy).then_inc(s.u.sem, 1)
            if more and c % 2:
                tokens(t + 1, c // 2)
        act.wait_ge(s.oT_ps.sem, s.oT_ps.at(t))
        for o in range(KD):
            act.activation(b.oT_hi[:, o, :], B[o][:, :], ACT.Copy).then_inc(s.oT_hi.sem, 1)
        if more:
            keys(t + 1, b.sg)
        for c in range(CT):
            act.wait_ge(s.xa.sem, s.xa.at(t, c // 2 + 1))
            act.activation(b.v[:, c, :], b.xa[:, c, :], ACT.Square, accum_out=b.ss2[:, c:c + 1]).then_inc(s.ss2.sem, 1)
        if more:
            values(t + 1)
        for k in range(KD):
            act.wait_ge(s.h2T_ps.sem, s.h2T_ps.at(t, k + 1))
            act.activation(b.h2T_hi[:, k, :], B[2 + k][:, :], ACT.Copy).then_inc(s.h2T_hi.sem, 1)
        silu(t, 0)
        silu(t, 1)
        hidden(t, 0)
        hidden(t, 1)
        silu(t, 2)
        silu(t, 3)
        hidden(t, 2)
        hidden(t, 3)
        if more:
            queries(t + 1)
            turned(t + 1)

    for c in range(CT):
        square(0, c, b.h1)
    a_weights_scalar(act, b, s)
    for k in range(KD):
        tokens(0, k)
    act.wait_ge(s.ss1.sem, s.ss1.at(0))
    keys(0, b.h1)
    values(0)
    queries(0)
    act.wait_ge(s.kss.sem, s.kss.at(0))
    turned(0)
    with act.Fori(0, NB - 1) as t:
        block(t, True)
    block(NB - 1, False)


def a_vector(v, b, s, link):
    B = b.bank
    f32 = lambda ap: ap.bitcast(F32)
    four = lambda ap: ap.rearrange("p (c n) -> p c n", c=CT)
    PER = 4

    def stats(t):
        for c in range(CT):
            v.bn_stats(b.stats[:, c, :], b.x[:, bass.ds((t * CT + c) * D, D)]).then_inc(s.stats.sem, 1)
        v.wait_ge(s.stats.sem, s.stats.at(t))
        absorb(v, b)
        for c in range(CT):
            v.bn_aggr(b.mv[:, c, :], b.stats[:, c, :]).then_inc(s.mv.sem, 1)

    def modulate(t, c):
        if c == 0:
            v.wait_ge(s.rs1.sem, s.rs1.at(t))
        v.scalar_tensor_tensor(b.h1_next[:, c, :], b.x[:, bass.ds((t * CT + c) * D, D)], b.mv[:, c, 0:1], b.mods[0][:, CA, :],
                               ALU.subtract, ALU.mult).then_inc(s.xn.sem, 1)
        v.wait_ge(s.xn.sem, s.xn.at(t, c + 1))
        v.scalar_tensor_tensor(b.h1_next[:, c, :], b.h1_next[:, c, :], b.rs1[:, c:c + 1], b.mods[0][:, SA, :], ALU.mult, ALU.add).then_inc(s.h1.sem, 1)

    def normalise(t):
        v.wait_ge(s.rs2.sem, s.rs2.at(t))
        for c in range(CT):
            v.tensor_scalar(b.hn[:, c, :], b.h1_next[:, c, :], b.rs2[:, c:c + 1], None, ALU.mult).then_inc(s.hn.sem, 1)

    def tokens(t, k):
        v.wait_ge(s.hT_hi.sem, s.hT_hi.at(t, k + 1))
        v.tensor_tensor(b.hT_lo[:, k, :], B[2 + k][:, :], f32(b.hT_hi[:, k, :]), ALU.subtract).then_inc(s.hT_lo.sem, 1)

    def keys(t):
        v.wait_ge(s.rk.sem, s.rk.at(t))
        for c in range(CT):
            v.tensor_scalar(b.k[:, c, :], B[6 + c // 2][:, (c % 2) * D:(c % 2 + 1) * D], b.rk[:, c:c + 1], None, ALU.mult).then_inc(s.k.sem, 1)

    def average(t):
        for o in range(KD):
            v.wait_ge(s.av.sem, s.av.at(t, o + 1))
            v.tensor_tensor_scan(b.ema[:, o, :], b.decay[:, o:o + 1].broadcast_to([P, TB]), b.av[:, o, :], b.carry[:, o:o + 1],
                                 ALU.mult, ALU.add).then_inc(s.ema.sem, 1)
        v.wait_ge(s.ema.sem, s.ema.at(t))
        v.tensor_copy(b.carry[:, :], b.ema[:, :, TB - 1:TB].squeeze(2)).then_inc(link.sem, 1)
        v.wait_ge(link.sem, link.next())

    def beta(t):
        v.wait_ge(s.beta_e.sem, s.beta_e.at(t))
        v.tensor_scalar(b.beta_e[:, :], b.beta_e[:, :], 1.0, None, ALU.add).then_inc(link.sem, 1)
        v.wait_ge(link.sem, link.next())
        v.reciprocal(b.beta[:, :], b.beta_e[:, :]).then_inc(link.sem, 1)
        v.wait_ge(link.sem, link.next())

    def product(t, o):
        v.wait_ge(s.sg.sem, s.sg.at(t, o + 1))
        v.wait_ge(s.up_ps.sem, s.up_ps.at(t, o + 1))
        up = B[UP_BANKS[o]][:, :]
        v.tensor_tensor(up, up, b.sg[:, o, :], ALU.mult).then_inc(s.mm.sem, 1)

    def low(t, o):
        v.wait_ge(s.mm_hi.sem, s.mm_hi.at(t, o + 1))
        v.tensor_tensor(b.mm_lo[:, o, :], B[UP_BANKS[o]][:, :], f32(b.mm_hi[:, o, :]), ALU.subtract).then_inc(s.mm_lo.sem, 1)

    def block(t, more):
        if more:
            stats(t + 1)
        v.wait_ge(s.g_ps.sem, s.g_ps.at(t))
        v.tensor_tensor(four(b.a[:, :]), four(B[6][:, :]), spread(b.beta[:, :], P), ALU.mult).then_inc(s.a.sem, 1)
        v.wait_ge(s.pt_ps.sem, s.pt_ps.at(t))
        v.tensor_tensor(four(b.pT[:, :]), four(B[7][:, :]), mid(b.upper, CT), ALU.mult).then_inc(s.pT.sem, 1)
        v.wait_ge(s.a.sem, s.a.at(t))
        v.tensor_tensor(four(b.tT[:, :]), four(b.a[:, :]), mid(b.mask0, CT), ALU.mult).then_inc(link.sem, 1)
        v.wait_ge(link.sem, link.next())
        v.tensor_tensor(four(b.xx[:, :]), mid(b.ident, CT), four(b.tT[:, :]), ALU.subtract).then_inc(s.x.sem, 1)
        v.wait_ge(s.aTm0.sem, s.aTm0.at(t))
        v.tensor_tensor(four(b.xT[:, :]), mid(b.ident, CT), four(b.aTm[0][:, :]), ALU.subtract).then_inc(s.xT.sem, 1)
        for l in range(1, LEVELS):
            if l < LEVELS - 1:
                v.wait_ge(s.xax_ps.sem, s.xax_ps.at(t, l))
                v.wait_ge(s.x.sem, s.x.at(t, l))
                v.tensor_tensor(b.xx[:, :], b.xx[:, :], B[2][:, :], ALU.subtract).then_inc(s.x.sem, 1)
            v.wait_ge(s.xaxT_ps.sem, s.xaxT_ps.at(t, l))
            v.wait_ge(s.xT.sem, s.xT.at(t, l))
            v.tensor_tensor(b.xT[:, :], b.xT[:, :], B[3][:, :], ALU.subtract).then_inc(s.xT.sem, 1)
            if more and l < 3:
                for c in (2 * l - 2, 2 * l - 1):
                    modulate(t + 1, c)
        v.wait_ge(s.xT.sem, s.xT.at(t))
        v.tensor_tensor(four(b.tT[:, :]), four(b.xT[:, :]), spread(b.beta[:, :], P), ALU.mult).then_inc(s.tT.sem, 1)
        if more:
            normalise(t + 1)
        for c in range(CT):
            v.wait_ge(s.dm_ps.sem, s.dm_ps.at(t, c + 1))
            v.wait_ge(s.m.sem, s.m.at(t, c))
            old, new = b.m[c % 2], b.m[1 - c % 2]
            v.tensor_tensor(new.rearrange("p k n -> p (k n)"), old.rearrange("p k n -> p (k n)"), B[7][:, :], ALU.add).then_inc(s.m.sem, 1)
            if more and c % 2:
                tokens(t + 1, c // 2)
        for o in range(KD):
            v.wait_ge(s.oT_hi.sem, s.oT_hi.at(t, o + 1))
            v.tensor_tensor(b.oT_lo[:, o, :], B[o][:, :], f32(b.oT_hi[:, o, :]), ALU.subtract).then_inc(s.oT_lo.sem, 1)
        v.wait_ge(s.h1_kept.sem, s.h1_kept.at(t))
        for i in range(2):
            v.wait_ge(s.wo_ps.sem, s.wo_ps.at(t, i + 1))
            v.tensor_tensor(b.xa[:, 2 * i:2 * i + 2, :], b.h1[:, 2 * i:2 * i + 2, :], B[4 + i][:, :].rearrange("p (c n) -> p c n", c=2),
                            ALU.add).then_inc(s.xa.sem, 1)
        if more:
            keys(t + 1)
        v.wait_ge(s.rs3.sem, s.rs3.at(t))
        for c in range(CT):
            v.tensor_scalar(b.hn2[:, c, :], b.xa[:, c, :], b.rs3[:, c:c + 1], None, ALU.mult).then_inc(s.hn2.sem, 1)
        for k in range(KD):
            v.wait_ge(s.h2T_hi.sem, s.h2T_hi.at(t, k + 1))
            v.tensor_tensor(b.h2T_lo[:, k, :], B[2 + k][:, :], f32(b.h2T_hi[:, k, :]), ALU.subtract).then_inc(s.h2T_lo.sem, 1)
        if more:
            average(t + 1)
        product(t, 0)
        product(t, 1)
        low(t, 0)
        low(t, 1)
        product(t, 2)
        product(t, 3)
        low(t, 2)
        low(t, 3)
        if more:
            beta(t + 1)
        for i in range(2):
            v.wait_ge(s.down_ps.sem, s.down_ps.at(t, i + 1))
            v.tensor_tensor(b.xa[:, 2 * i:2 * i + 2, :], b.xa[:, 2 * i:2 * i + 2, :], B[2 + i][:, :].rearrange("p (c n) -> p c n", c=2),
                            ALU.add).then_inc(s.y.sem, 1)

    stats(0)
    for c in range(CT):
        modulate(0, c)
    normalise(0)
    modulation_vector(v, b, s, link, 1)
    a_weights_vector(v, b, s, link)
    for k in range(KD):
        tokens(0, k)
    keys(0)
    average(0)
    beta(0)
    v.wait_ge(s.load_x.sem, s.load_x.at(0))
    with v.Fori(0, NB - 1) as t:
        link.loop(t, PER)
        block(t, True)
    link.end(NB - 1)
    block(NB - 1, False)


def a_gpsimd(g, b, s, link):
    four = lambda ap: ap.rearrange("p (c n) -> p c n", c=CT)
    PER = 4

    def rs1(t):
        g.wait_ge(s.mv.sem, s.mv.at(t))
        absorb(g, b, 0)
        rsqrt(g, link, b.rs1[:, :], b.mv[:, :, 1:2].squeeze(2), b.neg_half[:, 0:CT], 1.0, LN_EPS).then_inc(s.rs1.sem, 1)

    def rs2(t):
        g.wait_ge(s.ss1.sem, s.ss1.at(t))
        absorb(g, b, 1)
        rsqrt(g, link, b.rs2[:, :], b.ss1[:, :], b.neg_half[:, 0:CT], 1.0 / D, RMS_EPS).then_inc(s.rs2.sem, 1)

    def rk(t):
        g.wait_ge(s.kss.sem, s.kss.at(t))
        absorb(g, b, 2)
        rsqrt(g, link, b.rk[:, :], b.kss[:, :], b.neg_half[:, 0:CT], 1.0, 0.0, floor=1e-24).then_inc(s.rk.sem, 1)

    def block(t, more):
        if more:
            rs1(t + 1)
        g.wait_ge(s.aT.sem, s.aT.at(t))
        for l in range(LEVELS):
            if l == 2:
                g.wait_ge(s.xT.sem, s.xT.at(t, 1))
            if l > 2:
                g.wait_ge(s.ax_ps.sem, s.ax_ps.at(t, l - 2))
            g.tensor_tensor(four(b.aTm[l % 2][:, :]), four(b.aT[:, :]), mid(b.maskT[:, l, :], CT), ALU.mult).then_inc((s.aTm if l else s.aTm0).sem, 1)
            if more and l == LEVELS - 2:
                rs2(t + 1)
        if more:
            rk(t + 1)
        g.wait_ge(s.ss2.sem, s.ss2.at(t))
        absorb(g, b, 3)
        rsqrt(g, link, b.rs3[:, :], b.ss2[:, :], b.neg_half[:, 0:CT], 1.0 / D, RMS_EPS).then_inc(s.rs3.sem, 1)
        for c in range(CT):
            g.wait_ge(s.y.sem, s.y.at(t, c // 2 + 1))
            g.tensor_tensor(b.xa[:, c, :], b.xa[:, c, :], b.mods[0][:, GA, :], ALU.mult).then_inc(s.gy.sem, 1)
            g.wait_ge(s.gy.sem, s.gy.at(t, c + 1))
            xt = b.x[:, bass.ds((t * CT + c) * D, D)]
            g.tensor_tensor(xt, xt, b.xa[:, c, :], ALU.add).then_inc(s.x_done.sem, 1)

    rs1(0)
    rs2(0)
    rk(0)
    with g.Fori(0, NB - 1) as t:
        link.loop(t, PER)
        block(t, True)
    link.end(NB - 1)
    block(NB - 1, False)



def groups(eng):
    with eng.Fori(0, NB // 2) as q:
        for par in range(2):
            yield 2 * q + par, par


def staggered(eng):
    yield 0, 0, False, False, True
    yield 1, 1, True, False, True
    with eng.Fori(0, NB // 2 - 2) as q:
        for par in range(2):
            yield 2 * q + (2 + par), par, True, True, True
    yield NB - 2, 0, True, True, True
    yield NB - 1, 1, True, True, False


def prep_vector(v, b, s, kind, r):
    cm, sm = (CA, SA) if kind == "C" else (CB, SB)

    def stats(t, par):
        for c in range(CT):
            v.bn_stats(b.p_stats[par][:, c, :], b.x[:, bass.ds((t * CT + c) * D, D)]).then_inc(r.stats.sem, 1)
        v.wait_ge(r.stats.sem, r.stats.at(t))
        absorb(v, b, par)
        for c in range(CT):
            v.bn_aggr(b.p_mv[par][:, c, :], b.p_stats[par][:, c, :]).then_inc(r.mv.sem, 1)

    def modulate(t, par):
        v.wait_ge(r.rs.sem, r.rs.at(t))
        h = b.p_h[par]
        for c in range(CT):
            if kind == "B1":
                v.scalar_tensor_tensor(h[:, c, :], b.y[:, bass.ds((t * CT + c) * D, D)], b.p_rs[par][:, c:c + 1], b.rows[:, ROW["norm_w"]:ROW["norm_w"] + D],
                                       ALU.mult, ALU.mult).then_inc(r.h.sem, 1)
            else:
                v.scalar_tensor_tensor(h[:, c, :], b.x[:, bass.ds((t * CT + c) * D, D)], b.p_mv[par][:, c, 0:1], b.mod[:, cm, :],
                                       ALU.subtract, ALU.mult).then_inc(r.xn.sem, 1)
        if kind != "B1":
            for c in range(CT):
                v.wait_ge(r.xn.sem, r.xn.at(t, c + 1))
                v.scalar_tensor_tensor(h[:, c, :], h[:, c, :], b.p_rs[par][:, c:c + 1], b.mod[:, sm, :], ALU.mult, ALU.add).then_inc(r.h.sem, 1)

    def gate(t, par):
        for c in range(CT):
            v.wait_ge(r.h.sem, r.h.at(t, c + 1))
            v.tensor_tensor(b.p_gh[par][:, c, :], b.p_h[par][:, c, :], b.mod[:, GB, :], ALU.mult).then_inc(r.gh.sem, 1)

    def normalise(t, par):
        v.wait_ge(r.rs2.sem, r.rs2.at(t))
        for c in range(CT):
            v.tensor_scalar(b.p_xn[par][:, c, :], b.p_h[par][:, c, :], b.p_rs2[par][:, c:c + 1], None, ALU.mult).then_inc(r.hn.sem, 1)

    def low(t, par):
        for k in range(KD):
            v.wait_ge(r.hT_hi.sem, r.hT_hi.at(t, k + 1))
            v.tensor_tensor(b.hT_lo_all[:, k, bass.ds(t * TB, TB)], b.bank[2 * par + k][:, :], b.hT_hi_all[:, k, bass.ds(t * TB, TB)].bitcast(F32),
                            ALU.subtract).then_inc(r.hT_lo.sem, 1)
        if kind != "C":
            E = E1 if kind == "D" else E0
            v.wait_ge(r.logit_ps.sem, r.logit_ps.at(t))
            src = b.bank[4 + par][:, 0:CT * E].rearrange("p (c e) -> p c e", c=CT)
            dst = b.logits[:, bass.ds(t * CT, CT), 0:E]
            if kind == "D":
                v.tensor_copy(dst, src).then_inc(r.logits.sem, 1)
            else:
                row = ROW["rb"] + (kind == "B1") * E0
                v.tensor_tensor(dst, src, mid(b.rows[:, row:row + E0], CT), ALU.add).then_inc(r.logits.sem, 1)

    if kind != "B1":
        stats(0, 0)
    for t, par, second, third, more in staggered(v):
        if kind == "D" and third:
            v.wait_ge(r.hn.sem, r.hn.at(t - 2))
        modulate(t, par)
        if kind != "B1" and more:
            stats(t + 1, 1 - par)
        if kind == "D":
            gate(t, par)
            if second:
                normalise(t - 1, 1 - par)
            if third:
                low(t - 2, par)
        elif second:
            low(t - 1, 1 - par)
    if kind == "D":
        normalise(NB - 1, 1)
        low(NB - 2, 0)
    low(NB - 1, 1)


def prep_gpsimd(g, b, s, link, kind, r):
    def rs(t, par):
        if kind == "B1":
            g.wait_ge(r.ss.sem, r.ss.at(t))
            absorb(g, b, par)
            g.tensor_scalar(b.p_rs[par][:, :], b.p_ss[par][:, :], 1.0 / D, RMS_EPS, ALU.mult, ALU.add).then_inc(r.var.sem, 1)
        else:
            g.wait_ge(r.mv.sem, r.mv.at(t))
            absorb(g, b, par)
            g.tensor_scalar(b.p_rs[par][:, :], b.p_mv[par][:, :, 1:2].squeeze(2), 1.0, LN_EPS, ALU.mult, ALU.add).then_inc(r.var.sem, 1)
        g.wait_ge(r.var.sem, r.var.at(t))
        g.tensor_tensor(b.p_rs[par][:, :], b.p_rs[par][:, :], b.neg_half[:, 0:CT], ALU.pow).then_inc(r.rs.sem, 1)

    if kind != "D":
        for t, par in groups(g):
            rs(t, par)
        return
    rs(0, 0)
    for t, par, _, _, more in staggered(g):
        if more:
            rs(t + 1, 1 - par)
        g.wait_ge(r.ss.sem, r.ss.at(t))
        absorb(g, b, 2 + par)
        g.tensor_scalar(b.p_rs2[par][:, :], b.p_ss[par][:, :], 1.0 / D, RMS_EPS, ALU.mult, ALU.add).then_inc(r.var2.sem, 1)
        g.wait_ge(r.var2.sem, r.var2.at(t))
        g.tensor_tensor(b.p_rs2[par][:, :], b.p_rs2[par][:, :], b.neg_half[:, 0:CT], ALU.pow).then_inc(r.rs2.sem, 1)
        for c in range(CT):
            xt = b.x[:, bass.ds((t * CT + c) * D, D)]
            g.wait_ge(r.gh.sem, r.gh.at(t, c + 1))
            g.tensor_tensor(xt, xt, b.p_gh[par][:, c, :], ALU.add).then_inc(r.xh.sem, 1)


def prep_scalar(act, b, s, kind, r):
    def squares(t, par, after=True):
        if kind == "B1" and after:
            act.wait_ge(r.ss.sem, r.ss.at(t - 1))
        for c in range(CT):
            if kind == "B1":
                act.activation(b.bank[6 + c // 2][:, (c % 2) * D:(c % 2 + 1) * D], b.y[:, bass.ds((t * CT + c) * D, D)], ACT.Square, accum_out=b.p_ss[par][:, c:c + 1]).then_inc(r.ss.sem, 1)
            else:
                act.wait_ge(r.h.sem, r.h.at(t, c + 1))
                act.activation(b.p_sq[par][:, c, :], b.p_h[par][:, c, :], ACT.Square, accum_out=b.p_ss[par][:, c:c + 1]).then_inc(r.ss.sem, 1)

    def take(t, par):
        if kind in ("B0", "B1"):
            act.wait_ge(r.h.sem, r.h.at(t))
            absorb(act, b, par)
            act.activation(b.y[:, bass.ds(t * CT * D, CT * D)], flat(b.p_h[par][:, :, :]), ACT.Copy).then_inc(r.y.sem, 1)
        for k in range(KD):
            act.wait_ge(r.hT_ps.sem, r.hT_ps.at(t, k + 1))
            if kind != "C":
                act.activation(b.p_hT[par][:, k, :], b.bank[2 * par + k][:, :], ACT.Copy).then_inc(r.hT.sem, 1)
            else:
                absorb(act, b, 2 * par + k)
            act.activation(b.hT_hi_all[:, k, bass.ds(t * TB, TB)], b.bank[2 * par + k][:, :], ACT.Copy).then_inc(r.hT_hi.sem, 1)

    if kind == "B1":
        squares(0, 0, after=False)
    for t, par, second, third, more in staggered(act):
        if kind == "B1" and more:
            squares(t + 1, 1 - par)
        if kind == "D":
            squares(t, par)
            if second:
                take(t - 1, 1 - par)
        else:
            take(t, par)
    if kind == "D":
        take(NB - 1, 1)


def prep_tensor(pe, b, s, kind, r):
    for t, par in groups(pe):
        src = b.p_xn if kind == "D" else b.p_h
        ready = r.hn if kind == "D" else r.h
        pe.wait_ge(ready.sem, ready.at(t))
        pe.wait_ge(r.free.sem, r.free.at(t - 2))
        for k in range(KD):
            for c in range(CT):
                ins = pe.transpose(b.bank[2 * par + k][:, c * P:(c + 1) * P], src[par][:, c, k * P:(k + 1) * P], b.ident)
            ins.then_inc(r.hT_ps.sem, 1)
        if kind != "C":
            E = E1 if kind == "D" else E0
            router = b.router[kind]
            pe.wait_ge(r.hT.sem, r.hT.at(t))
            for c in range(CT):
                for k in range(KD):
                    ins = pe.matmul(b.bank[4 + par][:, c * E:(c + 1) * E], b.p_hT[par][:, k, c * P:(c + 1) * P], router[:, k, :],
                                    start=k == 0, stop=k == KD - 1)
            ins.then_inc(r.logit_ps.sem, 1)


def routing_vector(v, b, s, link, kind):
    E, first = (E1, 0) if kind == "D" else (E0, NS)
    g = b.logits[:, :, 0:E]
    z, t, one, two = (x[:, :, 0:E] for x in (b.r_z, b.r_t, b.r_one, b.r_two))
    top, ga, gb = b.r_top[:, :], b.r_ga[:, :], b.r_gb[:, :]
    rank = mid(b.rank[:, 0:E], NT)
    if kind == "D":
        v.tensor_copy(z, g).then_inc(link.sem, 1)
        v.wait_ge(link.sem, link.next())
    else:
        row = ROW["gb"] + (kind == "B1") * E0
        v.tensor_tensor(z, g, mid(b.rows[:, row:row + E0], NT), ALU.add).then_inc(link.sem, 1)
        v.wait_ge(link.sem, link.next())
    for pick, gate in ((one, ga), (two, gb)):
        if pick is two:
            v.tensor_scalar(t, one, -2.0, 1.0, ALU.mult, ALU.add).then_inc(link.sem, 1)
            v.wait_ge(link.sem, link.next())
            v.tensor_scalar(t, t, BIG, None, ALU.mult).then_inc(link.sem, 1)
            v.wait_ge(link.sem, link.next())
            v.tensor_tensor(z, z, t, ALU.min).then_inc(link.sem, 1)
            v.wait_ge(link.sem, link.next())
        v.tensor_reduce(top, z, AX.X, ALU.max).then_inc(link.sem, 1)
        v.wait_ge(link.sem, link.next())
        v.tensor_tensor(t, z, spread(top, E), ALU.is_equal).then_inc(link.sem, 1)
        v.wait_ge(link.sem, link.next())
        v.tensor_tensor(t, t, rank, ALU.mult).then_inc(link.sem, 1)
        v.wait_ge(link.sem, link.next())
        v.tensor_reduce(top, t, AX.X, ALU.max).then_inc(link.sem, 1)
        v.wait_ge(link.sem, link.next())
        v.tensor_tensor(pick, t, spread(top, E), ALU.is_equal).then_inc(link.sem, 1)
        v.wait_ge(link.sem, link.next())
        v.tensor_tensor(t, pick, g, ALU.mult).then_inc(link.sem, 1)
        v.wait_ge(link.sem, link.next())
        v.tensor_reduce(gate, t, AX.X, ALU.add).then_inc(link.sem, 1)
        v.wait_ge(link.sem, link.next())
    v.tensor_tensor(top, ga, gb, ALU.max).then_inc(link.sem, 1)
    v.wait_ge(link.sem, link.next())
    v.tensor_tensor(ga, ga, top, ALU.subtract).then_inc(link.sem, 1)
    v.wait_ge(link.sem, link.next())
    v.tensor_tensor(gb, gb, top, ALU.subtract).then_inc(s.gates[kind].sem, 1)
    v.wait_ge(s.gate_exp[kind].sem, s.gate_exp[kind].at(0))
    v.tensor_tensor(top, ga, gb, ALU.add).then_inc(link.sem, 1)
    v.wait_ge(link.sem, link.next())
    v.reciprocal(top, top).then_inc(link.sem, 1)
    v.wait_ge(link.sem, link.next())
    v.tensor_tensor(ga, ga, top, ALU.mult).then_inc(link.sem, 1)
    v.wait_ge(link.sem, link.next())
    v.tensor_tensor(gb, gb, top, ALU.mult).then_inc(link.sem, 1)
    v.wait_ge(link.sem, link.next())
    v.tensor_tensor(one, one, spread(ga, E), ALU.mult).then_inc(link.sem, 1)
    v.wait_ge(link.sem, link.next())
    v.tensor_tensor(two, two, spread(gb, E), ALU.mult).then_inc(link.sem, 1)
    v.wait_ge(link.sem, link.next())
    v.tensor_tensor(b.weight[:, first:first + E, :].rearrange("p e t -> p t e"), one, two, ALU.add).then_inc(link.sem, 1)
    v.wait_ge(link.sem, link.next())


def routing_scalar(act, b, s, kind):
    act.wait_ge(s.gates[kind].sem, s.gates[kind].at(0))
    act.activation(b.r_ga[:, :], b.r_ga[:, :], ACT.Exp).then_inc(s.gate_exp[kind].sem, 1)
    act.activation(b.r_gb[:, :], b.r_gb[:, :], ACT.Exp).then_inc(s.gate_exp[kind].sem, 1)



class Step:
    def __init__(self, i, t, par, unit):
        self.i, self.t, self.par, self.unit = i, t, par, unit


def pair_steps(eng, p, i0):
    def at(j, expr=None):
        j0 = j if expr is None else expr
        return Step(2 * NB * p + j0 + i0, j0 - NB * (j // NB), j % 2, j // NB)

    yield at(0), at(1), None
    for unit in range(2):
        o = unit * NB
        with eng.Fori(0, NB // 2 - 1) as q:
            for n in (1, 2):
                e = 2 * q + (o + n)
                yield at(o + n, e), at(o + n + 1, e + 1) if n == 1 else Step(2 * NB * p + e + 1 + i0, e + 1 - o, 1, unit), at(o + n - 1, e - 1)
        if unit == 0:
            yield at(NB - 1), at(NB), at(NB - 2)
            yield at(NB), at(NB + 1), at(NB - 1)
    yield at(2 * NB - 1), None, at(2 * NB - 2)


def feature_block(b, st, k):
    return b.hT_hi_all[:, k, bass.ds(st.t * TB, TB)], b.hT_lo_all[:, k, bass.ds(st.t * TB, TB)]


def b_experts_tensor(pe, b, s, r, rnd):
    B = b.bank
    i0, p0 = rnd * U0 * NB, rnd * (U0 // 2)

    def part(st, mat, k, c0, w):
        return tuple(x[st.unit][:, mat * KD + k, c0:c0 + w] for x in (b.w_hi, b.w_lo))

    def up(st):
        pe.wait_ge(r.m_lo.sem, r.m_lo.at(st.i - 2))
        for o in range(KD):
            three(pe, B[2 * st.par + o][:, :], [part(st, 0, k, o * P, P) for k in range(KD)], [feature_block(b, st, k) for k in range(KD)]).then_inc(r.up_ps.sem, 1)

    def gate(st):
        pe.wait_ge(r.h_lo.sem, r.h_lo.at(st.i))
        pe.wait_ge(r.sg.sem, r.sg.at(st.i - 1))
        for o in range(KD):
            three(pe, B[4 + o][:, :], [part(st, 1, k, o * P, P) for k in range(KD)], [(b.h_hi[:, k, :], b.h_lo[:, k, :]) for k in range(KD)]).then_inc(r.gate_ps.sem, 1)

    def down(st, p):
        pe.wait_ge(r.m_lo.sem, r.m_lo.at(st.i))
        pe.wait_ge(r.acc.sem, r.acc.at(st.i - 1))
        for c in range(CT):
            out = B[6 + c // 2][:, (c % 2) * D:(c % 2 + 1) * D]
            three(pe, out, [(b.m_hi[st.par][:, k, c * P:(c + 1) * P], b.m_lo[st.par][:, k, c * P:(c + 1) * P]) for k in range(KD)],
                  [part(st, 2, k, 0, D) for k in range(KD)], last=False)
            ins = pe.matmul(out, b.ones_r[:, :], b.bias_all[:, bass.ds((2 * p + st.unit) * D, D)], start=False, stop=True)
            if c % 2:
                ins.then_inc(r.down_ps.sem, 1)

    with pe.Fori(0, U0 // 2) as p:
        for st, after, before in pair_steps(pe, p, i0):
            if before is None:
                pe.wait_ge(b.split[0].sem, b.split[0].at(p0 + p))
                up(st)
            gate(st)
            if after is not None:
                if after.unit != st.unit:
                    pe.wait_ge(b.split[1].sem, b.split[1].at(p0 + p))
                up(after)
            if before is not None:
                down(before, p)
            if after is None:
                down(st, p)


def b_experts_scalar(act, b, s, r, rnd):
    B = b.bank
    i0, p0 = rnd * U0 * NB, rnd * (U0 // 2)

    def h_hi(st):
        for o in range(KD):
            act.wait_ge(r.up_ps.sem, r.up_ps.at(st.i, o + 1))
            act.activation(b.h_hi[:, o, :], B[2 * st.par + o][:, :], ACT.Identity, bias=b.bias_cols[st.unit][:, o:o + 1]).then_inc(r.h_hi.sem, 1)

    with act.Fori(0, U0 // 2) as p:
        for st, after, before in pair_steps(act, p, i0):
            if before is None:
                act.wait_ge(b.split[0].sem, b.split[0].at(p0 + p))
                h_hi(st)
            for o in range(KD):
                act.wait_ge(r.gate_ps.sem, r.gate_ps.at(st.i, o + 1))
                act.wait_ge(r.m.sem, r.m.at(st.i - 1, o + 1))
                act.activation(b.sgate[o], B[4 + o][:, :], ACT.Silu, bias=b.bias_cols[st.unit][:, KD + o:KD + o + 1]).then_inc(r.sg.sem, 1)
            for o in range(KD):
                act.wait_ge(r.m.sem, r.m.at(st.i, o + 1))
                act.activation(b.m_hi[st.par][:, o, :], B[2 * st.par + o][:, :], ACT.Copy).then_inc(r.m_hi.sem, 1)
            if after is not None:
                if after.unit != st.unit:
                    act.wait_ge(b.split[1].sem, b.split[1].at(p0 + p))
                h_hi(after)


def b_experts_vector(v, b, s, r, rnd):
    B = b.bank
    i0 = rnd * U0 * NB

    def h_lo(st):
        for o in range(KD):
            v.wait_ge(r.h_hi.sem, r.h_hi.at(st.i, o + 1))
            v.scalar_tensor_tensor(b.h_lo[:, o, :], B[2 * st.par + o][:, :], b.bias_cols[st.unit][:, o:o + 1], b.h_hi[:, o, :].bitcast(F32),
                                   ALU.add, ALU.subtract).then_inc(r.h_lo.sem, 1)

    with v.Fori(0, U0 // 2) as p:
        for st, after, before in pair_steps(v, p, i0):
            if before is None:
                h_lo(st)
            for o in range(KD):
                v.wait_ge(r.sg.sem, r.sg.at(st.i, o + 1))
                bank = B[2 * st.par + o][:, :]
                v.scalar_tensor_tensor(bank, bank, b.bias_cols[st.unit][:, o:o + 1], b.sgate[o], ALU.add, ALU.mult).then_inc(r.m.sem, 1)
            for o in range(KD):
                v.wait_ge(r.m_hi.sem, r.m_hi.at(st.i, o + 1))
                v.tensor_tensor(b.m_lo[st.par][:, o, :], B[2 * st.par + o][:, :], b.m_hi[st.par][:, o, :].bitcast(F32), ALU.subtract).then_inc(r.m_lo.sem, 1)
            if after is not None:
                h_lo(after)
            if before is not None:
                accumulate(v, b, r, before, p, b.y, (B[6], B[7]))
            if after is None:
                accumulate(v, b, r, st, p, b.y, (B[6], B[7]))


def accumulate(v, b, r, st, p, to, banks):
    for c in range(CT):
        if c % 2 == 0:
            v.wait_ge(r.down_ps.sem, r.down_ps.at(st.i, c // 2 + 1))
        tile = to[:, bass.ds((st.t * CT + c) * D, D)]
        w = b.weight_flat[:, bass.ds((2 * p + st.unit) * NT + st.t * CT + c, 1)]
        v.scalar_tensor_tensor(tile, banks[c // 2][:, (c % 2) * D:(c % 2 + 1) * D], w, tile, ALU.mult, ALU.add).then_inc(r.acc.sem, 1)


def weights_sync(sp, b, dram, raw, rnd, pairs, split, loaded):
    with sp.Fori(0, pairs) as p:
        for unit in range(2):
            sp.wait_ge(split[1 - unit].sem, split[1 - unit].at(rnd * pairs + p + unit - 1))
            sp.dma_start(raw[:, :], dram[bass.ds(2 * p + unit, 1), :, :].squeeze(0)).then_inc(loaded[unit].sem, 16)


def weights_gpsimd(g, b, link, rnd, pairs, prepare, raw, hi, lo, split, loaded, r):
    with g.Fori(0, pairs) as p:
        link.loop(p, prepare.per)
        for unit in range(2):
            g.wait_ge(loaded[unit].sem, loaded[unit].at(rnd * pairs + p))
            g.wait_ge(r.down_ps.sem, r.down_ps.at(2 * NB * (rnd * pairs + p - 1) + NB * (unit + 1) - 1))
            absorb(g, b)
            prepare(g, link, p, unit)
            g.tensor_copy(hi[unit], raw[:, :]).then_inc(link.sem, 1)
            g.wait_ge(link.sem, link.next())
            g.tensor_tensor(lo[unit], raw[:, :], hi[unit].bitcast(F32), ALU.subtract).then_inc(split[unit].sem, 1)
    link.end(pairs)


def bias_table_vector(v, b, link, raw, tmp, scale):
    if scale is not None:
        v.tensor_tensor(raw.rearrange("p (u n) -> p u n", n=D), raw.rearrange("p (u n) -> p u n", n=D), mid(scale, EP), ALU.mult).then_inc(link.sem, 1)
        v.wait_ge(link.sem, link.next())
    v.tensor_copy(tmp.bitcast(F32R), raw).then_inc(link.sem, 1)
    v.wait_ge(link.sem, link.next())
    v.tensor_scalar(raw, raw, b.ident[:, 1:2], None, ALU.mult).then_inc(link.sem, 1)
    v.wait_ge(link.sem, link.next())
    v.tensor_scalar(b.row_sign[:, :], b.ident[:, 1:2], -2.0, 1.0, ALU.mult, ALU.add).then_inc(link.sem, 1)
    v.wait_ge(link.sem, link.next())
    v.scalar_tensor_tensor(b.bias_all[:, :], tmp, b.row_sign[:, :], raw, ALU.mult, ALU.add).then_inc(link.sem, 1)
    v.wait_ge(link.sem, link.next())


def close_scalar(act, b, r):
    for t, par in groups(act):
        act.wait_ge(r.xn.sem, r.xn.at(t - 2))
        absorb(act, b, par)
        for c in range(CT):
            act.activation(b.p_h[par][:, c, :], b.y[:, bass.ds((t * CT + c) * D, D)], ACT.Square, accum_out=b.p_ss[par][:, c:c + 1]).then_inc(r.ss.sem, 1)


def close_gpsimd(g, b, r):
    for t, par in groups(g):
        g.wait_ge(r.ss.sem, r.ss.at(t))
        absorb(g, b, par)
        g.tensor_scalar(b.p_rs[par][:, :], b.p_ss[par][:, :], 1.0 / D, RMS_EPS, ALU.mult, ALU.add).then_inc(r.var.sem, 1)
        g.wait_ge(r.var.sem, r.var.at(t))
        g.tensor_tensor(b.p_rs[par][:, :], b.p_rs[par][:, :], b.neg_half[:, 0:CT], ALU.pow).then_inc(r.rs.sem, 1)


def close_vector(v, b, r):
    for t, par in groups(v):
        v.wait_ge(r.rs.sem, r.rs.at(t))
        for c in range(CT):
            v.scalar_tensor_tensor(b.p_xn[par][:, c, :], b.y[:, bass.ds((t * CT + c) * D, D)], b.p_rs[par][:, c:c + 1], b.norm_gate[:, :],
                                   ALU.mult, ALU.mult).then_inc(r.xn.sem, 1)
        for c in range(CT):
            v.wait_ge(r.xn.sem, r.xn.at(t, c + 1))
            xt = b.x[:, bass.ds((t * CT + c) * D, D)]
            v.tensor_tensor(xt, xt, b.p_xn[par][:, c, :], ALU.add).then_inc(r.x.sem, 1)



def softplus_scale_vector(v, b, s, link):
    v.wait_ge(s.head_scale.sem, s.head_scale.at(0))
    v.tensor_scalar(b.c_scale[:, :], b.c_scale[:, :], DH ** -0.5, None, ALU.mult).then_inc(link.sem, 1)
    v.wait_ge(link.sem, link.next())
    for j, name in enumerate(("bq", "bk")):
        v.tensor_tensor(b.c_bias[:, j * KD:(j + 1) * KD], b.cols[:, COL[name]:COL[name] + KD], b.c_scale[:, :], ALU.mult).then_inc(link.sem, 1)
        v.wait_ge(link.sem, link.next())


def c_weights_vector(v, b, s, link):
    for i, name in enumerate(C_MATS):
        v.wait_ge(s.load_c[i].sem, s.load_c[i].at(0))
        raw, hi, lo = b.c_raw[name], b.c_hi[name], b.c_lo[name]
        v.tensor_copy(hi, raw).then_inc(link.sem, 1)
        v.wait_ge(link.sem, link.next())
        v.tensor_tensor(lo, raw, hi.bitcast(F32), ALU.subtract).then_inc(s.c_w.sem, 1)


C_MATS = ("c_wq", "c_wk", "c_wv", "c_wo")


def c_tensor(pe, b, s, r):
    B = b.bank
    W = lambda name, k, c0=0, w=D: (b.c_hi[name][:, k, c0:c0 + w], b.c_lo[name][:, k, c0:c0 + w])

    def project(t):
        pe.wait_ge(r.y.sem, r.y.at(t - 1))
        h = [(b.hT_hi_all[:, k, bass.ds(t * TB, TB)], b.hT_lo_all[:, k, bass.ds(t * TB, TB)]) for k in range(KD)]
        for j, name in enumerate(C_MATS[:3]):
            if j == 2:
                pe.wait_ge(r.v.sem, r.v.at(t - 1))
            for o in range(KD):
                three(pe, B[2 * j + o][:, :], [W(name, k, o * P, P) for k in range(KD)], h).then_inc(r.qkv_ps.sem, 1)

    def denominator(t):
        pe.wait_ge(r.o_taken.sem, r.o_taken.at(t - 1))
        for o in range(KD):
            pe.wait_ge(r.qk_lo.sem, r.qk_lo.at(t, o + 1))
            pe.matmul(B[6 + o][:, :], b.heads_r[:, :], b.qk_hi[:, o, :], start=True, stop=False)
            pe.matmul(B[6 + o][:, :], b.heads_r[:, :], b.qk_lo[:, o, :], start=False, stop=True).then_inc(r.den_ps.sem, 1)

    def output(t):
        pe.wait_ge(r.out_lo.sem, r.out_lo.at(t))
        for c in range(CT):
            ins = three(pe, B[6 + c // 2][:, (c % 2) * D:(c % 2 + 1) * D],
                        [(b.out_hi[:, k, c * P:(c + 1) * P], b.out_lo[:, k, c * P:(c + 1) * P]) for k in range(KD)], [W("c_wo", k) for k in range(KD)])
            if c % 2:
                ins.then_inc(r.o_ps.sem, 1)

    project(0)
    with pe.Fori(0, NB - 1) as t:
        denominator(t)
        project(t + 1)
        output(t)
    denominator(NB - 1)
    output(NB - 1)


def c_scalar(act, b, s, r):
    B = b.bank
    half = lambda x, j: x[:, j * KD:(j + 1) * KD, :].rearrange("p k n -> p (k n)")

    def take(t):
        for j in range(2 * KD):
            act.wait_ge(r.qkv_ps.sem, r.qkv_ps.at(t, j + 1))
            if j == 0:
                act.wait_ge(r.soft.sem, r.soft.at(t - 1))
            act.activation(b.c_y[:, j, :], B[j][:, :], ACT.Identity, bias=b.c_bias[:, j:j + 1], scale=b.c_scale[:, j % KD:j % KD + 1]).then_inc(r.y.sem, 1)

    def soften(t):
        act.wait_ge(r.y.sem, r.y.at(t))
        for j in range(2):
            act.activation(half(b.c_e, j), half(b.c_y, j), ACT.Abs).then_inc(r.abs.sem, 1)
        for j in range(2):
            act.wait_ge(r.abs.sem, r.abs.at(t, j + 1))
            act.activation(half(b.c_e, j), half(b.c_e, j), ACT.Exp, scale=-1.0).then_inc(r.exp.sem, 1)

    def logarithm(t):
        for j in range(2):
            act.wait_ge(r.exp.sem, r.exp.at(t, j + 1))
            act.activation(half(b.c_l, j), half(b.c_e, j), ACT.Ln, bias=b.ones[:, 0:1]).then_inc(r.ln.sem, 1)

    def product(t):
        act.wait_ge(r.qk.sem, r.qk.at(t))
        for o in range(KD):
            act.activation(b.qk_hi[:, o, :], b.c_qk[:, o, :], ACT.Copy).then_inc(r.qk_hi.sem, 1)

    def output(t):
        for o in range(KD):
            act.wait_ge(r.out.sem, r.out.at(t, o + 1))
            act.activation(b.out_hi[:, o, :], b.c_out[:, o, :], ACT.Copy).then_inc(r.out_hi.sem, 1)

    take(0)
    soften(0)
    logarithm(0)
    with act.Fori(0, NB - 1) as t:
        product(t)
        take(t + 1)
        soften(t + 1)
        output(t)
        logarithm(t + 1)
    product(NB - 1)
    output(NB - 1)


def c_gpsimd(g, b, s, r):
    def tail(t):
        for j in range(2):
            half = lambda x: x[:, j * KD:(j + 1) * KD, :].rearrange("p k n -> p (k n)")
            g.wait_ge(r.exp.sem, r.exp.at(t, j + 1))
            absorb(g, b)
            g.tensor_scalar(half(b.c_t), half(b.c_e), -0.5, 1.0, ALU.mult, ALU.add).then_inc(r.tail0.sem, 1)
            g.wait_ge(r.tail0.sem, r.tail0.at(t, j + 1))
            g.tensor_tensor(half(b.c_t), half(b.c_t), half(b.c_e), ALU.mult).then_inc(r.tail.sem, 1)

    def add(t):
        for c in range(CT):
            g.wait_ge(r.o_taken.sem, r.o_taken.at(t, c // 2 + 1))
            g.tensor_tensor(b.c_o[:, c, :], b.c_o[:, c, :], b.mod[:, GA, :], ALU.mult).then_inc(r.go.sem, 1)
            g.wait_ge(r.go.sem, r.go.at(t, c + 1))
            xt = b.x[:, bass.ds((t * CT + c) * D, D)]
            g.tensor_tensor(xt, xt, b.c_o[:, c, :], ALU.add).then_inc(r.x.sem, 1)

    tail(0)
    with g.Fori(0, NB - 1) as t:
        tail(t + 1)
        add(t)
    add(NB - 1)


def c_vector(v, b, s, r):
    B = b.bank
    half = lambda x, j: x[:, j * KD:(j + 1) * KD, :].rearrange("p k n -> p (k n)")

    def values(t):
        v.wait_ge(r.out.sem, r.out.at(t - 1))
        for o in range(KD):
            v.wait_ge(r.qkv_ps.sem, r.qkv_ps.at(t, 2 * KD + o + 1))
            v.tensor_scalar(b.c_v[:, o, :], B[4 + o][:, :], b.cols[:, COL["bv"] + o:COL["bv"] + o + 1], None, ALU.add).then_inc(r.v.sem, 1)

    def product(t):
        for j in range(2):
            v.wait_ge(r.ln.sem, r.ln.at(t, j + 1))
            v.wait_ge(r.tail.sem, r.tail.at(t, j + 1))
            v.tensor_tensor(half(b.c_l, j), half(b.c_l, j), half(b.c_t, j), ALU.max).then_inc(r.lmax.sem, 1)
            v.wait_ge(r.lmax.sem, r.lmax.at(t, j + 1))
            v.scalar_tensor_tensor(half(b.c_l, j), half(b.c_y, j), 0.0, half(b.c_l, j), ALU.max, ALU.add).then_inc(r.soft.sem, 1)
        v.wait_ge(r.soft.sem, r.soft.at(t))
        v.wait_ge(r.qk_lo.sem, r.qk_lo.at(t - 1))
        v.tensor_tensor(b.c_qk[:, :, :], b.c_l[:, 0:KD, :], b.c_l[:, KD:2 * KD, :], ALU.mult).then_inc(r.qk.sem, 1)

    def low(t):
        for o in range(KD):
            v.wait_ge(r.qk_hi.sem, r.qk_hi.at(t, o + 1))
            v.tensor_tensor(b.qk_lo[:, o, :], b.c_qk[:, o, :], b.qk_hi[:, o, :].bitcast(F32), ALU.subtract).then_inc(r.qk_lo.sem, 1)

    def divide(t):
        for o in range(KD):
            v.wait_ge(r.den_ps.sem, r.den_ps.at(t, o + 1))
            v.tensor_tensor(b.c_v[:, o, :], b.c_v[:, o, :], B[6 + o][:, :], ALU.mult).then_inc(r.num.sem, 1)
            v.reciprocal(b.c_r[:, o, :], B[6 + o][:, :]).then_inc(r.rden.sem, 1)
            v.wait_ge(r.rden.sem, r.rden.at(t, o + 1))
            v.tensor_tensor(b.c_out[:, o, :], b.c_v[:, o, :], b.c_r[:, o, :], ALU.mult).then_inc(r.out.sem, 1)

    def output(t):
        for o in range(KD):
            v.wait_ge(r.out_hi.sem, r.out_hi.at(t, o + 1))
            v.tensor_tensor(b.out_lo[:, o, :], b.c_out[:, o, :], b.out_hi[:, o, :].bitcast(F32), ALU.subtract).then_inc(r.out_lo.sem, 1)

    def project(t):
        v.wait_ge(r.x.sem, r.x.at(t - 1))
        for i in range(2):
            v.wait_ge(r.o_ps.sem, r.o_ps.at(t, i + 1))
            v.tensor_tensor(b.c_o[:, 2 * i:2 * i + 2, :], B[6 + i][:, :].rearrange("p (c n) -> p c n", c=2), mid(b.c_bo, 2),
                            ALU.add).then_inc(r.o_taken.sem, 1)

    values(0)
    product(0)
    with v.Fori(0, NB - 1) as t:
        low(t)
        divide(t)
        values(t + 1)
        output(t)
        product(t + 1)
        project(t)
    low(NB - 1)
    divide(NB - 1)
    output(NB - 1)
    project(NB - 1)


def d_experts_tensor(pe, b, s, r):
    B = b.bank

    def up(st):
        for o in range(KH):
            pe.wait_ge(r.m_lo.sem, r.m_lo.at(st.i - 1, o + 1))
            three(pe, B[o][:, :], [(b.v1_hi[st.unit][:, k, o * P:(o + 1) * P], b.v1_lo[st.unit][:, k, o * P:(o + 1) * P]) for k in range(KD)],
                  [feature_block(b, st, k) for k in range(KD)]).then_inc(r.up_ps.sem, 1)

    def down(st, p):
        pe.wait_ge(r.m_lo.sem, r.m_lo.at(st.i))
        pe.wait_ge(s.d_ready.sem, s.d_ready.at(0))
        pe.wait_ge(r.acc.sem, r.acc.at(st.i - 2))
        for c in range(CT):
            out = B[4 + 2 * st.par + c // 2][:, (c % 2) * D:(c % 2 + 1) * D]
            three(pe, out, [(b.m_hi[st.par][:, k, c * P:(c + 1) * P], b.m_lo[st.par][:, k, c * P:(c + 1) * P]) for k in range(KH)],
                  [(b.v2_hi[st.unit][:, k, :], b.v2_lo[st.unit][:, k, :]) for k in range(KH)], last=False)
            ins = pe.matmul(out, b.ones_r[:, :], b.bias_all[:, bass.ds((2 * p + st.unit) * D, D)], start=False, stop=True)
            if c % 2:
                ins.then_inc(r.down_ps.sem, 1)

    with pe.Fori(0, E1 // 2) as p:
        for st, after, before in pair_steps(pe, p, 0):
            if before is None:
                pe.wait_ge(b.split1[0].sem, b.split1[0].at(p))
                up(st)
            if after is not None:
                if after.unit != st.unit:
                    pe.wait_ge(b.split1[1].sem, b.split1[1].at(p))
                up(after)
            down(st, p)


def d_experts_scalar(act, b, s, r):
    with act.Fori(0, E1 // 2) as p:
        for st, after, before in pair_steps(act, p, 0):
            for o in range(KH):
                act.wait_ge(r.up_ps.sem, r.up_ps.at(st.i, o + 1))
                act.activation(b.bank[o][:, :], b.bank[o][:, :], ACT.Gelu, bias=b.bias_cols1[st.unit][:, o:o + 1]).then_inc(r.m.sem, 1)
            for o in range(KH):
                act.wait_ge(r.m.sem, r.m.at(st.i, o + 1))
                act.activation(b.m_hi[st.par][:, o, :], b.bank[o][:, :], ACT.Copy).then_inc(r.m_hi.sem, 1)


def d_experts_vector(v, b, s, r):
    with v.Fori(0, E1 // 2) as p:
        for st, after, before in pair_steps(v, p, 0):
            for o in range(KH):
                v.wait_ge(r.m_hi.sem, r.m_hi.at(st.i, o + 1))
                v.tensor_tensor(b.m_lo[st.par][:, o, :], b.bank[o][:, :], b.m_hi[st.par][:, o, :].bitcast(F32), ALU.subtract).then_inc(r.m_lo.sem, 1)
            for x in ((before, st) if after is None else (before,)):
                if x is not None:
                    accumulate(v, b, r, x, p, b.x, b.bank[4 + 2 * x.par:6 + 2 * x.par])




def program(nc, d, out):
    ctx = ExitStack()
    with ctx:
        b = Names()
        b.gpsimd, b.scalar = nc.gpsimd, nc.scalar

        def sb(scope, name, shape, dt=F32):
            return scope.enter_context(nc.sbuf_tensor(name, shape, dt))[(slice(None),) * len(shape)]

        def signal(name, per=1, credit=0):
            return Signal(ctx.enter_context(nc.semaphore(name)), per, credit)

        def signals(prefix, table):
            return {name: signal(prefix + name, *(spec if isinstance(spec, tuple) else (spec,))) for name, spec in table.items()}

        b.bank = [ctx.enter_context(nc.psum_tensor(f"bank{i}", [P, TB], F32)) for i in range(8)]
        b.x = sb(ctx, "x", [P, NT * D])
        b.cols = sb(ctx, "cols", [P, NCOL])
        b.rows = sb(ctx, "rows", [P, NROW])
        b.mods = [sb(ctx, f"mod{i}", [P, 6, D]) for i in range(2)]
        b.mod = b.mods[0]
        b.ident = sb(ctx, "ident", [P, P])
        b.neg_half = sb(ctx, "neg_half", [P, NT])
        b.spare_g, b.spare_v, b.spare_s = (sb(ctx, "spare_" + e, [P, 4]) for e in "gvs")
        b.ones = sb(ctx, "ones", [P, P])
        b.silu_c = [sb(ctx, f"silu_c{i}", [P, KD]) for i in range(2)]
        b.alpha, b.decay, b.carry = (sb(ctx, n, [P, KD]) for n in ("alpha", "decay", "carry"))
        b.neg_beta_b = sb(ctx, "neg_beta_b", [P, 1])

        with ExitStack() as a:
            masks = sb(a, "masks", [P, 2 + LEVELS, P])
            b.upper, b.mask0, b.maskT = masks[:, 0, :], masks[:, 1, :], masks[:, 2:, :]
            b.a_hi, b.a_lo, b.a_raw = {}, {}, {}
            for name, kb, w, _ in A_MATS:
                b.a_hi[name] = sb(a, "a_hi_" + name, [P, kb, w], F32R)[:, :, :]
                b.a_lo[name] = sb(a, "a_lo_" + name, [P, kb, w], F32R)[:, :, :]
            b.hT_hi, b.hT_lo, b.oT_hi, b.oT_lo = (sb(a, "a_" + n, [P, KD, TB], F32R) for n in ("hT_hi", "hT_lo", "oT_hi", "oT_lo"))
            with ExitStack() as raw:
                b.wmod = [sb(raw, f"wmod{i}", [P, KD, 6 * D]) for i in range(2)]
                b.silu_rep = [sb(raw, f"silu_rep{i}", [P, KD, P]) for i in range(2)]
            b.qT, b.av, b.ema, b.kT = (sb(a, "a_" + n, [P, KD, TB]) for n in ("qT", "av", "ema", "kT"))
            b.wT = b.av
            b.k, b.v, b.xa, b.h1, b.h1_next, b.hn = (sb(a, "a_" + n, [P, CT, D]) for n in ("k", "v", "xa", "h1", "h1_next", "hn"))
            b.hn2 = b.v
            b.a, b.aT, b.xx, b.xT, b.ax, b.pT, b.tT = (sb(a, "a_" + n, [P, TB]) for n in ("a", "aT", "xx", "xT", "ax", "pT", "tT"))
            b.aTm = [sb(a, f"a_aTm{i}", [P, TB]) for i in range(2)]
            b.u = [sb(a, f"a_u{i}", [P, D]) for i in range(2)]
            b.m = [sb(a, f"a_m{i}", [P, KD, D])[:, :, :] for i in range(2)]
            b.stats = sb(a, "a_stats", [P, CT, 6])
            b.mv = sb(a, "a_mv", [P, CT, 2])
            b.ss1, b.ss2, b.kss, b.rs1, b.rs2, b.rs3, b.rk, b.beta, b.beta_e = (
                sb(a, "a_" + n, [P, CT]) for n in ("ss1", "ss2", "kss", "rs1", "rs2", "rs3", "rk", "beta", "beta_e"))
            with ExitStack() as raw:
                for name, kb, w, _ in A_MATS:
                    b.a_raw[name] = sb(raw, "a_raw_" + name, [P, kb, w])[:, :, :]
                b.gate_sign = [sb(raw, f"gate_sign{i}", [P, D]) for i in range(2)]
            with ExitStack() as late:
                b.h2T_hi = sb(late, "a_h2T_hi", [P, KD, TB], F32R)
                b.h2T_lo = sb(late, "a_h2T_lo", [P, KD, TB], F32R)
                b.sg = sb(late, "a_sg", [P, KH, TB])
                b.mm_hi = sb(late, "a_mm_hi", [P, KH, TB], F32R)
                b.mm_lo = sb(late, "a_mm_lo", [P, KH, TB], F32R)

        s_table = signals("", dict(load_small=80, load_x0=16, load_x=16, a_scaled=1, a_hi_done=1, set=1, alpha_e=1, h1_kept=1, stored=16, a_w=len(A_MATS), stats=CT, mv=CT, rs1=1, xn=CT, h1=CT, ss1=CT,
                               rs2=1, hn=CT, hT_ps=KD, hT_hi=KD, hT_lo=KD, k_ps=2, kss=CT, rk=1, k=CT, beta_ps=1, beta_e=1, v_ps=KD, q_ps=KD, av=KD,
                               ema=KD, qT=KD, vtok_ps=2, vtok=2, kT_ps=KD, kT=KD, g_ps=1, pt_ps=1, a=1, pT=1, aT_ps=1, aT=1, aTm0=1, aTm=LEVELS - 1,
                               x=LEVELS - 1, xT=LEVELS, ax_ps=LEVELS - 1, ax=LEVELS - 1, xax_ps=LEVELS - 2, xaxT_ps=LEVELS - 1, tT=1, wT_ps=KD, wT=KD,
                               u_ps=CT, u=CT, dm_ps=CT, m=(CT, 1), oT_ps=1, oT_hi=KD, oT_lo=KD, wo_ps=2, xa=2, ss2=CT, rs3=1, hn2=CT,
                               h2T_ps=KD, h2T_hi=KD, h2T_lo=KD, gate_ps=KH, up_ps=KH, sg=KH, mm=KH, mm_hi=KH, mm_lo=KH, down_ps=2, y=(2, 1),
                               gy=CT, x_done=CT))
        s = Names(**s_table)
        s.load_a = [signal("load_" + name, 16) for name, _, _, _ in A_MATS]
        s.silu_c = [signal(f"silu_c{i}") for i in range(2)]
        s.silu_rep = [signal(f"silu_rep{i}", KD) for i in range(2)]
        s.load_wmod = [signal(f"load_wmod{i}", 16) for i in range(2)]
        s.mod_ps = [signal(f"mod_ps{i}", 3) for i in range(2)]
        s.mod_raw = [signal(f"mod_raw{i}", 3) for i in range(2)]
        s.mod = [signal(f"mod{i}") for i in range(2)]
        W0, W1 = 3 * KD * D, KD * HID + KH * D
        after_a = ctx.enter_context(ExitStack())
        b.hT_hi_all = sb(after_a, "hT_hi_all", [P, KD, N], F32R)
        b.hT_lo_all = sb(after_a, "hT_lo_all", [P, KD, N], F32R)
        weight = sb(after_a, "weight", [P, EP * NT])
        b.weight, b.weight_flat = weight[:, :].rearrange("p (e t) -> p e t", e=EP), weight
        b.rank = sb(after_a, "rank", [P, EP])
        b.row_sign = sb(after_a, "row_sign", [P, 1])
        b.ones_r = sb(after_a, "ones_r", [P, P], F32R)
        b.bias_all = sb(after_a, "bias_all", [P, EP * D], F32R)
        b.router = {kind: sb(after_a, "router_" + kind, [P, KD, E1 if kind == "D" else E0]) for kind in ("B0", "B1", "D")}
        b.bias_cols = [sb(after_a, f"bias_cols{i}", [P, 2 * KD]) for i in range(2)]
        b.bias_cols1 = [sb(after_a, f"bias_cols1{i}", [P, KH]) for i in range(2)]

        def prep_buffers(scope, name, kinds):
            pair = lambda n, shape: [sb(scope, f"{name}_{n}{i}", shape) for i in range(2)]
            b.p_stats, b.p_mv, b.p_h = pair("stats", [P, CT, 6]), pair("mv", [P, CT, 2]), pair("h", [P, CT, D])
            b.p_rs, b.p_rs2, b.p_ss = pair("rs", [P, CT]), pair("rs2", [P, CT]), pair("ss", [P, CT])
            if kinds == "B":
                with ExitStack() as over:
                    b.p_xn = [sb(over, f"{name}_xn{i}", [P, CT, D]) for i in range(2)]
            if kinds == "D":
                b.p_xn = pair("xn", [P, CT, D])
                b.bias_raw, b.bias_tmp = (sb(scope, n, [P, EP * D]) for n in ("bias_raw", "bias_tmp"))
                b.p_gh, b.p_sq = ([table[:, i * CT * D:(i + 1) * CT * D].rearrange("p (c n) -> p c n", c=CT) for i in range(2)]
                                  for table in (b.bias_raw, b.bias_tmp))
            if kinds != "C":
                b.logits = sb(scope, name + "_logits", [P, NT, EP])
                b.r_top, b.r_ga, b.r_gb = (sb(scope, f"{name}_r_{n}", [P, NT]) for n in ("top", "ga", "gb"))
                with ExitStack() as over:
                    b.p_hT = [sb(over, f"{name}_hT{i}", [P, KD, TB]) for i in range(2)]
                with ExitStack() as over:
                    b.r_z, b.r_t, b.r_one, b.r_two = (sb(over, f"{name}_r_{n}", [P, NT, EP]) for n in ("z", "t", "one", "two"))

        with ExitStack() as sc:
            b.y = sb(sc, "y", [P, NT * D])
            b.w_raw = sb(sc, "w_raw", [P, W0])
            b.w_hi_flat = [sb(sc, f"w_hi{i}", [P, W0], F32R) for i in range(2)]
            b.w_lo_flat = [sb(sc, f"w_lo{i}", [P, W0], F32R) for i in range(2)]
            b.w_hi, b.w_lo = ([w[:, :].rearrange("p (m n) -> p m n", n=D) for w in ws] for ws in (b.w_hi_flat, b.w_lo_flat))
            with ExitStack() as e:
                b.h_hi, b.h_lo = (sb(e, n, [P, KD, TB], F32R) for n in ("h_hi", "h_lo"))
                b.m_hi, b.m_lo = ([sb(e, f"{n}{i}", [P, KD, TB], F32R) for i in range(2)] for n in ("m_hi", "m_lo"))
                b.sgate = [b.mods[0][:, j:j + 2, :].rearrange("p a n -> p (a n)") for j in (SA, SB)]
            with ExitStack() as e:
                b.norm_gate = sb(e, "norm_gate", [P, D])
                prep_buffers(e, "pb", "B")
            b.split, b.loaded = ([signal(f"split{i}", 1, i) for i in range(2)], [signal(f"loaded{i}", 16) for i in range(2)])
            bB = Names(b)
        b.mod = b.mods[1]
        with ExitStack() as sc:
            b.c_hi = {n: sb(sc, n + "_hi", [P, KD, D], F32R) for n in C_MATS}
            b.c_lo = {n: sb(sc, n + "_lo", [P, KD, D], F32R) for n in C_MATS}
            b.heads, b.c_bo = sb(sc, "heads", [P, P]), sb(sc, "c_bo", [P, D])
            b.heads_r = sb(sc, "heads_r", [P, P], F32R)
            b.c_scale, b.c_bias = sb(sc, "c_scale", [P, KD]), sb(sc, "c_bias", [P, 2 * KD])
            with ExitStack() as e:
                b.c_raw = {n: sb(e, n + "_raw", [P, KD, D]) for n in C_MATS}
                prep_buffers(e, "pc", "C")
            with ExitStack() as e:
                b.c_y, b.c_e, b.c_l, b.c_t = (sb(e, n, [P, 2 * KD, TB]) for n in ("c_y", "c_e", "c_l", "c_t"))
                b.c_qk, b.c_v, b.c_r, b.c_out = (sb(e, n, [P, KD, TB]) for n in ("c_qk", "c_v", "c_r", "c_out"))
                b.qk_hi, b.qk_lo, b.out_hi, b.out_lo = (sb(e, n, [P, KD, TB], F32R) for n in ("qk_hi", "qk_lo", "out_hi", "out_lo"))
                b.c_o = sb(e, "c_o", [P, CT, D])
            bC = Names(b)
        with ExitStack() as sc:
            b.w_raw = sb(sc, "v_raw", [P, W1])
            b.w_hi_flat = [sb(sc, f"v_hi{i}", [P, W1], F32R) for i in range(2)]
            b.w_lo_flat = [sb(sc, f"v_lo{i}", [P, W1], F32R) for i in range(2)]
            b.v1_hi, b.v1_lo = ([w[:, 0:KD * HID].rearrange("p (k n) -> p k n", k=KD) for w in ws] for ws in (b.w_hi_flat, b.w_lo_flat))
            b.v2_hi, b.v2_lo = ([w[:, KD * HID:W1].rearrange("p (k n) -> p k n", k=KH) for w in ws] for ws in (b.w_hi_flat, b.w_lo_flat))
            with ExitStack() as e:
                b.m_hi, b.m_lo = ([sb(e, f"d_{n}{i}", [P, KH, TB], F32R) for i in range(2)] for n in ("m_hi", "m_lo"))
            with ExitStack() as e:
                prep_buffers(e, "pd", "D")
            b.split1 = b.split = [sig.again(R0 * U0 // 2) for sig in bB.split]
            b.loaded = [sig.again(R0 * U0 // 2) for sig in bB.loaded]
            bD = Names(b)

        common = signals("prep_", dict(rs=1, xn=CT, h=CT, var=1, hT_ps=KD, hT_hi=KD, hT_lo=(KD, 3), hT=KD, logit_ps=1,
                                              logits=(1, 2), stats=CT, mv=CT, y=1, ss=CT, rs2=1, var2=1, hn=CT, gh=CT, xh=CT))
        turns = {name: 0 for name in common}

        def prep_signals(*names):
            r = {}
            for name in names:
                r[name] = common[name].again(turns[name])
                turns[name] += NB
            return Names(**r)

        moved = ("hT_ps", "hT_hi", "hT_lo")
        routed = ("hT", "logit_ps", "logits")
        modulated = ("stats", "mv", "rs", "xn", "h", "var")
        rp = {"B0": prep_signals(*moved, *routed, *modulated, "y"), "B1": prep_signals(*moved, *routed, "rs", "h", "var", "y", "ss")}
        rx = prep_signals("ss", "var", "rs", "xn")
        rx.x = signal("close_x", CT)
        rp["C"] = prep_signals(*moved, *modulated)
        rp["D"] = prep_signals(*moved, *routed, *modulated, "ss", "hn", "rs2", "var2", "gh", "xh")
        for kind, r in rp.items():
            r.free = r.hT_lo if kind == "C" else r.logits
        experts = signals("expert_", dict(up_ps=KD, h_hi=KD, h_lo=KD, gate_ps=KD, sg=(KD, 1), m=(KD, 2), m_hi=KD,
                                            m_lo=(KD, 3), down_ps=(2, 17), acc=(CT, 1)))
        rb = Names(**experts)
        rd = Names(**{name: experts[name].again(R0 * U0 * NB, per) for name, per in dict(up_ps=KH, m=KH, m_hi=KH, m_lo=KH, down_ps=2, acc=CT).items()})
        rc = Names(**{name: s_table[old].again(NB, per) for name, (old, per) in dict(
                y=("ss1", 2 * KD), abs=("hT_hi", 2), exp=("beta_e", 2), ln=("kss", 2), qk_hi=("av", KD), out_hi=("qT", KD),
                v=("k", KD), o_taken=("y", 2), qk_lo=("hT_lo", KD), out_lo=("oT_lo", KD), soft=("m", 2), qk=("a", 1), out=("xn", KD), lmax=("pT", 2),
                num=("hn", KD), rden=("xa", KD), qkv_ps=("v_ps", 3 * KD), den_ps=("q_ps", KD), o_ps=("wo_ps", 2),
                tail0=("rs1", 2), tail=("rs2", 2), go=("gy", CT), x=("x_done", CT)).items()})
        s.load_b, s.load_bias1, s.head_scale, s.c_w = signal("load_b", 16 * 6), signal("load_bias1", 32), signal("head_scale"), signal("c_w", len(C_MATS))
        s.load_c_small = signal("load_c_small", 32)
        s.zeroed, s.zeroed1, s.b_ready, s.d_ready = (signal(n) for n in ("zeroed", "zeroed1", "b_ready", "d_ready"))
        s.load_c = [signal("load_" + n, 16) for n in C_MATS]
        s.gates = {k: signal("gates_" + k) for k in ("B0", "B1", "D")}
        s.gate_exp = {k: signal("gate_exp_" + k, 2) for k in ("B0", "B1", "D")}
        last = NB - 1
        vector_chain, gpsimd_chain = (ctx.enter_context(nc.semaphore(n)) for n in ("vector_chain", "gpsimd_chain"))
        def sync_b(sp):
            sp.wait_ge(s.x_done.sem, s.x_done.at(last))
            sp.dma_start(b.rank[:, :], d["rank"]).then_inc(s.load_b.sem, 16)
            for i, kind in enumerate(("B0", "B1")):
                sp.dma_start(b.router[kind][:, :, :], d["router"][i].rearrange("(k p) e -> p k e", p=P)).then_inc(s.load_b.sem, 16)
            sp.dma_start(b.router["D"][:, :, :], d["gate_w"].rearrange("(k p) e -> p k e", p=P)).then_inc(s.load_b.sem, 16)
            sp.wait_ge(s.zeroed.sem, s.zeroed.at(0))
            for row in range(2):
                sp.dma_start(bB.y[row:row + 1, 0:EP * D], d["b_down0"]).then_inc(s.load_b.sem, 16)
            for rnd in range(R0):
                weights_sync(sp, bB, d["units0"], bB.w_raw, rnd, U0 // 2, bB.split, bB.loaded)

        def sync_c(sp):
            sp.wait_ge(rx.x.sem, rx.x.at(last))
            sp.dma_start(bC.heads, d["consts"][:, 1, :]).then_inc(s.load_c_small.sem, 16)
            sp.dma_start(bC.c_bo, d["bo"]).then_inc(s.load_c_small.sem, 16)
            for name, sig in zip(C_MATS, s.load_c):
                sp.dma_start(bC.c_raw[name][:, :, :], d[name].rearrange("(k p) n -> p k n", p=P)).then_inc(sig.sem, 16)

        def sync_d(sp):
            sp.wait_ge(rc.x.sem, rc.x.at(last))
            sp.wait_ge(s.zeroed1.sem, s.zeroed1.at(0))
            for row in range(2):
                sp.dma_start(bD.bias_raw[row:row + 1, :], d["b_down1"]).then_inc(s.load_bias1.sem, 16)
            weights_sync(sp, bD, d["units1"], bD.w_raw, 0, E1 // 2, bD.split, bD.loaded)

        def prepare0(g, link, p, unit):
            for i, name in enumerate(("bup", "bg")):
                g.tensor_copy(bB.bias_cols[unit][:, i * KD:(i + 1) * KD], b.cols[:, bass.ds(COL[name] + (2 * p + unit) * KD, KD)])

        def prepare1(g, link, p, unit):
            g.tensor_copy(bD.bias_cols1[unit][:, :], b.cols[:, bass.ds(COL["b1"] + (2 * p + unit) * KH, KH)])
            for k in range(KD):
                w = bD.w_raw[:, k * HID:(k + 1) * HID]
                g.tensor_scalar(w, w, b.cols[:, COL["norm3"] + k:COL["norm3"] + k + 1], None, ALU.mult)
            w = bD.w_raw[:, KD * HID:W1].rearrange("p (k n) -> p k n", n=D)
            g.tensor_tensor(w, w, mid(b.mod[:, GB, :], KH), ALU.mult).then_inc(link.sem, 1)
            g.wait_ge(link.sem, link.next())
            absorb(g, b)

        prepare0.per, prepare1.per = 2, 4

        def gpsimd_b(g, link):
            g.wait_ge(s.x_done.sem, s.x_done.at(last))
            g.memset(bB.y[:, 0:EP * D], 0.0)
            g.memset(b.weight_flat[:, 0:NS * NT], 1.0).then_inc(s.zeroed.sem, 1)
            prep_gpsimd(g, bB, s, link, "B0", rp["B0"])
            weights_gpsimd(g, bB, link, 0, U0 // 2, prepare0, bB.w_raw, bB.w_hi_flat, bB.w_lo_flat, bB.split, bB.loaded, rb)
            prep_gpsimd(g, bB, s, link, "B1", rp["B1"])
            weights_gpsimd(g, bB, link, 1, U0 // 2, prepare0, bB.w_raw, bB.w_hi_flat, bB.w_lo_flat, bB.split, bB.loaded, rb)
            close_gpsimd(g, bB, rx)

        def scalar_b(act):
            act.wait_ge(s.b_ready.sem, s.b_ready.at(0))
            prep_scalar(act, bB, s, "B0", rp["B0"])
            routing_scalar(act, bB, s, "B0")
            b_experts_scalar(act, bB, s, rb, 0)
            act.wait_ge(rb.acc.sem, rb.acc.at(U0 * NB - 1))
            prep_scalar(act, bB, s, "B1", rp["B1"])
            routing_scalar(act, bB, s, "B1")
            b_experts_scalar(act, bB, s, rb, 1)
            act.wait_ge(rb.acc.sem, rb.acc.at(R0 * U0 * NB - 1))
            close_scalar(act, bB, rx)

        def vector_b(v, link):
            v.wait_ge(s.x_done.sem, s.x_done.at(last))
            v.wait_ge(s.load_b.sem, s.load_b.at(0))
            v.tensor_copy(b.ones_r[:, :], b.ones[:, :]).then_inc(link.sem, 1)
            v.wait_ge(link.sem, link.next())
            bias_table_vector(v, b, link, bB.y[:, 0:EP * D], bB.y[:, EP * D:2 * EP * D], None)
            for k in range(KD):
                v.tensor_scalar(b.router["D"][:, k, :], b.router["D"][:, k, :], b.cols[:, COL["norm3"] + k:COL["norm3"] + k + 1], None, ALU.mult).then_inc(link.sem, 1)
                v.wait_ge(link.sem, link.next())
            v.memset(b.spare_v[:, 0:1], 0.0).then_inc(s.b_ready.sem, 1)
            v.wait_ge(s.b_ready.sem, s.b_ready.at(0))
            for rnd, kind in enumerate(("B0", "B1")):
                prep_vector(v, bB, s, kind, rp[kind])
                v.wait_ge(rp[kind].logits.sem, rp[kind].logits.at(last))
                routing_vector(v, bB, s, link, kind)
                v.wait_ge(rp[kind].y.sem, rp[kind].y.at(last))
                b_experts_vector(v, bB, s, rb, rnd)
                v.wait_ge(rb.acc.sem, rb.acc.at((rnd + 1) * U0 * NB - 1))
            v.tensor_tensor(bB.norm_gate[:, :], b.rows[:, ROW["norm_w"] + D:ROW["norm_w"] + 2 * D], b.mods[0][:, GB, :], ALU.mult).then_inc(link.sem, 1)
            v.wait_ge(link.sem, link.next())
            close_vector(v, bB, rx)

        def tensor_b(pe):
            pe.wait_ge(s.b_ready.sem, s.b_ready.at(0))
            for rnd, kind in enumerate(("B0", "B1")):
                prep_tensor(pe, bB, s, kind, rp[kind])
                pe.wait_ge(rp[kind].logits.sem, rp[kind].logits.at(last))
                pe.wait_ge(rp[kind].hT_lo.sem, rp[kind].hT_lo.at(last))
                b_experts_tensor(pe, bB, s, rb, rnd)
                pe.wait_ge(rb.acc.sem, rb.acc.at((rnd + 1) * U0 * NB - 1))

        def gpsimd_c(g, link):
            g.wait_ge(rx.x.sem, rx.x.at(last))
            prep_gpsimd(g, bC, s, link, "C", rp["C"])
            c_gpsimd(g, bC, s, rc)

        def scalar_c(act):
            act.wait_ge(rx.x.sem, rx.x.at(last))
            act.activation(b.c_scale[:, :], b.cols[:, COL["hbeta"]:COL["hbeta"] + KD], ACT.Exp, scale=-1.0).then_inc(s.head_scale.sem, 1)
            prep_scalar(act, bC, s, "C", rp["C"])
            act.wait_ge(s.c_w.sem, s.c_w.at(0))
            c_scalar(act, bC, s, rc)

        def vector_c(v, link):
            v.wait_ge(rx.x.sem, rx.x.at(last))
            softplus_scale_vector(v, bC, s, link)
            v.wait_ge(s.load_c_small.sem, s.load_c_small.at(0))
            v.tensor_copy(bC.heads_r[:, :], bC.heads).then_inc(link.sem, 1)
            v.wait_ge(link.sem, link.next())
            prep_vector(v, bC, s, "C", rp["C"])
            c_weights_vector(v, bC, s, link)
            c_vector(v, bC, s, rc)

        def tensor_c(pe):
            pe.wait_ge(rx.x.sem, rx.x.at(last))
            prep_tensor(pe, bC, s, "C", rp["C"])
            pe.wait_ge(rp["C"].hT_lo.sem, rp["C"].hT_lo.at(last))
            pe.wait_ge(s.c_w.sem, s.c_w.at(0))
            c_tensor(pe, bC, s, rc)

        def gpsimd_d(g, link):
            g.wait_ge(rc.x.sem, rc.x.at(last))
            prep_gpsimd(g, bD, s, link, "D", rp["D"])
            g.wait_ge(rp["D"].xh.sem, rp["D"].xh.at(last))
            g.memset(bD.bias_raw[:, :], 0.0).then_inc(s.zeroed1.sem, 1)
            weights_gpsimd(g, bD, link, 0, E1 // 2, prepare1, bD.w_raw, bD.w_hi_flat, bD.w_lo_flat, bD.split, bD.loaded, rd)

        def scalar_d(act):
            act.wait_ge(rc.x.sem, rc.x.at(last))
            prep_scalar(act, bD, s, "D", rp["D"])
            routing_scalar(act, bD, s, "D")
            act.wait_ge(bD.split[0].sem, bD.split[0].at(0))
            d_experts_scalar(act, bD, s, rd)

        def vector_d(v, link):
            v.wait_ge(rc.x.sem, rc.x.at(last))
            prep_vector(v, bD, s, "D", rp["D"])
            v.wait_ge(rp["D"].logits.sem, rp["D"].logits.at(last))
            routing_vector(v, bD, s, link, "D")
            v.wait_ge(s.load_bias1.sem, s.load_bias1.at(0))
            bias_table_vector(v, b, link, bD.bias_raw[:, :], bD.bias_tmp[:, :], b.mod[:, GB, :])
            v.memset(b.spare_v[:, 0:1], 0.0).then_inc(s.d_ready.sem, 1)
            v.wait_ge(rp["D"].xh.sem, rp["D"].xh.at(last))
            d_experts_vector(v, bD, s, rd)

        def tensor_d(pe):
            pe.wait_ge(rc.x.sem, rc.x.at(last))
            prep_tensor(pe, bD, s, "D", rp["D"])
            pe.wait_ge(rp["D"].logits.sem, rp["D"].logits.at(last))
            pe.wait_ge(rp["D"].hT_lo.sem, rp["D"].hT_lo.at(last))
            d_experts_tensor(pe, bD, s, rd)

        x_tiles = b.x[:, :].rearrange("p (t n) -> p t n", t=NT)
        block = ctx.enter_context(nc.Block())

        @block.sync
        def _(sp):
            sp.dma_start(b.cols[:, :], d["cols"]).then_inc(s.load_small.sem, 16)
            sp.dma_start(b.rows[:, :], d["rows"]).then_inc(s.load_small.sem, 16)
            sp.dma_start(b.ident, d["consts"][:, 0, :]).then_inc(s.load_small.sem, 16)
            sp.dma_start(masks[:, :, :], d["consts"][:, 2:, :]).then_inc(s.load_small.sem, 16)
            sp.dma_start(b.ones[:, :], d["ones"]).then_inc(s.load_small.sem, 16)
            for layer, name in enumerate(("wmod0", "wmod1")):
                sp.dma_start(b.wmod[layer][:, :, :], d[name].rearrange("(k p) n -> p k n", p=P)).then_inc(s.load_wmod[layer].sem, 16)
                if layer == 0:
                    sp.dma_start(x_tiles[:, 0:CT, :], d["x"][0:TB, :].rearrange("(t p) n -> p t n", p=P)).then_inc(s.load_x0.sem, 16)
            for (name, _, _, _), sig in zip(A_MATS, s.load_a):
                sp.dma_start(b.a_raw[name], d[name].rearrange("(k p) n -> p k n", p=P)).then_inc(sig.sem, 16)
            sp.dma_start(x_tiles[:, CT:, :], d["x"][TB:, :].rearrange("(t p) n -> p t n", p=P)).then_inc(s.load_x.sem, 16)
            sync_b(sp)
            sync_c(sp)
            sync_d(sp)
            sp.wait_ge(rd.acc.sem, rd.acc.at(E1 * NB - 1))
            sp.dma_start(out.rearrange("(t p) n -> p t n", p=P), b.x[:, :].rearrange("p (t n) -> p t n", t=NT)).then_inc(s.stored.sem, 16)
            sp.wait_ge(s.stored.sem, s.stored.at(0))

        @block.gpsimd
        def _(g):
            g.sem_inc(bB.split[1].sem, bB.split[1].credit)
            link = Chain(gpsimd_chain)
            g.memset(b.neg_half[:, :], -0.5)
            g.memset(b.m[0], 0.0)
            g.memset(b.carry[:, :], 0.0).then_inc(s.set.sem, 1)
            g.wait_ge(s.set.sem, s.set.at(0))
            g.wait_ge(s.mod[0].sem, s.mod[0].at(0))
            a_gpsimd(g, b, s, link)
            gpsimd_b(g, link)
            gpsimd_c(g, link)
            gpsimd_d(g, link)

        @block.scalar
        def _(act):
            act.sem_inc(rb.sg.sem, rb.sg.credit)
            for layer in range(2):
                modulation_scalar(act, b, s, layer)
            act.activation(b.alpha[:, :], b.cols[:, COL["alpha"]:COL["alpha"] + KD], ACT.Exp, scale=-1.0)
            act.activation(b.neg_beta_b[:, :], b.rows[:, ROW["beta_b"]:ROW["beta_b"] + 1], ACT.Copy, scale=-1.0).then_inc(s.alpha_e.sem, 1)
            act.wait_ge(s.alpha_e.sem, s.alpha_e.at(0))
            a_scalar(act, b, s)
            scalar_b(act)
            scalar_c(act)
            scalar_d(act)

        @block.vector
        def _(v):
            v.sem_inc(s.m.sem, s.m.credit)
            v.sem_inc(s.y.sem, s.y.credit)
            v.sem_inc(rp["B0"].hT_lo.sem, rp["B0"].hT_lo.credit)
            v.sem_inc(rp["B0"].logits.sem, rp["B0"].logits.credit)
            v.sem_inc(rb.m.sem, rb.m.credit)
            v.sem_inc(rb.m_lo.sem, rb.m_lo.credit)
            v.sem_inc(rb.acc.sem, rb.acc.credit)
            link = Chain(vector_chain)
            modulation_vector(v, b, s, link, 0)
            v.wait_ge(s.alpha_e.sem, s.alpha_e.at(0))
            v.tensor_scalar(b.alpha[:, :], b.alpha[:, :], 1.0, None, ALU.add).then_inc(link.sem, 1)
            v.wait_ge(link.sem, link.next())
            v.reciprocal(b.alpha[:, :], b.alpha[:, :]).then_inc(link.sem, 1)
            v.wait_ge(link.sem, link.next())
            v.tensor_scalar(b.decay[:, :], b.alpha[:, :], -1.0, 1.0, ALU.mult, ALU.add).then_inc(link.sem, 1)
            v.wait_ge(link.sem, link.next())
            v.wait_ge(s.load_x0.sem, s.load_x0.at(0))
            v.wait_ge(s.set.sem, s.set.at(0))
            a_vector(v, b, s, link)
            vector_b(v, link)
            vector_c(v, link)
            vector_d(v, link)

        @block.tensor
        def _(pe):
            pe.sem_inc(rb.down_ps.sem, rb.down_ps.credit)
            for layer in range(2):
                modulation_tensor(pe, b, s, layer)
                pe.wait_ge(s.mod_raw[layer].sem, s.mod_raw[layer].at(0))
            pe.wait_ge(s.set.sem, s.set.at(0))
            a_tensor(pe, b, s)
            tensor_b(pe)
            tensor_c(pe)
            tensor_d(pe)


def columns(a):
    import numpy as np

    return np.ascontiguousarray(np.asarray(a).reshape(-1, P).T)


def constants():
    import numpy as np

    i = np.arange(P)
    row, col = i[:, None], i[None, :]
    level = [((row // (2 << l)) == (col // (2 << l))) & (row % (2 << l) >= (1 << l)) & (col % (2 << l) < (1 << l)) for l in range(LEVELS)]
    parts = [row == col, row // DH == col // DH, row <= col, level[0]] + [m.T for m in level]
    return np.ascontiguousarray(np.stack([m.astype(np.float32) for m in parts], axis=1))


def laid_out(i):
    import numpy as np

    i = {k: np.asarray(v) for k, v in i.items()}
    g = lambda name: i["L0_attn_" + name]
    f = lambda name: i["L0_ffn_" + name]
    w = {}
    w["x"] = g("x").reshape(N, D)
    w["cols"] = np.concatenate([columns(v) for v in (
        g("norm1_w"), g("norm2_w"), g("alpha_logit"), i["L1_ffn_norm_weight"], i["L1_attn_bq"], i["L1_attn_bk"], i["L1_attn_bv"],
        np.repeat(i["L1_attn_beta"], DH), i["L0_c"], i["L1_c"],
        np.concatenate([f("share_bup").reshape(NS, D), f("exp_bup")]), np.concatenate([np.stack([f("share_bg")] * NS), f("exp_bg")]),
        i["L1_ffn_b1"])], axis=1)
    rows = np.concatenate([v.reshape(-1) for v in (f("norm_w"), f("router_b"), f("gate_bias"), g("beta_b"))])
    w["rows"] = np.broadcast_to(rows, (P, NROW))
    w["bo"] = np.broadcast_to(i["L1_attn_bo"], (P, D))
    w["consts"] = constants()
    w["ones"] = np.ones((P, P), np.float32)
    w["wmod0"], w["wmod1"] = i["L0_wmod"], i["L1_wmod"]
    w["wq"], w["wk"], w["wv"], w["wo"] = g("Wq"), g("Wk"), g("Wv"), g("Wo")
    w["c_wq"], w["c_wk"], w["c_wv"], w["c_wo"] = (i["L1_attn_W" + n].T for n in "qkvo")
    w["router"], w["gate_w"] = f("router_W"), i["L1_ffn_gate_w"].T
    w["rank"] = np.broadcast_to(np.arange(EP, 0, -1, dtype=np.float32), (P, EP))
    on_partitions = lambda m: m.reshape(m.shape[0], -1, P, m.shape[2]).transpose(0, 2, 1, 3).reshape(m.shape[0], P, -1)
    w["units0"] = np.concatenate([on_partitions(m) for m in (
        np.concatenate([f("share_Wup").reshape(D, NS, D).transpose(1, 0, 2), f("exp_Wup")]),
        np.concatenate([np.stack([f("share_Wg")] * NS), f("exp_Wg")]),
        np.concatenate([np.stack([f("share_Wdown")] * NS), f("exp_Wdown")]))], axis=2)
    w["units1"] = np.concatenate([on_partitions(i["L1_ffn_w1"].transpose(0, 2, 1)), on_partitions(i["L1_ffn_w2"].transpose(0, 2, 1))], axis=2)
    w["b_down0"] = np.concatenate([np.stack([f("share_bdown")] * NS), f("exp_bdown")]).reshape(1, -1)
    w["b_down1"] = i["L1_ffn_b2"].reshape(1, -1)
    w["beta_w"] = np.concatenate([g("beta_w")] * 2, axis=1)
    w["w_gate"], w["w_up"], w["w_down"] = g("w_gate"), g("w_up"), g("w_down")
    return {k: np.ascontiguousarray(v) for k, v in w.items()}


def kernel(**inputs):
    import numpy as np
    import concourse.bacc as bacc
    from concourse.bass_utils import run_bass_kernel_spmd

    nc = bacc.Bacc("TRN2", target_bir_lowering=False, num_devices=1)
    arrays = {"in_" + k: v for k, v in laid_out(inputs).items()}
    d = {k[3:]: nc.dram_tensor(k, v.shape, mybir.dt.from_np(v.dtype), kind="ExternalInput").ap() for k, v in arrays.items()}
    out = nc.dram_tensor("out_x", (N, D), F32, kind="ExternalOutput").ap()
    program(nc, d, out)
    r = run_bass_kernel_spmd(nc, [arrays], core_ids=[0])
    return r.results[0]["out_x"].reshape(1, N, D)
```
